# Optimizing a Trainium2 kernel written in Bass

```python
import numpy as np
import jax
import jax.numpy as jnp

def _softmax(x, axis=-1):
    return jax.nn.softmax(x, axis=axis)

def _gelu(x):
    return jax.nn.gelu(x, approximate=True)

def _silu(x):
    return jax.nn.silu(x)

def _sigmoid(x):
    return jax.nn.sigmoid(x)

def _layernorm(x, axis=-1, eps=1e-05):
    m = jnp.mean(x, axis=axis, keepdims=True)
    v = jnp.var(x, axis=axis, keepdims=True)
    return (x - m) / jnp.sqrt(v + eps)

def _scatter_add(tgt, idx, src, axis=0):
    return tgt.at[idx].add(src)

def _segment_sum(src, seg, n):
    return jax.ops.segment_sum(src, seg, n)
kernel_name = 'mk_gps_d1_gnn_r8_de25e9'

def setup_inputs(seed: int=0):
    np.random.seed(seed)
    _w = jnp.asarray

    def _rec_inputs():
        import jax
        import jax.numpy as jnp
        _gk = jax.random.key(seed)
        x = -8.776e-05 + 1 * jax.random.normal(jax.random.fold_in(_gk, 1), (2500, 256), jnp.float32)
        src = jax.random.randint(jax.random.fold_in(_gk, 2), (80000,), 0, 2500, jnp.int32)
        dst = jnp.minimum((2500 * jax.random.uniform(jax.random.fold_in(_gk, 3), (80000,)) ** 2.0).astype(jnp.int32), 19999)
        _o = jnp.argsort(dst, stable=True)
        src = src[_o]
        dst = dst[_o]
        return (x, src, dst)
    x, src, dst = _rec_inputs()

    def _L0_gnn_setup():
        import jax, jax.numpy as jnp
        import numpy as np
        N, E, IN_DIM, HEADS, HEAD_DIM = (2500, 40000, 256, 4, 64)
        OUT_DIM = HEADS * HEAD_DIM
        NEG_SLOPE = 0.2
        LN_EPS = 1e-05
        SM_EPS = 1e-16

        def _gatv2_block(x, edge_index, W_l, W_r, att, bias, gamma, beta):
            src, dst = (edge_index[0], edge_index[1])
            xl = (x @ W_l).reshape(N, HEADS, HEAD_DIM)
            xr = (x @ W_r).reshape(N, HEADS, HEAD_DIM)
            e = xl[src] + xr[dst]
            e = jnp.where(e >= 0, e, NEG_SLOPE * e)
            score = jnp.einsum('ehd,hd->eh', e, att)
            m = jax.ops.segment_max(score, dst, num_segments=N)
            m = jnp.where(jnp.isfinite(m), m, 0.0)
            ex = jnp.exp(score - m[dst])
            denom = jax.ops.segment_sum(ex, dst, num_segments=N)
            alpha = ex / (denom[dst] + SM_EPS)
            agg = jax.ops.segment_sum(alpha[:, :, None] * xl[src], dst, num_segments=N)
            out = agg.reshape(N, OUT_DIM) + bias
            h = jax.nn.elu(out) + x
            mu = jnp.mean(h, axis=-1, keepdims=True)
            var = jnp.mean(jnp.square(h - mu), axis=-1, keepdims=True)
            return (h - mu) * jax.lax.rsqrt(var + LN_EPS) * gamma + beta
        key = jax.random.key(seed)
        ks = jax.random.split(key, 9)
        s = 1.0 / np.sqrt(IN_DIM)
        return {'x': jax.random.normal(ks[0], (N, IN_DIM), jnp.float32), 'edge_index': jax.random.randint(ks[1], (2, E), 0, N, jnp.int32), 'W_l': jax.random.normal(ks[2], (IN_DIM, OUT_DIM), jnp.float32) * s, 'W_r': jax.random.normal(ks[3], (IN_DIM, OUT_DIM), jnp.float32) * s, 'att': jax.random.normal(ks[4], (HEADS, HEAD_DIM), jnp.float32) * s, 'bias': jnp.zeros((OUT_DIM,), jnp.float32), 'gamma': jnp.ones((OUT_DIM,), jnp.float32), 'beta': jnp.zeros((OUT_DIM,), jnp.float32)}
    _L0_gnn_all = _L0_gnn_setup()
    _L0_gnn_in = {k: v for k, v in _L0_gnn_all.items() if k in ('W_l', 'W_r', 'att', 'bias', 'gamma', 'beta')}
    del _L0_gnn_all

    def _L0_mix_setup():
        import jax, jax.numpy as jnp
        import numpy as np
        BN_EPS = 1e-05
        key = jax.random.key(seed)
        ks = jax.random.split(key, 4)
        B, N, D = (8, 1024, 256)
        outD = 256
        s = 1.0 / np.sqrt(D)
        return {'feature': jax.random.normal(ks[0], (B, N, D), dtype=jnp.float32), 'W_qk': jax.random.normal(ks[1], (2, D, D), dtype=jnp.float32) * s, 'b_qk': jnp.zeros((2, D), dtype=jnp.float32), 'W_v': jax.random.normal(ks[2], (D, outD), dtype=jnp.float32) * s, 'b_v': jnp.zeros((outD,), dtype=jnp.float32), 'gamma': jnp.ones((D,), dtype=jnp.float32), 'beta': jnp.zeros((D,), dtype=jnp.float32)}
    _L0_mix_all = _L0_mix_setup()
    _L0_mix_in = {k: v for k, v in _L0_mix_all.items() if k in ('W_qk', 'b_qk', 'W_v', 'b_v', 'gamma', 'beta')}
    del _L0_mix_all

    def _L0_ffn_setup():
        import math
        import jax, jax.numpy as jnp
        import numpy as np
        CAPACITY_FACTOR = 1.25
        key = jax.random.key(seed)
        ks = jax.random.split(key, 5)
        B, L, D, F, E = (8, 1024, 256, 1024, 8)
        h = jax.random.normal(ks[0], (B, L, D), dtype=jnp.float32)
        gate_w = jax.random.normal(ks[1], (D, E), dtype=jnp.float32) * 0.02
        gate_b = jnp.zeros((E,), dtype=jnp.float32)
        w1 = jax.random.normal(ks[2], (E, D, F), dtype=jnp.float32) * (1.0 / math.sqrt(D))
        b1 = jnp.zeros((E, F), dtype=jnp.float32)
        w2 = jax.random.normal(ks[3], (E, F, D), dtype=jnp.float32) * (1.0 / math.sqrt(F))
        b2 = jnp.zeros((E, D), dtype=jnp.float32)
        return {'h': h, 'gate_w': gate_w, 'gate_b': gate_b, 'w1': w1, 'b1': b1, 'w2': w2, 'b2': b2}
    _L0_ffn_all = _L0_ffn_setup()
    _L0_ffn_in = {k: v for k, v in _L0_ffn_all.items() if k in ('gate_w', 'gate_b', 'w1', 'b1', 'w2', 'b2')}
    del _L0_ffn_all
    return {'x': x, 'src': src, 'dst': dst, 'L0_gnn_W_l': _L0_gnn_in['W_l'], 'L0_gnn_W_r': _L0_gnn_in['W_r'], 'L0_gnn_att': _L0_gnn_in['att'], 'L0_gnn_bias': _L0_gnn_in['bias'], 'L0_gnn_gamma': _L0_gnn_in['gamma'], 'L0_gnn_beta': _L0_gnn_in['beta'], 'L0_mix_W_qk': _L0_mix_in['W_qk'], 'L0_mix_b_qk': _L0_mix_in['b_qk'], 'L0_mix_W_v': _L0_mix_in['W_v'], 'L0_mix_b_v': _L0_mix_in['b_v'], 'L0_mix_gamma': _L0_mix_in['gamma'], 'L0_mix_beta': _L0_mix_in['beta'], 'L0_ffn_gate_w': _L0_ffn_in['gate_w'], 'L0_ffn_gate_b': _L0_ffn_in['gate_b'], 'L0_ffn_w1': _L0_ffn_in['w1'], 'L0_ffn_b1': _L0_ffn_in['b1'], 'L0_ffn_w2': _L0_ffn_in['w2'], 'L0_ffn_b2': _L0_ffn_in['b2']}

def reference(x, src, dst, L0_gnn_W_l, L0_gnn_W_r, L0_gnn_att, L0_gnn_bias, L0_gnn_gamma, L0_gnn_beta, L0_mix_W_qk, L0_mix_b_qk, L0_mix_W_v, L0_mix_b_v, L0_mix_gamma, L0_mix_beta, L0_ffn_gate_w, L0_ffn_gate_b, L0_ffn_w1, L0_ffn_b1, L0_ffn_w2, L0_ffn_b2):
    import jax
    import jax.numpy as jnp

    def _L0_gnn_ref(x, edge_index, W_l, W_r, att, bias, gamma, beta):
        import jax, jax.numpy as jnp
        import numpy as np
        N, E, IN_DIM, HEADS, HEAD_DIM = (2500, 40000, 256, 4, 64)
        OUT_DIM = HEADS * HEAD_DIM
        NEG_SLOPE = 0.2
        LN_EPS = 1e-05
        SM_EPS = 1e-16

        def _gatv2_block(x, edge_index, W_l, W_r, att, bias, gamma, beta):
            src, dst = (edge_index[0], edge_index[1])
            xl = (x @ W_l).reshape(N, HEADS, HEAD_DIM)
            xr = (x @ W_r).reshape(N, HEADS, HEAD_DIM)
            e = xl[src] + xr[dst]
            e = jnp.where(e >= 0, e, NEG_SLOPE * e)
            score = jnp.einsum('ehd,hd->eh', e, att)
            m = jax.ops.segment_max(score, dst, num_segments=N)
            m = jnp.where(jnp.isfinite(m), m, 0.0)
            ex = jnp.exp(score - m[dst])
            denom = jax.ops.segment_sum(ex, dst, num_segments=N)
            alpha = ex / (denom[dst] + SM_EPS)
            agg = jax.ops.segment_sum(alpha[:, :, None] * xl[src], dst, num_segments=N)
            out = agg.reshape(N, OUT_DIM) + bias
            h = jax.nn.elu(out) + x
            mu = jnp.mean(h, axis=-1, keepdims=True)
            var = jnp.mean(jnp.square(h - mu), axis=-1, keepdims=True)
            return (h - mu) * jax.lax.rsqrt(var + LN_EPS) * gamma + beta
        return _gatv2_block(x, edge_index, W_l, W_r, att, bias, gamma, beta)

    def _L0_mix_ref(feature, W_qk, b_qk, W_v, b_v, gamma, beta):
        import jax, jax.numpy as jnp
        import numpy as np
        BN_EPS = 1e-05
        QK = jnp.einsum('bnd,kde->bkne', feature, W_qk) + b_qk[None, :, None, :]
        value = jnp.einsum('bnd,de->bne', feature, W_v) + b_v
        query = QK[:, 0]
        key = QK[:, 1]
        sm = jax.nn.softmax(key, axis=1)
        lam = jnp.einsum('bnd,bne->bde', sm, value)
        mean = jnp.mean(lam, axis=(0, 2), keepdims=True)
        var = jnp.var(lam, axis=(0, 2), keepdims=True)
        bn = (lam - mean) * jax.lax.rsqrt(var + BN_EPS)
        bn = bn * gamma[None, :, None] + beta[None, :, None]
        return jnp.einsum('bnd,bde->bne', query, bn)

    def _L0_ffn_ref(h, gate_w, gate_b, w1, b1, w2, b2):
        import math
        import jax, jax.numpy as jnp
        import numpy as np
        CAPACITY_FACTOR = 1.25
        B, L, D = h.shape
        E = gate_w.shape[1]
        T = B * L
        C = max(1, math.ceil(CAPACITY_FACTOR * T / E))
        x = h.reshape(T, D)
        logits = x @ gate_w + gate_b
        probs = jax.nn.softmax(logits, axis=-1)
        idx = jnp.argmax(probs, axis=-1)
        prb = jnp.take_along_axis(probs, idx[:, None], axis=1)[:, 0]
        one_hot = jax.nn.one_hot(idx, E, dtype=jnp.float32)
        pos = (jnp.cumsum(one_hot, axis=0) * one_hot).sum(-1).astype(jnp.int32) - 1
        kept = pos < C
        pos_safe = jnp.where(kept, pos, C)
        buf = jnp.zeros((E, C, D), dtype=h.dtype).at[idx, pos_safe].set(x, mode='drop')
        hmid = jax.nn.relu(jnp.einsum('ecd,edf->ecf', buf, w1) + b1[:, None, :])
        ybuf = jnp.einsum('ecf,efd->ecd', hmid, w2) + b2[:, None, :]
        pos_g = jnp.minimum(pos, C - 1)
        y_tok = ybuf[idx, pos_g] * (prb * kept)[:, None]
        y = y_tok.reshape(B, L, D)
        y = jnp.nan_to_num(y, nan=0.0, posinf=10000.0, neginf=-10000.0)
        return y
    edge_index = jnp.stack([src, dst])
    xn = _layernorm(x, axis=-1)
    x = x + _L0_gnn_ref(xn, edge_index, L0_gnn_W_l, L0_gnn_W_r, L0_gnn_att, L0_gnn_bias, L0_gnn_gamma, L0_gnn_beta) + _L0_mix_ref(xn[None], L0_mix_W_qk, L0_mix_b_qk, L0_mix_W_v, L0_mix_b_v, L0_mix_gamma, L0_mix_beta)[0]
    x = x + _L0_ffn_ref(_layernorm(x, axis=-1)[None], L0_ffn_gate_w, L0_ffn_gate_b, L0_ffn_w1, L0_ffn_b1, L0_ffn_w2, L0_ffn_b2)[0]
    return x

_drawn_inputs = setup_inputs


def setup_inputs(seed=0):
    import zlib

    import numpy as np

    out = dict(_drawn_inputs(seed))
    spreads = {'L0_gnn_bias': (0.0, 0.8),
     'L0_gnn_gamma': (1.0, 0.6),
     'L0_gnn_beta': (0.0, 0.8),
     'L0_mix_b_qk': (0.0, 0.1),
     'L0_mix_b_v': (0.0, 0.1),
     'L0_mix_gamma': (1.0, 0.2),
     'L0_mix_beta': (0.0, 0.1),
     'L0_ffn_gate_b': (0.0, 0.8),
     'L0_ffn_b1': (0.0, 0.8),
     'L0_ffn_b2': (0.0, 2.0)}
    factors = {'L0_gnn_W_l': 4.913,
     'L0_gnn_W_r': 8.0,
     'L0_gnn_att': 8.0,
     'L0_ffn_gate_w': 8.0,
     'L0_ffn_w1': 8.0,
     'L0_ffn_w2': 8.0}
    for name, (base, spread) in spreads.items():
        noise = np.random.default_rng([zlib.crc32(name.encode()), seed]).standard_normal(out[name].shape)
        drawn = base * np.exp(spread * noise) if base else spread * noise
        out[name] = jnp.asarray(drawn.astype(out[name].dtype))
    for name, factor in factors.items():
        out[name] = (out[name] * factor).astype(out[name].dtype)
    return out
```

```python
from contextlib import ExitStack

import concourse.bass as bass
from concourse import mybir

F32 = mybir.dt.float32
BF16 = mybir.dt.bfloat16
I32 = mybir.dt.int32
I16 = mybir.dt.int16
U32 = mybir.dt.uint32
ALU = mybir.AluOpType
ACT = mybir.ActivationFunctionType
AX = mybir.AxisListType

P = 128
NODES, DIM = 2500, 256
HEADS, HEAD = 4, 64
EDGES = 80000
TILES = -(-NODES // P)
PAD = TILES * P
LAST = NODES - (TILES - 1) * P
G = 4
EDGES_STEP = G * P
BLOCKS = -(-EDGES // EDGES_STEP)
EDGES_PAD = BLOCKS * EDGES_STEP
STEPS = BLOCKS + TILES - 1
ECOLS = EDGES // P
ROW = DIM + HEADS
ROW3 = 3 * ROW + 4
HCOLS = HEAD + 1
RING = 4
BIG = 1e30
EXPERTS, FF = 8, 1024
CAP = -(-5 * NODES // (4 * EXPERTS))
FCH = FF // P
CT = -(-CAP // 4)
CTS = [CT, CT, CT, CAP - 3 * CT]
TRASH = EXPERTS * CAP
LN_EPS = 1e-5


def settle(eng, m):
    eng.sem_inc(m.met, 1)


class Chain:

    def __init__(self, eng, sem, base):
        self.eng, self.sem, self.base, self.n = eng, sem, base, 0

    def step(self, ins, settled=None):
        self.n += 1
        ins.then_inc(self.sem, 1)
        self.eng.wait_ge(self.sem, self.base + self.n)
        if settled:
            settle(self.eng, settled)


def over_tiles(eng, body, count=TILES):
    body(0, 0)
    body(1, 1)
    with eng.Fori(1, count // 2) as it:
        body(it * 2, 0)
        body(it * 2 + 1, 1)


def later(n):
    return not isinstance(n, int) or n >= 2



def sem_set(nc, ctx, prefix, names):
    sems = {}
    for name in names.split():
        if name[-1] == "*":
            sems[name[:-1]] = [ctx.enter_context(nc.semaphore(f"{prefix}_{name[:-1]}{i}")) for i in range(2)]
        else:
            sems[name] = ctx.enter_context(nc.semaphore(f"{prefix}_{name}"))
    return sems


class Memory:
    pass


class Arrays:
    pass


def memory(nc, ctx):
    m = Memory()

    def sb(name, shape, dt=F32):
        return ctx.enter_context(nc.sbuf_tensor(name, shape, dt))

    def dram(name, shape, dt=F32):
        return nc.dram_tensor(name, shape, dt, kind="Internal").ap()

    m.ident = sb("ident", [P, P])
    m.ones = sb("ones", [P, P])
    m.tri = sb("tri", [P, P])
    m.lane_row = sb("lane_row", [P, P], BF16)
    m.tile_ids = sb("tile_ids", [P, TILES, 2])
    m.expert_row = sb("expert_row", [P, EXPERTS])
    m.window = sb("window", [1, STEPS], I32)
    m.start = sb("start", [1, STEPS], I32)
    m.w_lr = sb("w_lr", [P, 2, 2 * DIM])
    m.w_q = sb("w_q", [P, 2, DIM])
    m.w_k = sb("w_k", [P, 2, DIM])
    m.w_v = sb("w_v", [P, 2, DIM])
    m.att_row = sb("att_row", [P, DIM])
    m.att_col = sb("att_col", [P, 2, HEADS])
    m.keys = sb("keys", [P, 2, PAD])
    m.w_mix = sb("w_mix", [P, 2, DIM])
    m.b_mix = sb("b_mix", [1, DIM])
    m.slot = sb("slot", [P, TILES], I32)
    m.share = sb("share", [P, TILES])
    m.bank = [ctx.enter_context(nc.psum_tensor(f"bank{i}", [P, 512], F32)) for i in range(8)]

    m.met = ctx.enter_context(nc.semaphore("met"))
    m.d_x = dram("d_x", (PAD, DIM))
    m.d_xn = dram("d_xn", (PAD, DIM))
    m.d_xnt = dram("d_xnt", (PAD, DIM))
    m.d_xl = dram("d_xl", (PAD, ROW))
    m.d_xr = dram("d_xr", (PAD, ROW3), BF16)
    m.d_src = dram("d_src", (EDGES_PAD,), I32)
    m.d_dst = dram("d_dst", (EDGES_PAD,))
    m.d_dst16 = dram("d_dst16", (EDGES_PAD,), I16)
    m.d_pen = dram("d_pen", (EDGES_PAD + P,))
    m.d_acc = dram("d_acc", (PAD, HEADS * HCOLS))
    m.d_x1 = dram("d_x1", (PAD, DIM))
    m.d_in = dram("d_in", (TRASH + PAD, DIM))
    m.d_out = dram("d_out", (TRASH, DIM))
    return m


def prepare(nc, ctx, m, a):
    sb = lambda name, shape, dt=F32: ctx.enter_context(nc.sbuf_tensor(name, shape, dt))
    s = sem_set(nc, m.sems, "pre", "weights att ids dst zero ident tri ones pool chain scaled edges cnt cntps cntsb step stepps xrows fill stored")
    dst = sb("p_dst", [P, ECOLS], I32)
    prev = sb("p_prev", [P, ECOLS], I32)
    dstf = sb("p_dstf", [P, ECOLS])
    prevf = sb("p_prevf", [P, ECOLS])
    junk = sb("p_junk", [P, ECOLS])
    dst16 = sb("p_dst16", [P, ECOLS], I16)
    pen = sb("p_pen", [P, ECOLS])
    padf = sb("p_padf", [P, 8])
    padpen = sb("p_padpen", [P, 8])
    pad16 = sb("p_pad16", [P, 8], I16)
    padi = sb("p_padi", [P, 8], I32)
    zero = sb("p_zero", [P, 2048])
    lane = sb("p_lane", [P, P], I32)
    ids = sb("p_ids", [P, TILES, 2], I32)
    eids = sb("p_eids", [P, EXPERTS], I32)
    limit = sb("p_limit", [TILES - 1, STEPS], I32)
    limitf = sb("p_limitf", [TILES - 1, STEPS])
    below = sb("p_below", [P, TILES - 1])
    cnt = sb("p_cnt", [TILES - 1, 1])
    passed = sb("p_passed", [TILES - 1, STEPS])
    att_raw = sb("p_att_raw", [P, DIM])
    tail = EDGES_PAD - EDGES
    TAILS = 48
    assert tail == TAILS * 8

    with nc.Block() as block:
        @block.sync
        def _(sp):
            sp.wait_ge(s["ones"], 8)
            flat = a.dst
            sp.dma_start(dst[:, :], flat.rearrange("(p c) -> p c", p=P)).then_inc(s["dst"], 16)
            sp.dma_start(prev[0:1, 1:ECOLS], flat[0:ECOLS - 1].unsqueeze(0)).then_inc(s["dst"], 16)
            sp.dma_start(prev[1:P, :], flat[ECOLS - 1:EDGES - 1].rearrange("(p c) -> p c", c=ECOLS)).then_inc(s["dst"], 16)
            sp.dma_start(m.d_src[0:EDGES].rearrange("(r c) -> r c", r=16), a.src.rearrange("(r c) -> r c", r=16)).then_inc(s["fill"], 16)
            sp.dma_start(m.d_x[0:NODES, :], a.x).then_inc(s["fill"], 16)
            for half in range(2):
                rows = slice(half * P, half * P + P)
                sp.dma_start(m.w_lr[:, half, 0:DIM], a.W_l[rows, :]).then_inc(s["weights"], 16)
                sp.dma_start(m.w_lr[:, half, DIM:2 * DIM], a.W_r[rows, :]).then_inc(s["weights"], 16)
                sp.dma_start(m.w_q[:, half, :], a.W_qk[0, rows, :]).then_inc(s["weights"], 16)
                sp.dma_start(m.w_k[:, half, :], a.W_qk[1, rows, :]).then_inc(s["weights"], 16)
                sp.dma_start(m.w_v[:, half, :], a.W_v[rows, :]).then_inc(s["weights"], 16)
            sp.dma_start(att_raw[:, :], a.att.rearrange("h c -> (h c)").partition_broadcast(P)).then_inc(s["att"], 16)
            for h in range(HEADS):
                lo = (h % 2) * HEAD
                sp.dma_start(m.att_col[lo:lo + HEAD, h // 2, h:h + 1], a.att[h, :].unsqueeze(1)).then_inc(s["att"], 16)
            sp.wait_ge(s["edges"], 3)
            for out, inn, pad in ((m.d_dst, dstf, padf[0:TAILS, :]), (m.d_dst16, dst16, pad16[0:TAILS, :]), (m.d_pen, pen, None)):
                sp.dma_start(out[0:EDGES].rearrange("(p c) -> p c", p=P), inn[:, :]).then_inc(s["stored"], 16)
                if pad is not None:
                    sp.dma_start(out[EDGES:EDGES_PAD].rearrange("(p c) -> p c", c=8), pad).then_inc(s["stored"], 16)
            sp.dma_start(m.d_pen[EDGES:EDGES_PAD + P].rearrange("(p c) -> p c", c=8), padpen[0:(tail + P) // 8, :]).then_inc(s["stored"], 16)
            sp.dma_start(m.d_src[EDGES:EDGES_PAD].rearrange("(p c) -> p c", c=8), padi[0:TAILS, :]).then_inc(s["stored"], 16)
            sp.dma_start(m.d_x[NODES:PAD, :], zero[0:PAD - NODES, 0:DIM]).then_inc(s["stored"], 16)
            total = TRASH * DIM
            for lo in range(0, total, P * 2048):
                n = min(P * 2048, total - lo) // 2048
                sp.dma_start(m.d_in.rearrange("r c -> (r c)")[lo:lo + n * 2048].rearrange("(p c) -> p c", c=2048),
                             zero[0:n, :]).then_inc(s["stored"], 16)
            sp.wait_ge(s["weights"], 160)
            sp.wait_ge(s["fill"], 32)
            sp.wait_ge(s["stored"], 16 * (8 + -(-total // (P * 2048))))

        @block.gpsimd
        def _(pool):
            pool.memset(prev[:, :], -1).then_inc(s["ones"], 1)
            pool.memset(m.att_col[:, :, :], 0.0).then_inc(s["ones"], 1)
            pool.memset(zero[:, :], 0.0).then_inc(s["ones"], 1)
            pool.memset(m.ones[:, :], 1.0).then_inc(s["ones"], 1)
            pool.memset(m.ident[:, :], 0.0).then_inc(s["ones"], 1)
            pool.memset(padf[:, :], 4095.0).then_inc(s["ones"], 1)
            pool.memset(padi[:, :], 0).then_inc(s["ones"], 1)
            pool.memset(padpen[:, :], -BIG).then_inc(s["ones"], 1)
            pool.iota(lane[:, :], [[1, P]], base=0, channel_multiplier=0).then_inc(s["ids"], 1)
            pool.iota(ids[:, :, 0], [[P, TILES]], base=0, channel_multiplier=1).then_inc(s["ids"], 1)
            pool.iota(ids[:, :, 1], [[P, TILES]], base=0, channel_multiplier=0).then_inc(s["ids"], 1)
            pool.iota(eids[:, :], [[1, EXPERTS]], base=0, channel_multiplier=0).then_inc(s["ids"], 1)
            pool.iota(limit[:, :], [[EDGES_STEP, STEPS]], base=0, channel_multiplier=-EDGES_STEP).then_inc(s["ids"], 1)
            pool.wait_ge(s["ones"], 8)
            pool.affine_select(out=m.ident[:, :], in_=m.ident[:, :], compare_op=ALU.not_equal, fill=1.0, base=0,
                               pattern=[[-1, P]], channel_multiplier=1).then_inc(s["ident"], 1)
            pool.affine_select(out=m.tri[:, :], in_=m.ones[:, :], compare_op=ALU.is_ge, fill=0.0, base=0,
                               pattern=[[1, P]], channel_multiplier=-1).then_inc(s["ident"], 1)

        @block.vector
        def _(dve):
            ch = Chain(dve, s["chain"], 0)
            dve.wait_ge(s["dst"], 48)
            ch.step(dve.tensor_copy(dstf[:, :], dst[:, :]))
            ch.step(dve.tensor_copy(prevf[:, :], prev[:, :]))
            ch.step(dve.tensor_tensor(pen[:, :], dstf[:, :], prevf[:, :], ALU.not_equal))
            dve.tensor_copy(dst16[:, :], dstf[:, :]).then_inc(s["edges"], 1)
            dve.tensor_scalar(pen[:, :], pen[:, :], -BIG, None, ALU.mult).then_inc(s["edges"], 1)
            dve.wait_ge(s["ones"], 8)
            dve.tensor_copy(pad16[:, :], padf[:, :]).then_inc(s["edges"], 1)
            for t in range(1, TILES):
                ch.step(dve.tensor_scalar(junk[:, :], dstf[:, :], float(P * t), 0.0, ALU.is_lt, ALU.add,
                                          accum_out=below[:, t - 1:t]))
            dve.wait_ge(s["ids"], 5)
            dve.tensor_copy(m.lane_row[:, :], lane[:, :]).then_inc(s["scaled"], 1)
            dve.tensor_copy(m.tile_ids[:, :, :], ids[:, :, :]).then_inc(s["scaled"], 1)
            dve.tensor_copy(m.expert_row[:, :], eids[:, :]).then_inc(s["scaled"], 1)
            dve.wait_ge(s["att"], 80)
            dve.tensor_scalar(m.att_row[:, :], att_raw[:, :], 0.2, None, ALU.mult).then_inc(s["scaled"], 1)
            dve.tensor_scalar(m.att_col[:, :, :], m.att_col[:, :, :], 0.8, None, ALU.mult).then_inc(s["scaled"], 1)
            ch.step(dve.tensor_copy(limitf[:, :], limit[:, :]))
            dve.wait_ge(s["cntps"], 1)
            ch.step(dve.tensor_copy(cnt[:, :], m.bank[0][0:TILES - 1, 0:1]))
            dve.tensor_scalar(passed[:, :], limitf[:, :], cnt[:, 0:1], None, ALU.is_gt).then_inc(s["step"], 1)
            dve.wait_ge(s["stepps"], 1)
            dve.tensor_copy(m.window[:, :], m.bank[1][0:1, 0:STEPS]).then_inc(s["step"], 1)
            dve.scalar_tensor_tensor(out=m.start[:, :], in0=m.bank[1][0:1, 0:STEPS], scalar=-float(EDGES_STEP),
                                     in1=limitf[0:1, :], op0=ALU.mult, op1=ALU.add).then_inc(s["step"], 1)

        @block.tensor
        def _(pe):
            pe.wait_ge(s["ones"], 8)
            pe.wait_ge(s["chain"], 3 + TILES - 1)
            pe.matmul(m.bank[0][0:TILES - 1, 0:1], below[:, :], m.ones[:, 0:1], start=True, stop=True).then_inc(s["cntps"], 1)
            pe.wait_ge(s["step"], 1)
            pe.matmul(m.bank[1][0:1, 0:STEPS], m.ones[0:TILES - 1, 0:1], passed[:, :], start=True, stop=True).then_inc(s["stepps"], 1)


def rstd_pool(pool, out, var, halves):
    return pool.tensor_tensor(out, var, halves, ALU.pow)


def project(nc, ctx, m, a):
    sb = lambda name, shape, dt=F32: ctx.enter_context(nc.sbuf_tensor(name, shape, dt))
    s = sem_set(nc, m.sems, "prj", "x* var rstd xn chain half xtps xt rows keysps keys xl hi hip mid xr stored* kst neg")
    xt = sb("a_x", [P, 2, DIM])
    st = sb("a_st", [P, 2, 6])
    mv = sb("a_mv", [P, 2, 2])
    ve = sb("a_ve", [P, 2, 1])
    rs = sb("a_rs", [P, 2, 1])
    neghalf = sb("a_neghalf", [P, 1])
    xn = sb("a_xn", [P, 2, DIM])
    xnt = sb("a_xnt", [P, 2, DIM])
    xl = sb("a_xl", [P, 2, ROW])
    xr = sb("a_xr", [P, 2, ROW])
    rest = sb("a_rest", [P, 2, ROW])
    tmp = sb("a_tmp", [P, DIM])
    xr3 = sb("a_xr3", [P, 2, ROW3], BF16)
    psx = [m.bank[0], m.bank[1]]
    pslr = [m.bank[2], m.bank[3]]
    psk = [m.bank[4], m.bank[5]]
    SP_IN = 16
    STORES = 64
    DV = 6 + 2

    with nc.Block() as block:
        @block.sync
        def _(sp):
            def tile(n, q):
                if later(n):
                    sp.wait_ge(s["xn"], n - 1)
                    settle(sp, m)
                sp.dma_start(xt[:, q, :], m.d_x[bass.ds(n * P, P), :]).then_inc(s["x"][q], SP_IN)
            over_tiles(sp, tile)

        @block.gpsimd
        def _(pool):
            pool.memset(neghalf[:, :], -0.5).then_inc(s["neg"], 1)
            pool.wait_ge(s["neg"], 1)

            def tile(n, q):
                rows = bass.ds(n * P, P)
                pool.wait_ge(s["var"], n + 1)
                rstd_pool(pool, rs[:, q, :], ve[:, q, :], neghalf[:, :]).then_inc(s["rstd"], 1)
                pool.wait_ge(s["xn"], n + 1)
                settle(pool, m)
                pool.dma_start(m.d_xn[rows, :], xn[:, q, :]).then_inc(s["stored"][q], 16)
                pool.wait_ge(s["xt"], n + 1)
                settle(pool, m)
                pool.dma_start(m.d_xnt[rows, :], xnt[:, q, :]).then_inc(s["stored"][q], 16)
                pool.wait_ge(s["xl"], n + 1)
                settle(pool, m)
                pool.dma_start(m.d_xl[rows, :], xl[:, q, :]).then_inc(s["stored"][q], 16)
                pool.wait_ge(s["xr"], n + 1)
                settle(pool, m)
                pool.dma_start(m.d_xr[rows, :], xr3[:, q, :]).then_inc(s["stored"][q], 16)
            over_tiles(pool, tile)
            for q in range(2):
                pool.wait_ge(s["stored"][q], STORES * (TILES // 2))

        @block.vector
        def _(dve):
            dve.wait_ge(s["neg"], 1)

            def tile(n, q):
                turn = (n + (1 - q) + 1) // 2 if isinstance(n, int) else None
                uses = n // 2 if isinstance(n, int) else (n - q) // 2
                ch = Chain(dve, s["chain"], n * 11)
                dve.wait_ge(s["x"][q], (uses + 1) * SP_IN)
                ch.step(dve.bn_stats(st[:, q, :], xt[:, q, :]), settled=m)
                ch.step(dve.bn_aggr(mv[:, q, :], st[:, q, :]))
                dve.tensor_scalar(ve[:, q, :], mv[:, q, 1:2], LN_EPS, None, ALU.add).then_inc(s["var"], 1)
                if later(n):
                    dve.wait_ge(s["stored"][q], uses * STORES)
                dve.wait_ge(s["rstd"], n + 1)
                dve.tensor_scalar(xn[:, q, :], xt[:, q, :], mv[:, q, 0:1], rs[:, q, 0:1], ALU.subtract,
                                  ALU.mult).then_inc(s["xn"], 1)
                dve.wait_ge(s["rows"], n + 1)
                lr = pslr[q]
                ch.step(dve.tensor_copy(xl[:, q, 0:DIM], lr[:, 0:DIM]))
                ch.step(dve.tensor_tensor(tmp[:, :], lr[:, 0:DIM], m.att_row[:, :], ALU.mult))
                dve.tensor_reduce(xl[:, q, DIM:ROW], tmp[:, :].rearrange("p (h c) -> p h c", h=HEADS), AX.X,
                                  ALU.add).then_inc(s["xl"], 1)
                dve.wait_ge(s["xl"], n + 1)
                ch.step(dve.tensor_copy(xr[:, q, 0:DIM], lr[:, DIM:2 * DIM]))
                ch.step(dve.tensor_tensor(tmp[:, :], lr[:, DIM:2 * DIM], m.att_row[:, :], ALU.mult))
                ch.step(dve.tensor_reduce(xr[:, q, DIM:ROW], tmp[:, :].rearrange("p (h c) -> p h c", h=HEADS), AX.X, ALU.add))
                ch.step(dve.tensor_copy(xr3[:, q, 0:ROW], xr[:, q, :]))
                ch.step(dve.tensor_tensor(rest[:, q, :], xr[:, q, :], xr3[:, q, 0:ROW], ALU.subtract))
                ch.step(dve.tensor_copy(xr3[:, q, ROW:2 * ROW], rest[:, q, :]))
                ch.step(dve.tensor_copy(xr3[:, q, 3 * ROW:ROW3].bitcast(F32), m.tile_ids[:, bass.ds(n, 1), :].rearrange("p t i -> p (t i)")))
                dve.tensor_tensor(xr3[:, q, 2 * ROW:3 * ROW], rest[:, q, :], xr3[:, q, ROW:2 * ROW],
                                  ALU.subtract).then_inc(s["xr"], 1)
                assert ch.n == 11
            over_tiles(dve, tile)
            dve.wait_ge(s["keys"], TILES)
            dve.memset(m.keys[:, :, NODES:PAD], -BIG).then_inc(s["kst"], 1)

        @block.tensor
        def _(pe):
            def tile(n, q):
                pe.wait_ge(s["xn"], n + 1)
                if later(n):
                    pe.wait_ge(s["xt"], n - 1)
                for half in range(2):
                    last = pe.transpose(psx[q][:, half * P:half * P + P], xn[:, q, half * P:half * P + P], m.ident[:, :])
                last.then_inc(s["xtps"], 1)
                pe.wait_ge(s["xt"], n + 1)
                if later(n):
                    pe.wait_ge(s["xr"], n - 1)
                    pe.wait_ge(s["keys"], n - 1)
                for half in range(2):
                    last = pe.matmul(pslr[q][:, :], xnt[:, q, half * P:half * P + P], m.w_lr[:, half, :],
                                     start=(half == 0), stop=(half == 1))
                last.then_inc(s["rows"], 1)
                for out in range(2):
                    for half in range(2):
                        last = pe.matmul(psk[q][:, out * P:out * P + P], m.w_k[:, half, out * P:out * P + P],
                                         xnt[:, q, half * P:half * P + P], start=(half == 0), stop=(half == 1))
                last.then_inc(s["keysps"], 1)
            over_tiles(pe, tile)

        @block.scalar
        def _(act):
            def tile(n, q):
                act.wait_ge(s["xtps"], n + 1)
                if later(n):
                    uses = n // 2 if isinstance(n, int) else (n - q) // 2
                    act.wait_ge(s["keysps"], n - 1)
                    act.wait_ge(s["stored"][q], uses * STORES)
                act.copy(xnt[:, q, :], psx[q][:, 0:DIM]).then_inc(s["xt"], 1)
                act.wait_ge(s["keysps"], n + 1)
                act.copy(m.keys[:, :, bass.ds(n * P, P)], psk[q][:, 0:DIM].rearrange("p (o n) -> p o n", o=2)).then_inc(s["keys"], 1)
            over_tiles(act, tile)


def lambdas(nc, ctx, m, a):
    sb = lambda name, shape, dt=F32: ctx.enter_context(nc.sbuf_tensor(name, shape, dt))
    s = sem_set(nc, m.sems, "lam", "const neg z xn* et etps en ctxps ctx chain lam var rstd wqps wq bn mixps mix")
    mx = sb("l_mx", [P, 2])
    neg = sb("l_neg", [P, 2])
    z = sb("l_z", [P, 2])
    rz = sb("l_rz", [P, 2])
    et = sb("l_et", [P, 2, 2, P])
    en = sb("l_en", [P, 2, DIM])
    xn = sb("l_xn", [P, 2, DIM])
    acc = sb("l_acc", [P, 2, DIM])
    lam = sb("l_lam", [P, 2, DIM])
    bn = sb("l_bn", [P, 2, DIM])
    bv = sb("l_bv", [P, DIM])
    cols = sb("l_cols", [P, 2, 3])
    st = sb("l_st", [P, 2, 6])
    mv = sb("l_mv", [P, 2, 2])
    ve = sb("l_ve", [P, 2])
    rs = sb("l_rs", [P, 2])
    sc = sb("l_sc", [P, 2])
    neghalf = sb("l_neghalf", [P, 2])
    wqt = sb("l_wqt", [P, 2, DIM])

    with nc.Block() as block:
        @block.sync
        def _(sp):
            sp.dma_start(bv[:, :], a.b_v.partition_broadcast(P)).then_inc(s["const"], 16)
            for half in range(2):
                for i, vec in enumerate((a.mix_gamma, a.mix_beta, a.b_qk[0, :])):
                    sp.dma_start(cols[:, half, i:i + 1], vec[half * P:half * P + P].unsqueeze(1)).then_inc(s["const"], 16)

            def tile(n, q):
                if later(n):
                    sp.wait_ge(s["ctxps"], n - 1)
                    settle(sp, m)
                sp.dma_start(xn[:, q, :], m.d_xn[bass.ds(n * P, P), :]).then_inc(s["xn"][q], 16)
            over_tiles(sp, tile)
            sp.wait_ge(s["const"], 16 * 7)

        @block.scalar
        def _(act):
            act.wait_ge(s["neg"], 2)
            for half in range(2):
                act.activation(m.keys[:, half, :], m.keys[:, half, :], ACT.Exp, bias=neg[:, half:half + 1],
                               accum_out=z[:, half:half + 1]).then_inc(s["z"], 1)
            act.wait_ge(s["z"], 2)

            def tile(n, q):
                if later(n):
                    act.wait_ge(s["etps"], n - 1)
                act.copy(et[:, q, :, :], m.keys[:, :, bass.ds(n * P, P)]).then_inc(s["et"], 1)
            over_tiles(act, tile)

        @block.gpsimd
        def _(pool):
            pool.memset(neghalf[:, :], -0.5).then_inc(s["rstd"], 1)
            pool.wait_ge(s["rstd"], 1)
            pool.wait_ge(s["var"], 1)
            rstd_pool(pool, rs[:, :], ve[:, :], neghalf[:, :]).then_inc(s["rstd"], 1)

        @block.vector
        def _(dve):
            ch = Chain(dve, s["chain"], 0)
            for half in range(2):
                ch.step(dve.tensor_reduce(mx[:, half:half + 1], m.keys[:, half, :], AX.X, ALU.max))
                dve.tensor_scalar(neg[:, half:half + 1], mx[:, half:half + 1], -1.0, None, ALU.mult).then_inc(s["neg"], 1)
            ch.step(dve.memset(acc[:, :, :], 0.0))

            def tile(n, q):
                dve.wait_ge(s["etps"], n + 1)
                if later(n):
                    dve.wait_ge(s["ctxps"], n - 1)
                dve.tensor_copy(en[:, q, :], m.bank[q][:, 0:DIM]).then_inc(s["en"], 1)
                dve.wait_ge(s["ctxps"], n + 1)
                flat = acc[:, :, :].rearrange("p h d -> p (h d)")
                dve.tensor_tensor(flat, flat, m.bank[2 + q][:, :], ALU.add).then_inc(s["ctx"], 1)
                dve.wait_ge(s["ctx"], n + 1)
            over_tiles(dve, tile)
            dve.wait_ge(s["z"], 2)
            dve.wait_ge(s["const"], 16 * 7)
            ch.step(dve.reciprocal(rz[:, :], z[:, :]))
            dve.wait_ge(s["lam"], 1)
            for half in range(2):
                ch.step(dve.scalar_tensor_tensor(out=lam[:, half, :], in0=m.bank[4 + half][:, 0:DIM],
                                                 scalar=rz[:, half:half + 1], in1=bv[:, :], op0=ALU.mult, op1=ALU.add))
                ch.step(dve.bn_stats(st[:, half, :], lam[:, half, :]), settled=m)
                ch.step(dve.bn_aggr(mv[:, half, :], st[:, half, :]))
            dve.tensor_scalar(ve[:, :], mv[:, :, 1], LN_EPS, None, ALU.add).then_inc(s["var"], 1)
            dve.wait_ge(s["rstd"], 2)
            ch.step(dve.tensor_tensor(sc[:, :], rs[:, :], cols[:, :, 0], ALU.mult))
            for half in range(2):
                ch.step(dve.tensor_scalar(lam[:, half, :], lam[:, half, :], mv[:, half, 0:1], sc[:, half:half + 1],
                                          ALU.subtract, ALU.mult))
                dve.tensor_scalar(bn[:, half, :], lam[:, half, :], cols[:, half, 1:2], None, ALU.add).then_inc(s["bn"], 1)
            dve.wait_ge(s["wqps"], 1)
            dve.tensor_copy(wqt[:, :, :].rearrange("p h d -> p (h d)"), m.bank[6][:, :]).then_inc(s["wq"], 1)
            dve.wait_ge(s["mixps"], 1)
            for half in range(2):
                dve.tensor_copy(m.w_mix[:, half, :], m.bank[half][:, 0:DIM]).then_inc(s["mix"], 1)
            dve.tensor_copy(m.b_mix[:, :], m.bank[2][0:1, 0:DIM]).then_inc(s["mix"], 1)

        @block.tensor
        def _(pe):
            def tile(n, q):
                pe.wait_ge(s["et"], n + 1)
                if later(n):
                    pe.wait_ge(s["en"], n - 1)
                for half in range(2):
                    last = pe.transpose(m.bank[q][:, half * P:half * P + P], et[:, q, half, :], m.ident[:, :])
                last.then_inc(s["etps"], 1)
                pe.wait_ge(s["en"], n + 1)
                uses = n // 2 if isinstance(n, int) else (n - q) // 2
                pe.wait_ge(s["xn"][q], (uses + 1) * 16)
                if later(n):
                    pe.wait_ge(s["ctx"], n - 1)
                for half in range(2):
                    last = pe.matmul(m.bank[2 + q][:, half * DIM:half * DIM + DIM], xn[:, q, half * P:half * P + P],
                                     en[:, q, :], start=True, stop=True)
                last.then_inc(s["ctxps"], 1)
            over_tiles(pe, tile)
            for half in range(2):
                for inn in range(2):
                    last = pe.transpose(m.bank[6][:, half * DIM + inn * P:half * DIM + inn * P + P],
                                        m.w_q[:, inn, half * P:half * P + P], m.ident[:, :])
            last.then_inc(s["wqps"], 1)
            pe.wait_ge(s["ctx"], TILES)
            for half in range(2):
                for inn in range(2):
                    last = pe.matmul(m.bank[4 + half][:, 0:DIM], acc[:, inn, half * P:half * P + P], m.w_v[:, inn, :],
                                     start=(inn == 0), stop=(inn == 1))
            last.then_inc(s["lam"], 1)
            pe.wait_ge(s["bn"], 2)
            pe.wait_ge(s["wq"], 1)
            for inn in range(2):
                for half in range(2):
                    pe.matmul(m.bank[inn][:, 0:DIM], wqt[:, half, inn * P:inn * P + P], bn[:, half, :],
                              start=(half == 0), stop=(half == 1))
            for half in range(2):
                last = pe.matmul(m.bank[2][0:1, 0:DIM], cols[:, half, 2:3], bn[:, half, :], start=(half == 0), stop=(half == 1))
            last.then_inc(s["mixps"], 1)


def attend(nc, ctx, m, a):
    sb = lambda name, shape, dt=F32: ctx.enter_context(nc.sbuf_tensor(name, shape, dt))
    s = sem_set(nc, m.sems, "att", "init base sel relu score_e acc_chain scoreps score scoret scan mps diff rr rd rps p ex agg f acc chain stored*")
    loaded = [m.sems.enter_context(nc.semaphore(f"att_loaded{r}")) for r in range(RING)]
    gathered = [m.sems.enter_context(nc.semaphore(f"att_gathered{r}")) for r in range(RING)]
    idx = [sb(f"e_idx{r}", [P, G], I32) for r in range(RING)]
    dcol = sb("e_dcol", [P, RING, G])
    drow = sb("e_drow", [P, RING, EDGES_STEP], I16)
    pen = sb("e_pen", [HEADS, RING, EDGES_STEP + 1])
    xr3 = sb("e_xr3", [P, RING, ROW3], BF16)
    xl = [sb(f"e_xl{r}", [P, G, ROW]) for r in range(RING)]
    base = sb("e_base", [P, 2])
    drel = sb("e_drel", [P, G])
    sel = sb("e_sel", [P, 2, EDGES_STEP], BF16)
    selt = sb("e_selt", [P, RING, G, P])
    first = sb("e_first", [P, RING])
    same = sb("e_same", [P, RING])
    gate = sb("e_gate", [HEADS, 1])
    carry = sb("e_carry", [HEADS, 1])
    relu = sb("e_relu", [P, 2, EDGES_STEP])
    score = sb("e_score", [P, 2, G, HEADS])
    run = sb("e_run", [HEADS, EDGES_STEP])
    top = sb("e_top", [HEADS, 2, EDGES_STEP])
    drop = sb("e_drop", [HEADS, 2])
    rr = sb("e_rr", [HEADS, 2])
    rd = sb("e_rd", [HEADS, 2, HEADS])
    diff = sb("e_diff", [P, G, HEADS])
    prod = sb("e_prod", [P, 2, G, HEADS, HCOLS])
    fac = sb("e_fac", [P, HEADS])
    facs = sb("e_facs", [P, HEADS])
    old = sb("e_old", [P, HEADS, HCOLS])
    acc = sb("e_acc", [P, 2, HEADS, HCOLS])

    ps_e = [m.bank[0], m.bank[1]]
    ps_score = m.bank[2][:, 0:G * HEADS]
    ps_scoret = m.bank[3][0:HEADS, :]
    ps_top = m.bank[4][:, 0:G * HEADS]
    ps_ex = m.bank[5][:, 0:G * HEADS]
    ps_r = m.bank[6][:, 0:HEADS]
    ps_agg = m.bank[7][:, 0:HEADS * HCOLS]
    LOADS = 5 * 16
    TURNS = STEPS // RING
    assert STEPS % RING == 0

    def since(k, first_step):
        return not isinstance(k, int) or k >= first_step

    def is_step(k):
        return not isinstance(k, int) or 0 <= k < STEPS

    def over_steps(eng, body, head=1, behind=0):
        for k in range(head * RING):
            body(k, k % RING, k // RING)
        with eng.Fori(head, TURNS - 1) as it:
            for j in range(RING):
                body(it * RING + j, j, it)
        for k in range(STEPS - RING, STEPS + behind):
            body(k, k % RING, k // RING)

    with nc.Block() as block:
        @block.sync
        def _(sp):
            def store(k, q, uses):
                sp.wait_ge(s["acc"], k + 1)
                if since(k, 1):
                    sp.wait_ge(s["stored"][1 - q], 16 * (uses + q))
                    settle(sp, m)
                t = sp.value_load(m.window[0:1, bass.ds(k, 1)], min_val=0, max_val=TILES - 1)
                sp.dma_start(m.d_acc[bass.ds(t * P, P), :], acc[:, q, :, :].rearrange("p h c -> p (h c)")).then_inc(s["stored"][q], 16)

            def load(k, r, turn):
                if since(k, RING):
                    sp.wait_ge(gathered[r], turn * 64)
                    settle(sp, m)
                    sp.wait_ge(s["scoreps"], k - RING + 1)
                    sp.wait_ge(s["scan"], k - RING + 1)
                    settle(sp, m)
                t = sp.value_load(m.window[0:1, bass.ds(k, 1)], min_val=0, max_val=TILES - 1)
                block_at = sp.value_load(m.start[0:1, bass.ds(k, 1)], min_val=0, max_val=EDGES_PAD - EDGES_STEP)
                edges = bass.ds(block_at, EDGES_STEP)
                sp.dma_start(idx[r][:, :], m.d_src[edges].rearrange("(p g) -> p g", g=G)).then_inc(loaded[r], 16)
                sp.dma_start(dcol[:, r, :], m.d_dst[edges].rearrange("(p g) -> p g", g=G)).then_inc(loaded[r], 16)
                sp.dma_start(drow[:, r, :], m.d_dst16[edges].partition_broadcast(P)).then_inc(loaded[r], 16)
                sp.dma_start(pen[:, r, :], m.d_pen[bass.ds(block_at, EDGES_STEP + 1)].partition_broadcast(HEADS)).then_inc(loaded[r], 16)
                sp.dma_start(xr3[:, r, :], m.d_xr[bass.ds(t * P, P), :]).then_inc(loaded[r], 16)

            def step(k, r, turn):
                if is_step(k):
                    load(k, r, turn)
                if since(k, RING):
                    store(k - RING, r % 2, (turn - 1) * (RING // 2) + r // 2)
            over_steps(sp, step, head=2, behind=RING)
            for q in range(2):
                sp.wait_ge(s["stored"][q], 16 * (STEPS // 2))

        @block.gpsimd
        def _(pool):
            pool.memset(base[:, :], -1.0).then_inc(s["init"], 1)
            pool.memset(acc[:, :, :, :], 0.0).then_inc(s["init"], 1)
            pool.memset(top[:, :, :], -BIG).then_inc(s["init"], 1)

            def gather(k, r, turn):
                pool.wait_ge(loaded[r], (turn + 1) * LOADS)
                if since(k, RING):
                    pool.wait_ge(s["p"], k - RING + 1)
                settle(pool, m)
                for g in range(G):
                    pool.indirect_dma_start(xl[r][:, g, :], None, m.d_xl, bass.IndirectOffsetOnAxis(
                        ap=idx[r][:, g:g + 1], axis=0)).then_inc(gathered[r], 16)
            over_steps(pool, gather)

        @block.vector
        def _(dve):
            dve.wait_ge(s["init"], 3)

            def select(k, r, turn):
                q = r % 2
                ch = Chain(dve, s["base"], k * 3)
                dve.wait_ge(loaded[r], (turn + 1) * LOADS)
                number = xr3[:, r, 3 * ROW:3 * ROW + 2].bitcast(F32)
                start = xr3[:, r, 3 * ROW + 2:ROW3].bitcast(F32)
                dve.tensor_scalar(sel[:, q, :], drow[:, r, :], number, None, ALU.is_equal).then_inc(s["sel"], 1)
                dve.tensor_scalar(first[:, r:r + 1], drow[:, r, 0:1], number, None, ALU.is_equal)
                ch.step(dve.tensor_scalar(drel[:, :], dcol[:, r, :], start, None, ALU.subtract))
                ch.step(dve.tensor_copy(base[:, q:q + 1], start))
                for g in range(G):
                    dve.tensor_scalar(selt[:, r, g, :], m.lane_row[:, :], drel[:, g:g + 1], None, ALU.is_equal)
                ch.step(dve.tensor_scalar(same[:, r:r + 1], base[:, q:q + 1], base[:, 1 - q:2 - q], None, ALU.is_equal))

            def close_score(k, r, turn):
                q = r % 2
                dve.wait_ge(s["scoreps"], k + 1)
                dve.wait_ge(gathered[r], (turn + 1) * 64)
                dve.tensor_tensor(score[:, q, :, :], ps_score.rearrange("p (g h) -> p g h", g=G),
                                  xl[r][:, :, DIM:ROW], ALU.add).then_inc(s["score"], 1)
                ch = Chain(dve, s["chain"], k * 3)
                ch.step(dve.tensor_scalar(gate[:, :], same[0:HEADS, r:r + 1], -1.0, BIG, ALU.add, ALU.mult))
                ch.step(dve.tensor_tensor(carry[:, :], top[:, 1 - q, EDGES_STEP - 1:EDGES_STEP], gate[:, :], ALU.add))

            def maximum(k, r):
                q = r % 2
                ch = Chain(dve, s["chain"], k * 3 + 2)
                dve.wait_ge(s["scoret"], k + 1)
                ch.step(dve.tensor_tensor_scan(run[:, :], pen[:, r, 0:EDGES_STEP], ps_scoret, carry[:, 0:1], ALU.add, ALU.max))
                back = slice(None, None, -1)
                dve.tensor_tensor_scan(top[:, q, back], pen[:, r, 1:EDGES_STEP + 1][:, back], run[:, back], -BIG,
                                       ALU.add, ALU.max).then_inc(s["scan"], 1)
                dve.wait_ge(s["scan"], k + 1)
                dve.tensor_scalar(drop[:, q:q + 1], carry[:, :], top[:, q, 0:1], 0.0, ALU.subtract, ALU.min).then_inc(s["f"], 1)

            def weigh(k, r):
                q = r % 2
                dve.wait_ge(s["mps"], k + 1)
                dve.tensor_tensor(diff[:, :, :], score[:, q, :, :], ps_top.rearrange("p (g h) -> p g h", g=G),
                                  ALU.subtract).then_inc(s["diff"], 1)
                dve.wait_ge(s["ex"], k + 1)
                ex = ps_ex.rearrange("p (g h) -> p g h", g=G)
                dve.tensor_copy(prod[:, q, :, :, HEAD:HCOLS], ex.unsqueeze(3))
                dve.tensor_tensor(prod[:, q, :, :, 0:HEAD], xl[r][:, :, 0:DIM].rearrange("p g (h c) -> p g h c", h=HEADS),
                                  ex.unsqueeze(3).to_broadcast([P, G, HEADS, HEAD]), ALU.mult).then_inc(s["p"], 1)
                dve.wait_ge(s["rr"], k + 1)
                dve.tensor_scalar(rd[:, q, :], m.ident[0:HEADS, 0:HEADS], rr[:, q:q + 1], None, ALU.mult).then_inc(s["rd"], 1)

            def add_sums(k, r, uses):
                q = r % 2
                ch = Chain(dve, s["acc_chain"], k * 3)
                dve.wait_ge(s["rps"], k + 1)
                ch.step(dve.tensor_scalar(fac[:, :], ps_r, -1.0, first[:, r:r + 1], ALU.add, ALU.mult))
                ch.step(dve.tensor_scalar(facs[:, :], fac[:, :], 1.0, same[:, r:r + 1], ALU.add, ALU.mult))
                ch.step(dve.tensor_tensor(old[:, :, :], acc[:, 1 - q, :, :],
                                          facs[:, :].unsqueeze(2).to_broadcast([P, HEADS, HCOLS]), ALU.mult))
                dve.wait_ge(s["agg"], k + 1)
                if since(k, 2):
                    dve.wait_ge(s["stored"][q], 16 * uses)
                dve.tensor_tensor(acc[:, q, :, :], old[:, :, :], ps_agg.rearrange("p (h c) -> p h c", h=HEADS),
                                  ALU.add).then_inc(s["acc"], 1)
                dve.wait_ge(s["acc"], k + 1)

            def step(k, r, turn):
                before, two_before = (r - 1) % RING, (r - 2) % RING
                if since(k, 1) and is_step(k - 1):
                    close_score(k - 1, before, turn if r >= 1 else turn - 1)
                if is_step(k + 1):
                    select(k + 1, (r + 1) % RING, turn if r + 1 < RING else turn + 1)
                if since(k, 1) and is_step(k - 1):
                    maximum(k - 1, before)
                    weigh(k - 1, before)
                if since(k, 2):
                    add_sums(k - 2, two_before, turn * (RING // 2) + (r - 2) // 2)
            select(0, 0, 0)
            over_steps(dve, step, behind=2)

        @block.tensor
        def _(pe):
            def edge_features(k, r, turn, half):
                q = r % 2
                if half == 0:
                    pe.wait_ge(s["sel"], k + 1)
                if since(k, 1):
                    pe.wait_ge(s["relu"], 2 * k - 1 + half)

                def of_nodes(part):
                    at = part * ROW + half * P
                    return pe.matmul(ps_e[half][:, :], xr3[:, r, at:at + P], sel[:, q, :], start=(part == 0),
                                     stop=(part == 2))
                of_nodes(0)
                of_nodes(1)
                if half == 0:
                    pe.wait_ge(gathered[r], (turn + 1) * 64)
                for g in range(G):
                    pe.matmul(ps_e[half][:, g::G], xl[r][:, g, half * P:half * P + P], m.ident[:, :],
                              start=False, stop=False)
                last = of_nodes(2)
                last.then_inc(s["score_e"], 1)

            def tops(k, q):
                pe.wait_ge(s["scan"], k + 1)
                if since(k, 1):
                    pe.wait_ge(s["diff"], k)
                settle(pe, m)
                for g in range(G):
                    last = pe.transpose(ps_top[:, g * HEADS:(g + 1) * HEADS], top[:, q, g::G], m.ident[0:HEADS, 0:HEADS])
                last.then_inc(s["mps"], 1)

            def scores(k, r):
                q = r % 2
                pe.wait_ge(s["relu"], 2 * k + 2)
                if since(k, 1):
                    pe.wait_ge(s["score"], k)
                for g in range(G):
                    out = ps_score[:, g * HEADS:(g + 1) * HEADS]
                    for half in range(2):
                        pe.matmul(out, relu[:, half, g::G], m.att_col[:, half, :], start=(half == 0), stop=False)
                    for part in range(3):
                        last = pe.matmul(out, sel[:, q, g::G], xr3[:, r, part * ROW + DIM:(part + 1) * ROW],
                                         start=False, stop=(part == 2))
                last.then_inc(s["scoreps"], 1)

            def score_rows(k, q):
                pe.wait_ge(s["score"], k + 1)
                if since(k, 1):
                    pe.wait_ge(s["scan"], k)
                for g in range(G):
                    last = pe.transpose(ps_scoret[:, g::G], score[:, q, g, :], m.ident[:, :])
                last.then_inc(s["scoret"], 1)

            def sums(k, r):
                q = r % 2
                pe.wait_ge(s["rd"], k + 1)
                if since(k, 1):
                    pe.wait_ge(s["acc"], k)
                pe.matmul(ps_r, m.ones[0:HEADS, :], rd[:, q, :], start=True, stop=True).then_inc(s["rps"], 1)
                pe.wait_ge(s["p"], k + 1)
                for g in range(G):
                    last = pe.matmul(ps_agg, selt[:, r, g, :], prod[:, q, g, :, :].rearrange("p h c -> p (h c)"),
                                     start=(g == 0), stop=(g == G - 1))
                last.then_inc(s["agg"], 1)

            def step(k, r, turn):
                if is_step(k):
                    edge_features(k, r, turn, 0)
                if since(k, 1) and is_step(k - 1):
                    score_rows(k - 1, 1 - r % 2)
                if is_step(k):
                    edge_features(k, r, turn, 1)
                if since(k, 1) and is_step(k - 1):
                    tops(k - 1, 1 - r % 2)
                if since(k, 2):
                    sums(k - 2, (r - 2) % RING)
                if is_step(k):
                    scores(k, r)
            over_steps(pe, step, behind=2)

        @block.scalar
        def _(act):
            def rescale(k, q):
                act.wait_ge(s["f"], k + 1)
                act.activation(rr[:, q:q + 1], drop[:, q:q + 1], ACT.Exp).then_inc(s["rr"], 1)

            def relus(k, half):
                act.wait_ge(s["score_e"], 2 * k + 1 + half)
                if since(k, 1):
                    act.wait_ge(s["scoreps"], k)
                act.activation(relu[:, half, :], ps_e[half][:, :], ACT.Relu).then_inc(s["relu"], 1)

            def weights(k):
                act.wait_ge(s["diff"], k + 1)
                if since(k, 1):
                    act.wait_ge(s["p"], k)
                act.activation(ps_ex, diff[:, :, :].rearrange("p g h -> p (g h)"), ACT.Exp).then_inc(s["ex"], 1)

            def step(k, r, turn):
                if is_step(k):
                    relus(k, 0)
                if since(k, 1):
                    rescale(k - 1, 1 - r % 2)
                if is_step(k):
                    relus(k, 1)
                if since(k, 1):
                    weights(k - 1)
            over_steps(act, step, behind=1)


def node_update(nc, ctx, m, a):
    sb = lambda name, shape, dt=F32: ctx.enter_context(nc.sbuf_tensor(name, shape, dt))
    s = sem_set(nc, m.sems, "upd", "const in* mixps low low_e var rstd chain x1 norm normps normt logits gex gexed oh posps slot stored* neg")
    bias = sb("u_bias", [P, DIM])
    gamma = sb("u_gamma", [P, DIM])
    beta = sb("u_beta", [P, DIM])
    gate_w = sb("u_gate_w", [P, 2, EXPERTS])
    gate_b = sb("u_gate_b", [1, EXPERTS])
    xt = sb("u_xt", [P, 2, DIM])
    xn = sb("u_xn", [P, 2, DIM])
    xnt = sb("u_xnt", [P, 2, DIM])
    acc = sb("u_acc", [P, 2, HEADS, HCOLS])
    den = sb("u_den", [P, 2, HEADS])
    out = sb("u_out", [P, DIM])
    low = sb("u_low", [P, DIM])
    lowe = sb("u_lowe", [P, DIM])
    hid = sb("u_hid", [P, DIM])
    st = sb("u_st", [P, 6])
    mv = sb("u_mv", [P, 2])
    ve = sb("u_ve", [P, 1])
    rs = sb("u_rs", [P, 1])
    neghalf = sb("u_neghalf", [P, 1])
    x1 = sb("u_x1", [P, 2, DIM])
    norm = [sb(f"u_norm{q}", [P, DIM]) for q in range(2)]
    normt = sb("u_normt", [P, DIM])
    lg = sb("u_lg", [P, EXPERTS])
    mx = sb("u_mx", [P, 1])
    ex = sb("u_ex", [P, EXPERTS])
    tot = sb("u_tot", [P, 1])
    rtot = sb("u_rtot", [P, 1])
    prob = sb("u_prob", [P, EXPERTS])
    best = sb("u_best", [P, 1])
    cand = sb("u_cand", [P, EXPERTS])
    which = sb("u_which", [P, 1])
    hot = sb("u_hot", [P, EXPERTS])
    seen = sb("u_seen", [P, EXPERTS])
    pos = sb("u_pos", [P, EXPERTS])
    posr = sb("u_posr", [P, 1])
    kept = sb("u_kept", [P, 1])
    first = sb("u_first", [P, 1])
    at = sb("u_at", [P, 1])
    trash = sb("u_trash", [P, 1])
    place = [sb(f"u_place{q}", [P, 1], I32) for q in range(2)]
    ps_mix = [m.bank[0], m.bank[1]]
    ps_t = m.bank[2]
    ps_log = m.bank[3][:, 0:EXPERTS]
    ps_pos = m.bank[4][:, 0:EXPERTS]
    CH = 30

    with nc.Block() as block:
        @block.sync
        def _(sp):
            for t, vec in ((bias, a.bias), (gamma, a.gamma), (beta, a.beta)):
                sp.dma_start(t[:, :], vec.partition_broadcast(P)).then_inc(s["const"], 16)
            for half in range(2):
                sp.dma_start(gate_w[:, half, :], a.gate_w[half * P:half * P + P, :]).then_inc(s["const"], 16)
            sp.dma_start(gate_b[:, :], a.gate_b.unsqueeze(0)).then_inc(s["const"], 16)

            def tile(n, q):
                rows = bass.ds(n * P, P)
                if later(n):
                    sp.wait_ge(s["x1"], n - 1)
                    settle(sp, m)
                for t, d in ((xt, m.d_x), (xn, m.d_xn), (xnt, m.d_xnt)):
                    sp.dma_start(t[:, q, :], d[rows, :]).then_inc(s["in"][q], 16)
                sp.dma_start(acc[:, q, :, :].rearrange("p h c -> p (h c)"), m.d_acc[rows, :]).then_inc(s["in"][q], 16)
            over_tiles(sp, tile)
            sp.wait_ge(s["const"], 96)

        @block.gpsimd
        def _(pool):
            pool.memset(neghalf[:, :], -0.5).then_inc(s["neg"], 1)
            pool.memset(seen[:, :], 0.0).then_inc(s["neg"], 1)
            pool.wait_ge(s["neg"], 2)

            def tile(n, q):
                pool.wait_ge(s["var"], n * 2 + 1)
                rstd_pool(pool, rs[:, :], ve[:, :], neghalf[:, :]).then_inc(s["rstd"], 1)
                pool.wait_ge(s["var"], n * 2 + 2)
                rstd_pool(pool, rs[:, :], ve[:, :], neghalf[:, :]).then_inc(s["rstd"], 1)
                pool.wait_ge(s["x1"], n + 1)
                settle(pool, m)
                pool.dma_start(m.d_x1[bass.ds(n * P, P), :], x1[:, q, :]).then_inc(s["stored"][q], 16)
                pool.wait_ge(s["slot"], n + 1)
                settle(pool, m)
                pool.indirect_dma_start(m.d_in, bass.IndirectOffsetOnAxis(ap=place[q][:, 0:1], axis=0),
                                        norm[q][:, :], None).then_inc(s["stored"][q], 16)
            over_tiles(pool, tile)
            for q in range(2):
                pool.wait_ge(s["stored"][q], 32 * (TILES // 2))

        @block.scalar
        def _(act):
            def tile(n, q):
                act.wait_ge(s["low"], n + 1)
                act.activation(lowe[:, :], low[:, :], ACT.Exp).then_inc(s["low_e"], 1)
                act.wait_ge(s["normps"], n + 1)
                act.copy(normt[:, :], ps_t[:, 0:DIM]).then_inc(s["normt"], 1)
                act.wait_ge(s["gex"], n + 1)
                act.activation(ex[:, :], lg[:, :], ACT.Exp, accum_out=tot[:, 0:1]).then_inc(s["gexed"], 1)
            over_tiles(act, tile)

        @block.vector
        def _(dve):
            dve.wait_ge(s["const"], 96)
            dve.wait_ge(s["neg"], 2)

            def tile(n, q):
                uses = n // 2 if isinstance(n, int) else (n - q) // 2
                ch = Chain(dve, s["chain"], n * CH)
                heads = lambda t: t.rearrange("p (h c) -> p h c", h=HEADS)
                dve.wait_ge(s["in"][q], (uses + 1) * 64)
                ch.step(dve.tensor_scalar(den[:, q, :], acc[:, q, :, HEAD], 1e-16, None, ALU.add))
                ch.step(dve.reciprocal(den[:, q, :], den[:, q, :]))
                ch.step(dve.tensor_tensor(heads(out[:, :]), acc[:, q, :, 0:HEAD], den[:, q, :].unsqueeze(2).to_broadcast([P, HEADS, HEAD]), ALU.mult))
                ch.step(dve.tensor_tensor(out[:, :], out[:, :], bias[:, :], ALU.add))
                dve.tensor_scalar(low[:, :], out[:, :], 0.0, None, ALU.min).then_inc(s["low"], 1)
                dve.wait_ge(s["low_e"], n + 1)
                ch.step(dve.scalar_tensor_tensor(out=hid[:, :], in0=out[:, :], scalar=0.0, in1=lowe[:, :], op0=ALU.max, op1=ALU.add))
                ch.step(dve.scalar_tensor_tensor(out=hid[:, :], in0=hid[:, :], scalar=-1.0, in1=xn[:, q, :], op0=ALU.add, op1=ALU.add))
                ch.step(dve.bn_stats(st[:, :], hid[:, :]), settled=m)
                ch.step(dve.bn_aggr(mv[:, :], st[:, :]))
                dve.tensor_scalar(ve[:, :], mv[:, 1:2], LN_EPS, None, ALU.add).then_inc(s["var"], 1)
                dve.wait_ge(s["rstd"], n * 2 + 1)
                ch.step(dve.tensor_scalar(hid[:, :], hid[:, :], mv[:, 0:1], rs[:, 0:1], ALU.subtract, ALU.mult))
                ch.step(dve.tensor_tensor(hid[:, :], hid[:, :], gamma[:, :], ALU.mult))
                ch.step(dve.tensor_tensor(hid[:, :], hid[:, :], beta[:, :], ALU.add))
                ch.step(dve.tensor_tensor(hid[:, :], hid[:, :], xt[:, q, :], ALU.add))
                dve.wait_ge(s["mixps"], n + 1)
                if later(n):
                    dve.wait_ge(s["stored"][q], uses * 32)
                dve.tensor_tensor(x1[:, q, :], hid[:, :], ps_mix[q][:, 0:DIM], ALU.add).then_inc(s["x1"], 1)
                dve.wait_ge(s["x1"], n + 1)
                ch.step(dve.bn_stats(st[:, :], x1[:, q, :]), settled=m)
                ch.step(dve.bn_aggr(mv[:, :], st[:, :]))
                dve.tensor_scalar(ve[:, :], mv[:, 1:2], LN_EPS, None, ALU.add).then_inc(s["var"], 1)
                dve.wait_ge(s["rstd"], n * 2 + 2)
                dve.tensor_scalar(norm[q][:, :], x1[:, q, :], mv[:, 0:1], rs[:, 0:1], ALU.subtract, ALU.mult).then_inc(s["norm"], 1)
                dve.wait_ge(s["logits"], n + 1)
                ch.step(dve.tensor_reduce(mx[:, :], ps_log, AX.X, ALU.max))
                dve.tensor_scalar(lg[:, :], ps_log, mx[:, 0:1], None, ALU.subtract).then_inc(s["gex"], 1)
                dve.wait_ge(s["gexed"], n + 1)
                ch.step(dve.reciprocal(rtot[:, :], tot[:, :]))
                ch.step(dve.tensor_scalar(prob[:, :], ex[:, :], rtot[:, 0:1], None, ALU.mult))
                ch.step(dve.tensor_reduce(best[:, :], prob[:, :], AX.X, ALU.max))
                ch.step(dve.tensor_scalar(cand[:, :], prob[:, :], best[:, 0:1], 100.0, ALU.is_lt, ALU.mult))
                ch.step(dve.tensor_tensor(cand[:, :], cand[:, :], m.expert_row[:, :], ALU.add))
                ch.step(dve.tensor_reduce(which[:, :], cand[:, :], AX.X, ALU.min))
                dve.tensor_scalar(hot[:, :], m.expert_row[:, :], which[:, 0:1], None, ALU.is_equal).then_inc(s["oh"], 1)
                dve.wait_ge(s["posps"], n + 1)
                ch.step(dve.tensor_tensor(pos[:, :], ps_pos, hot[:, :], ALU.mult))
                ch.step(dve.tensor_tensor(seen[:, :], seen[:, :], hot[:, :], ALU.add))
                ch.step(dve.tensor_reduce(posr[:, :], pos[:, :], AX.X, ALU.add))
                dve.tensor_scalar(kept[:, :], posr[:, :], float(CAP), None, ALU.is_le)
                dve.tensor_scalar(first[:, :], which[:, :], float(CAP), None, ALU.mult)
                ch.step(dve.tensor_scalar(at[:, :], posr[:, :], float(CAP), -1.0, ALU.min, ALU.add))
                ch.step(dve.tensor_tensor(at[:, :], at[:, :], first[:, :], ALU.add))
                ch.step(dve.tensor_copy(m.slot[:, bass.ds(n, 1)], at[:, :]))
                ch.step(dve.tensor_tensor(m.share[:, bass.ds(n, 1)], best[:, :], kept[:, :], ALU.mult))
                ch.step(dve.tensor_scalar(trash[:, :], m.tile_ids[:, bass.ds(n, 1), 0], float(TRASH), None, ALU.add))
                ch.step(dve.tensor_tensor(at[:, :], at[:, :], trash[:, :], ALU.subtract))
                dve.scalar_tensor_tensor(out=place[q][:, :], in0=at[:, :], scalar=kept[:, 0:1], in1=trash[:, :],
                                         op0=ALU.mult, op1=ALU.add).then_inc(s["slot"], 1)
                assert ch.n == CH, ch.n
            over_tiles(dve, tile)

        @block.tensor
        def _(pe):
            pe.wait_ge(s["const"], 96)
            pe.wait_ge(s["neg"], 2)

            def tile(n, q):
                uses = n // 2 if isinstance(n, int) else (n - q) // 2
                pe.wait_ge(s["in"][q], (uses + 1) * 64)
                if later(n):
                    pe.wait_ge(s["x1"], n - 1)
                for half in range(2):
                    pe.matmul(ps_mix[q][:, 0:DIM], xnt[:, q, half * P:half * P + P], m.w_mix[:, half, :], start=(half == 0), stop=False)
                pe.matmul(ps_mix[q][:, 0:DIM], m.ones[0:1, :], m.b_mix[:, :], start=False, stop=True).then_inc(s["mixps"], 1)
                pe.wait_ge(s["norm"], n + 1)
                for half in range(2):
                    last = pe.transpose(ps_t[:, half * P:half * P + P], norm[q][:, half * P:half * P + P], m.ident[:, :])
                last.then_inc(s["normps"], 1)
                pe.wait_ge(s["normt"], n + 1)
                for half in range(2):
                    pe.matmul(ps_log, normt[:, half * P:half * P + P], gate_w[:, half, :], start=(half == 0), stop=False)
                pe.matmul(ps_log, m.ones[0:1, :], gate_b[:, :], start=False, stop=True).then_inc(s["logits"], 1)
                pe.wait_ge(s["oh"], n + 1)
                pe.matmul(ps_pos, m.tri[:, :], hot[:, :], start=True, stop=False)
                pe.matmul(ps_pos, m.ones[:, :], seen[:, :], start=False, stop=True).then_inc(s["posps"], 1)
            over_tiles(pe, tile)


def experts(nc, ctx, m, a):
    sb = lambda name, shape, dt=F32: ctx.enter_context(nc.sbuf_tensor(name, shape, dt))
    s = sem_set(nc, m.sems, "exp", "w* rows* rowst rowsb up hid down y yt yb stored*")
    w1 = sb("f_w1", [P, 2, 2, FF])
    w2 = sb("f_w2", [P, 2, FCH, DIM])
    b1 = sb("f_b1", [P, 2, FCH])
    b2 = sb("f_b2", [P, 2, 2])
    rows = sb("f_rows", [P, 2, 4, DIM])
    rowst = sb("f_rowst", [P, 2, CAP])
    hid = sb("f_hid", [P, FCH, CAP])
    yt = sb("f_yt", [P, 2, CAP])
    y = sb("f_y", [P, 2, 4, DIM])
    WL = 16 * 4

    def over_experts(eng, body):
        body(0, 0, 0)
        body(1, 1, 0)
        with eng.Fori(1, EXPERTS // 2) as it:
            body(it * 2, 0, it)
            body(it * 2 + 1, 1, it)

    with nc.Block() as block:
        @block.sync
        def _(sp):
            def expert(e, q, turn):
                if later(e):
                    sp.wait_ge(s["y"], (e - 1) * 2)
                    settle(sp, m)
                one = bass.ds(e, 1)
                sp.dma_start(w1[:, q, :, :], a.w1[one].rearrange("e (c p) f -> p (e c) f", p=P)).then_inc(s["w"][q], 16)
                sp.dma_start(w2[:, q, :, :], a.w2[one].rearrange("e (c p) d -> p (e c) d", p=P)).then_inc(s["w"][q], 16)
                sp.dma_start(b1[:, q, :], a.b1[one].rearrange("e (c p) -> p (e c)", p=P), allow_slow_non_contiguous=True).then_inc(s["w"][q], 16)
                sp.dma_start(b2[:, q, :], a.b2[one].rearrange("e (c p) -> p (e c)", p=P), allow_slow_non_contiguous=True).then_inc(s["w"][q], 16)
                for j, n in enumerate(CTS):
                    sp.dma_start(rows[0:n, q, j, :], m.d_in[bass.ds(e * CAP + j * CT, n), :]).then_inc(s["rows"][q], 16)
            over_experts(sp, expert)

        @block.tensor
        def _(pe):
            def expert(e, q, turn):
                pe.wait_ge(s["rows"][q], (turn + 1) * 64)
                if later(e) or e >= 1:
                    pe.wait_ge(s["y"], e * 2)
                    pe.wait_ge(s["rowsb"], e * 2)
                for half in range(2):
                    for j, n in enumerate(CTS):
                        last = pe.transpose(m.bank[half][:, j * CT:j * CT + n], rows[0:n, q, j, half * P:half * P + P], m.ident[0:n, 0:n])
                    last.then_inc(s["rowst"], 1)
                pe.wait_ge(s["w"][q], (turn + 1) * WL)
                pe.wait_ge(s["rowsb"], e * 2 + 2)
                for f in range(FCH):
                    if not (isinstance(e, int) and e == 0 and f < 2):
                        pe.wait_ge(s["hid"], e * FCH + f - 1)
                    for half in range(2):
                        last = pe.matmul(m.bank[2 + f % 2][:, 0:CAP], w1[:, q, half, f * P:f * P + P], rowst[:, half, :],
                                         start=(half == 0), stop=(half == 1))
                    last.then_inc(s["up"], 1)
                for out in range(2):
                    for f in range(FCH):
                        pe.wait_ge(s["hid"], e * FCH + f + 1)
                        last = pe.matmul(m.bank[4 + out][:, 0:CAP], w2[:, q, f, out * P:out * P + P], hid[:, f, :],
                                         start=(f == 0), stop=(f == FCH - 1))
                    last.then_inc(s["down"], 1)
                pe.wait_ge(s["y"], e * 2 + 2)
                for j, n in enumerate(CTS):
                    if j % 2 == 0 and not (isinstance(e, int) and e == 0):
                        pe.wait_ge(s["yb"], e * 4)
                    for out in range(2):
                        last = pe.transpose(m.bank[6 + j // 2][0:n, (j % 2) * DIM + out * P:(j % 2) * DIM + out * P + P],
                                            yt[:, out, j * CT:j * CT + n], m.ident[:, :])
                    last.then_inc(s["yt"], 1)
            over_experts(pe, expert)

        @block.scalar
        def _(act):
            def expert(e, q, turn):
                for half in range(2):
                    act.wait_ge(s["rowst"], e * 2 + 1 + half)
                    act.copy(rowst[:, half, :], m.bank[half][:, 0:CAP]).then_inc(s["rowsb"], 1)
                act.wait_ge(s["w"][q], (turn + 1) * WL)
                for f in range(FCH):
                    act.wait_ge(s["up"], e * FCH + f + 1)
                    act.activation(hid[:, f, :], m.bank[2 + f % 2][:, 0:CAP], ACT.Relu, bias=b1[:, q, f:f + 1]).then_inc(s["hid"], 1)
                for out in range(2):
                    act.wait_ge(s["down"], e * 2 + out + 1)
                    if later(e) or e >= 1:
                        act.wait_ge(s["yt"], e * 4)
                    act.activation(yt[:, out, :], m.bank[4 + out][:, 0:CAP], ACT.Identity, bias=b2[:, q, out:out + 1]).then_inc(s["y"], 1)
            over_experts(act, expert)

        @block.vector
        def _(dve):
            def expert(e, q, turn):
                if later(e):
                    dve.wait_ge(s["stored"][q], turn * 64)
                for j, n in enumerate(CTS):
                    dve.wait_ge(s["yt"], e * 4 + j // 2 * 2 + 2)
                    dve.tensor_copy(y[0:n, q, j, :], m.bank[6 + j // 2][0:n, (j % 2) * DIM:(j % 2) * DIM + DIM]).then_inc(s["yb"], 1)
            over_experts(dve, expert)

        @block.gpsimd
        def _(pool):
            def expert(e, q, turn):
                for j, n in enumerate(CTS):
                    pool.wait_ge(s["yb"], e * 4 + j + 1)
                    settle(pool, m)
                    pool.dma_start(m.d_out[bass.ds(e * CAP + j * CT, n), :], y[0:n, q, j, :]).then_inc(s["stored"][q], 16)
            over_experts(pool, expert)
            for q in range(2):
                pool.wait_ge(s["stored"][q], 64 * (EXPERTS // 2))


def combine(nc, ctx, m, a):
    sb = lambda name, shape, dt=F32: ctx.enter_context(nc.sbuf_tensor(name, shape, dt))
    s = sem_set(nc, m.sems, "cmb", "init slot x1* y* chain out stored*")
    slot = [sb(f"c_slot{q}", [P, 1], I32) for q in range(2)]
    x1 = sb("c_x1", [P, 2, DIM])
    y = [sb(f"c_y{q}", [P, DIM]) for q in range(2)]
    ys = sb("c_ys", [P, DIM])
    bad = sb("c_bad", [P, 3, DIM], I32)
    subst = sb("c_subst", [P, 3, DIM])
    out = sb("c_out", [P, 2, DIM])
    HUGE = 3.4028234663852886e38
    CH = 7

    def all_tiles(eng, body):
        body(0, 0, P)
        body(1, 1, P)
        with eng.Fori(1, TILES // 2 - 1) as it:
            body(it * 2, 0, P)
            body(it * 2 + 1, 1, P)
        body(TILES - 2, 0, P)
        body(TILES - 1, 1, LAST)

    with nc.Block() as block:
        @block.sync
        def _(sp):
            def tile(n, q, rows):
                if later(n):
                    sp.wait_ge(s["out"], n - 1)
                    settle(sp, m)
                sp.dma_start(x1[:, q, :], m.d_x1[bass.ds(n * P, P), :]).then_inc(s["x1"][q], 16)
            all_tiles(sp, tile)

        @block.gpsimd
        def _(pool):
            for i, value in enumerate((0.0, 1e4, -1e4)):
                pool.memset(subst[:, i, :], value).then_inc(s["init"], 1)

            def tile(n, q, rows):
                pool.wait_ge(s["slot"], n + 1)
                if later(n):
                    pool.wait_ge(s["out"], n - 1)
                settle(pool, m)
                pool.indirect_dma_start(y[q][:, :], None, m.d_out, bass.IndirectOffsetOnAxis(ap=slot[q][:, 0:1], axis=0)).then_inc(s["y"][q], 16)
            all_tiles(pool, tile)

        @block.vector
        def _(dve):
            dve.wait_ge(s["init"], 3)

            def look_up(n, q):
                dve.tensor_copy(slot[q][:, :], m.slot[:, bass.ds(n, 1)]).then_inc(s["slot"], 1)

            def tile(n, q, rows):
                uses = n // 2 if isinstance(n, int) else (n - q) // 2
                ch = Chain(dve, s["chain"], n * CH)
                if isinstance(n, int) and n == 0:
                    look_up(0, 0)
                if not (isinstance(n, int) and n == TILES - 1):
                    if not (isinstance(n, int) and n == 0):
                        dve.wait_ge(s["y"][1 - q], (uses + q) * 16)
                    look_up(n + 1, 1 - q)
                dve.wait_ge(s["y"][q], (uses + 1) * 16)
                ch.step(dve.tensor_scalar(ys[:, :], y[q][:, :], m.share[:, bass.ds(n, 1)], None, ALU.mult))
                ch.step(dve.tensor_tensor(bad[:, 0, :], ys[:, :], ys[:, :], ALU.not_equal))
                ch.step(dve.tensor_scalar(bad[:, 1, :], ys[:, :], HUGE, None, ALU.is_gt))
                ch.step(dve.tensor_scalar(bad[:, 2, :], ys[:, :], -HUGE, None, ALU.is_lt), settled=m)
                for i in range(3):
                    ch.step(dve.copy_predicated(ys[:, :], bad[:, i, :], subst[:, i, :]), settled=m if i < 2 else None)
                dve.wait_ge(s["x1"][q], (uses + 1) * 16)
                if later(n):
                    dve.wait_ge(s["stored"][q], uses * 16)
                dve.tensor_tensor(out[:, q, :], ys[:, :], x1[:, q, :], ALU.add).then_inc(s["out"], 1)
                dve.wait_ge(s["out"], n + 1)
                assert ch.n == CH
            all_tiles(dve, tile)

        @block.scalar
        def _(act):
            def tile(n, q, rows):
                act.wait_ge(s["out"], n + 1)
                act.dma_start(a.out[bass.ds(n * P, rows), :], out[0:rows, q, :]).then_inc(s["stored"][q], 16)
            all_tiles(act, tile)
            for q in range(2):
                act.wait_ge(s["stored"][q], 16 * (TILES // 2))


_INS = ["x", "src", "dst", "L0_gnn_W_l", "L0_gnn_W_r", "L0_gnn_att", "L0_gnn_bias", "L0_gnn_gamma", "L0_gnn_beta",
        "L0_mix_W_qk", "L0_mix_b_qk", "L0_mix_W_v", "L0_mix_b_v", "L0_mix_gamma", "L0_mix_beta", "L0_ffn_gate_w",
        "L0_ffn_gate_b", "L0_ffn_w1", "L0_ffn_b1", "L0_ffn_w2", "L0_ffn_b2"]


def graph_block(nc, x, src, dst, W_l, W_r, att, bias, gamma, beta, W_qk, b_qk, W_v, b_v, mix_gamma, mix_beta,
                gate_w, gate_b, w1, b1, w2, b2, out):
    a = Arrays()
    a.x, a.src, a.dst, a.out = x, src, dst, out
    a.W_l, a.W_r, a.att, a.bias, a.gamma, a.beta = W_l, W_r, att, bias, gamma, beta
    a.W_qk, a.b_qk, a.W_v, a.b_v, a.mix_gamma, a.mix_beta = W_qk, b_qk, W_v, b_v, mix_gamma, mix_beta
    a.gate_w, a.gate_b, a.w1, a.b1, a.w2, a.b2 = gate_w, gate_b, w1, b1, w2, b2
    with ExitStack() as whole:
        m = memory(nc, whole)
        m.sems = whole
        for stage in (prepare, project, lambdas, attend, node_update, experts, combine):
            with ExitStack() as buffers:
                stage(nc, buffers, m, a)


def kernel(**inputs):
    import numpy as _np
    import concourse.bacc as _bacc
    from concourse import mybir as _mybir
    from concourse.bass_utils import run_bass_kernel_spmd as _run

    nc = _bacc.Bacc("TRN2", target_bir_lowering=False, num_devices=1)
    arrays, args = {}, []
    for name in _INS:
        a = _np.ascontiguousarray(inputs[name])
        arrays[f"in_{name}_dram"] = a
        args.append(nc.dram_tensor(f"in_{name}_dram", a.shape, _mybir.dt.from_np(a.dtype), kind="ExternalInput").ap())
    args.append(nc.dram_tensor("out_0_dram", (NODES, DIM), F32, kind="ExternalOutput").ap())
    graph_block(nc, *args)
    r = _run(nc, [arrays], core_ids=[0])
    return r.results[0]["out_0_dram"]
```

```python
from contextlib import ExitStack

import concourse.bass as bass
from concourse import mybir

F32 = mybir.dt.float32
BF16 = mybir.dt.bfloat16
I32 = mybir.dt.int32
I16 = mybir.dt.int16
U32 = mybir.dt.uint32
ALU = mybir.AluOpType
ACT = mybir.ActivationFunctionType
AX = mybir.AxisListType

P = 128
NODES, DIM = 2500, 256
HEADS, HEAD = 4, 64
EDGES = 80000
TILES = -(-NODES // P)
PAD = TILES * P
LAST = NODES - (TILES - 1) * P
G = 4
EDGES_STEP = G * P
BLOCKS = -(-EDGES // EDGES_STEP)
EDGES_PAD = BLOCKS * EDGES_STEP
STEPS = BLOCKS + TILES - 1
ECOLS = EDGES // P
ROW = DIM + HEADS
ROW3 = 3 * ROW + 4
HCOLS = HEAD + 1
RING = 4
BIG = 1e30
EXPERTS, FF = 8, 1024
CAP = -(-5 * NODES // (4 * EXPERTS))
FCH = FF // P
CT = -(-CAP // 4)
CTS = [CT, CT, CT, CAP - 3 * CT]
TRASH = EXPERTS * CAP
LN_EPS = 1e-5


def settle(eng, m):
    eng.sem_inc(m.met, 1)


class Chain:

    def __init__(self, eng, sem, base):
        self.eng, self.sem, self.base, self.n = eng, sem, base, 0

    def step(self, ins, settled=None):
        self.n += 1
        ins.then_inc(self.sem, 1)
        self.eng.wait_ge(self.sem, self.base + self.n)
        if settled:
            settle(self.eng, settled)


def over_tiles(eng, body, count=TILES):
    body(0, 0)
    body(1, 1)
    with eng.Fori(1, count // 2) as it:
        body(it * 2, 0)
        body(it * 2 + 1, 1)


def skewed(eng, turn):
    turn(0, 0, None, None)
    for n in range(1, 4):
        turn(n, n % 2, n - 1, (n - 1) % 2)
    with eng.Fori(2, TILES // 2) as it:
        turn(it * 2, 0, it * 2 - 1, 1)
        turn(it * 2 + 1, 1, it * 2, 0)
    turn(None, None, TILES - 1, (TILES - 1) % 2)


def uses(n, q):
    return n // 2 if isinstance(n, int) else (n - q) // 2


def later(n):
    return not isinstance(n, int) or n >= 2



def sem_set(nc, ctx, prefix, names):
    sems = {}
    for name in names.split():
        if name[-1] == "*":
            sems[name[:-1]] = [ctx.enter_context(nc.semaphore(f"{prefix}_{name[:-1]}{i}")) for i in range(2)]
        else:
            sems[name] = ctx.enter_context(nc.semaphore(f"{prefix}_{name}"))
    return sems


class Memory:
    pass


class Arrays:
    pass


def memory(nc, ctx):
    m = Memory()

    def sb(name, shape, dt=F32):
        return ctx.enter_context(nc.sbuf_tensor(name, shape, dt))

    def dram(name, shape, dt=F32):
        return nc.dram_tensor(name, shape, dt, kind="Internal").ap()

    m.ident = sb("ident", [P, P])
    m.ones = sb("ones", [P, P])
    m.tri = sb("tri", [P, P])
    m.lane_row = sb("lane_row", [P, P], BF16)
    m.tile_ids = sb("tile_ids", [P, TILES, 2])
    m.expert_row = sb("expert_row", [P, EXPERTS])
    m.window = sb("window", [1, STEPS], I32)
    m.start = sb("start", [1, STEPS], I32)
    m.x = sb("x_rows", [P, TILES, DIM])
    m.xn = sb("xn_rows", [P, TILES, DIM + 1])
    m.xnt = sb("xnt_rows", [P, TILES, DIM])
    m.w_lr = sb("w_lr", [P, 2, 2, ROW])
    m.w_q = sb("w_q", [P, 2, DIM])
    m.w_k = sb("w_k", [P, 2, DIM])
    m.w_v = sb("w_v", [P, 2, DIM])
    m.att_row = sb("att_row", [P, DIM])
    m.att_col = sb("att_col", [P, 2, HEADS])
    m.key_max = sb("key_max", [P, 2, TILES])
    m.w_mix = sb("w_mix", [P, 2, DIM])
    m.b_mix = sb("b_mix", [1, DIM])
    m.slot = sb("slot", [P, TILES], I32)
    m.share = sb("share", [P, TILES])
    m.bank = [ctx.enter_context(nc.psum_tensor(f"bank{i}", [P, 512], F32)) for i in range(8)]

    m.met = ctx.enter_context(nc.semaphore("met"))
    m.d_xl = dram("d_xl", (PAD, ROW))
    m.d_xr = dram("d_xr", (PAD, ROW3), BF16)
    m.d_src = dram("d_src", (EDGES_PAD,), I32)
    m.d_dst = dram("d_dst", (EDGES_PAD,))
    m.d_dst16 = dram("d_dst16", (EDGES_PAD,), I16)
    m.d_pen = dram("d_pen", (EDGES_PAD + P,))
    m.d_acc = dram("d_acc", (PAD, HEADS * HCOLS))
    m.d_in = dram("d_in", (TRASH + PAD, DIM))
    m.d_out = dram("d_out", (TRASH, DIM))
    return m


def prepare(nc, ctx, m, a):
    sb = lambda name, shape, dt=F32: ctx.enter_context(nc.sbuf_tensor(name, shape, dt))
    s = sem_set(nc, m.sems, "pre", "weights att ids dst zero ident tri ones pool chain scaled edges cnt cntps cntsb step stepps xrows fill stored")
    dst = sb("p_dst", [P, ECOLS], I32)
    prev = sb("p_prev", [P, ECOLS], I32)
    dstf = sb("p_dstf", [P, ECOLS])
    prevf = sb("p_prevf", [P, ECOLS])
    junk = sb("p_junk", [P, ECOLS])
    dst16 = sb("p_dst16", [P, ECOLS], I16)
    pen = sb("p_pen", [P, ECOLS])
    padf = sb("p_padf", [P, 8])
    padpen = sb("p_padpen", [P, 8])
    pad16 = sb("p_pad16", [P, 8], I16)
    padi = sb("p_padi", [P, 8], I32)
    zero = sb("p_zero", [P, 2048])
    lane = sb("p_lane", [P, P], I32)
    ids = sb("p_ids", [P, TILES, 2], I32)
    eids = sb("p_eids", [P, EXPERTS], I32)
    limit = sb("p_limit", [TILES - 1, STEPS], I32)
    limitf = sb("p_limitf", [TILES - 1, STEPS])
    below = sb("p_below", [P, TILES - 1])
    cnt = sb("p_cnt", [TILES - 1, 1])
    passed = sb("p_passed", [TILES - 1, STEPS])
    att_raw = sb("p_att_raw", [P, DIM])
    wa = sb("p_wa", [P, DIM])
    tail = EDGES_PAD - EDGES
    TAILS = 48
    assert tail == TAILS * 8

    with nc.Block() as block:
        @block.sync
        def _(sp):
            sp.wait_ge(s["ones"], 9)
            flat = a.dst
            sp.dma_start(dst[:, :], flat.rearrange("(p c) -> p c", p=P)).then_inc(s["dst"], 16)
            sp.dma_start(prev[0:1, 1:ECOLS], flat[0:ECOLS - 1].unsqueeze(0)).then_inc(s["dst"], 16)
            sp.dma_start(prev[1:P, :], flat[ECOLS - 1:EDGES - 1].rearrange("(p c) -> p c", c=ECOLS)).then_inc(s["dst"], 16)
            sp.dma_start(m.d_src[0:EDGES].rearrange("(r c) -> r c", r=16), a.src.rearrange("(r c) -> r c", r=16)).then_inc(s["fill"], 16)
            full = TILES - 1
            sp.dma_start(m.x[:, 0:full, :], a.x[0:full * P, :].rearrange("(t p) c -> p t c", p=P)).then_inc(s["fill"], 16)
            sp.dma_start(m.x[0:LAST, full, :], a.x[full * P:NODES, :]).then_inc(s["fill"], 16)
            for half in range(2):
                rows = slice(half * P, half * P + P)
                sp.dma_start(m.w_lr[:, half, 0, 0:DIM], a.W_l[rows, :]).then_inc(s["weights"], 16)
                sp.dma_start(m.w_lr[:, half, 1, 0:DIM], a.W_r[rows, :]).then_inc(s["weights"], 16)
                sp.dma_start(m.w_q[:, half, :], a.W_qk[0, rows, :]).then_inc(s["weights"], 16)
                sp.dma_start(m.w_k[:, half, :], a.W_qk[1, rows, :]).then_inc(s["weights"], 16)
                sp.dma_start(m.w_v[:, half, :], a.W_v[rows, :]).then_inc(s["weights"], 16)
            sp.dma_start(att_raw[:, :], a.att.rearrange("h c -> (h c)").partition_broadcast(P)).then_inc(s["att"], 16)
            for h in range(HEADS):
                lo = (h % 2) * HEAD
                sp.dma_start(m.att_col[lo:lo + HEAD, h // 2, h:h + 1], a.att[h, :].unsqueeze(1)).then_inc(s["att"], 16)
            sp.wait_ge(s["edges"], 3)
            for out, inn, pad in ((m.d_dst, dstf, padf[0:TAILS, :]), (m.d_dst16, dst16, pad16[0:TAILS, :]), (m.d_pen, pen, None)):
                sp.dma_start(out[0:EDGES].rearrange("(p c) -> p c", p=P), inn[:, :]).then_inc(s["stored"], 16)
                if pad is not None:
                    sp.dma_start(out[EDGES:EDGES_PAD].rearrange("(p c) -> p c", c=8), pad).then_inc(s["stored"], 16)
            sp.dma_start(m.d_pen[EDGES:EDGES_PAD + P].rearrange("(p c) -> p c", c=8), padpen[0:(tail + P) // 8, :]).then_inc(s["stored"], 16)
            sp.dma_start(m.d_src[EDGES:EDGES_PAD].rearrange("(p c) -> p c", c=8), padi[0:TAILS, :]).then_inc(s["stored"], 16)
            total = TRASH * DIM
            for lo in range(0, total, P * 2048):
                n = min(P * 2048, total - lo) // 2048
                sp.dma_start(m.d_in.rearrange("r c -> (r c)")[lo:lo + n * 2048].rearrange("(p c) -> p c", c=2048),
                             zero[0:n, :]).then_inc(s["stored"], 16)
            sp.wait_ge(s["weights"], 160)
            sp.wait_ge(s["fill"], 48)
            sp.wait_ge(s["stored"], 16 * (7 + -(-total // (P * 2048))))

        @block.gpsimd
        def _(pool):
            pool.memset(prev[:, :], -1).then_inc(s["ones"], 1)
            pool.memset(m.att_col[:, :, :], 0.0).then_inc(s["ones"], 1)
            pool.memset(zero[:, :], 0.0).then_inc(s["ones"], 1)
            pool.memset(m.ones[:, :], 1.0).then_inc(s["ones"], 1)
            pool.memset(m.ident[:, :], 0.0).then_inc(s["ones"], 1)
            pool.memset(padf[:, :], 4095.0).then_inc(s["ones"], 1)
            pool.memset(m.x[:, TILES - 1, :], 0.0).then_inc(s["ones"], 1)
            pool.memset(padi[:, :], 0).then_inc(s["ones"], 1)
            pool.memset(padpen[:, :], -BIG).then_inc(s["ones"], 1)
            pool.iota(lane[:, :], [[1, P]], base=0, channel_multiplier=0).then_inc(s["ids"], 1)
            pool.iota(ids[:, :, 0], [[P, TILES]], base=0, channel_multiplier=1).then_inc(s["ids"], 1)
            pool.iota(ids[:, :, 1], [[P, TILES]], base=0, channel_multiplier=0).then_inc(s["ids"], 1)
            pool.iota(eids[:, :], [[1, EXPERTS]], base=0, channel_multiplier=0).then_inc(s["ids"], 1)
            pool.iota(limit[:, :], [[EDGES_STEP, STEPS]], base=0, channel_multiplier=-EDGES_STEP).then_inc(s["ids"], 1)
            pool.wait_ge(s["ones"], 9)
            pool.affine_select(out=m.ident[:, :], in_=m.ident[:, :], compare_op=ALU.not_equal, fill=1.0, base=0,
                               pattern=[[-1, P]], channel_multiplier=1).then_inc(s["ident"], 1)
            pool.affine_select(out=m.tri[:, :], in_=m.ones[:, :], compare_op=ALU.is_ge, fill=0.0, base=0,
                               pattern=[[1, P]], channel_multiplier=-1).then_inc(s["ident"], 1)

        @block.vector
        def _(dve):
            ch = Chain(dve, s["chain"], 0)
            dve.wait_ge(s["dst"], 48)
            ch.step(dve.tensor_copy(dstf[:, :], dst[:, :]))
            ch.step(dve.tensor_copy(prevf[:, :], prev[:, :]))
            ch.step(dve.tensor_tensor(pen[:, :], dstf[:, :], prevf[:, :], ALU.not_equal))
            dve.tensor_copy(dst16[:, :], dstf[:, :]).then_inc(s["edges"], 1)
            dve.tensor_scalar(pen[:, :], pen[:, :], -BIG, None, ALU.mult).then_inc(s["edges"], 1)
            dve.wait_ge(s["ones"], 9)
            dve.tensor_copy(pad16[:, :], padf[:, :]).then_inc(s["edges"], 1)
            for t in range(1, TILES):
                ch.step(dve.tensor_scalar(junk[:, :], dstf[:, :], float(P * t), 0.0, ALU.is_lt, ALU.add,
                                          accum_out=below[:, t - 1:t]))
            dve.wait_ge(s["ids"], 5)
            dve.tensor_copy(m.lane_row[:, :], lane[:, :]).then_inc(s["scaled"], 1)
            dve.tensor_copy(m.tile_ids[:, :, :], ids[:, :, :]).then_inc(s["scaled"], 1)
            dve.wait_ge(s["scaled"], 2)
            dve.tensor_scalar(m.xn[:, :, DIM], m.tile_ids[:, :, 0], float(NODES), None, ALU.is_lt).then_inc(s["scaled"], 1)
            dve.tensor_copy(m.expert_row[:, :], eids[:, :]).then_inc(s["scaled"], 1)
            dve.wait_ge(s["att"], 80)
            dve.tensor_scalar(m.att_row[:, :], att_raw[:, :], 0.2, None, ALU.mult).then_inc(s["scaled"], 1)
            dve.tensor_scalar(m.att_col[:, :, :], m.att_col[:, :, :], 0.8, None, ALU.mult).then_inc(s["scaled"], 1)
            ch.step(dve.tensor_copy(limitf[:, :], limit[:, :]))
            dve.wait_ge(s["cntps"], 1)
            ch.step(dve.tensor_copy(cnt[:, :], m.bank[0][0:TILES - 1, 0:1]))
            dve.tensor_scalar(passed[:, :], limitf[:, :], cnt[:, 0:1], None, ALU.is_gt).then_inc(s["step"], 1)
            dve.wait_ge(s["stepps"], 1)
            dve.tensor_copy(m.window[:, :], m.bank[1][0:1, 0:STEPS]).then_inc(s["step"], 1)
            dve.scalar_tensor_tensor(out=m.start[:, :], in0=m.bank[1][0:1, 0:STEPS], scalar=-float(EDGES_STEP),
                                     in1=limitf[0:1, :], op0=ALU.mult, op1=ALU.add).then_inc(s["step"], 1)
            dve.wait_ge(s["weights"], 160)
            dve.wait_ge(s["scaled"], 6)
            for half in range(2):
                for side in range(2):
                    ch.step(dve.tensor_tensor(wa[:, :], m.w_lr[:, half, side, 0:DIM], m.att_row[:, :], ALU.mult))
                    ch.step(dve.tensor_reduce(m.w_lr[:, half, side, DIM:ROW], wa[:, :].rearrange("p (h c) -> p h c", h=HEADS),
                                              AX.X, ALU.add))

        @block.tensor
        def _(pe):
            pe.wait_ge(s["ones"], 9)
            pe.wait_ge(s["chain"], 3 + TILES - 1)
            pe.matmul(m.bank[0][0:TILES - 1, 0:1], below[:, :], m.ones[:, 0:1], start=True, stop=True).then_inc(s["cntps"], 1)
            pe.wait_ge(s["step"], 1)
            pe.matmul(m.bank[1][0:1, 0:STEPS], m.ones[0:TILES - 1, 0:1], passed[:, :], start=True, stop=True).then_inc(s["stepps"], 1)


def rstd_pool(pool, out, var, halves):
    return pool.tensor_tensor(out, var, halves, ALU.pow)


def project(nc, ctx, m, a):
    sb = lambda name, shape, dt=F32: ctx.enter_context(nc.sbuf_tensor(name, shape, dt))
    s = sem_set(nc, m.sems, "prj", "var rstd xn xn_kept norm_chain split_chain xtps xt kept right left keysps hi xl rest xr max stored_l* stored_r* neg")
    st = sb("a_st", [P, 6])
    mv = sb("a_mv", [P, 2])
    ve = sb("a_ve", [P, 1])
    rs = sb("a_rs", [P, 1])
    neghalf = sb("a_neghalf", [P, 1])
    xn = sb("a_xn", [P, 2, DIM])
    xnt = sb("a_xnt", [P, 2, DIM])
    xl = sb("a_xl", [P, 2, ROW])
    rest = sb("a_rest", [P, ROW])
    xr3 = sb("a_xr3", [P, 2, ROW3], BF16)
    ps_x = [m.bank[0], m.bank[1]]
    ps_l = [m.bank[2], m.bank[3]]
    ps_r = [m.bank[4], m.bank[5]]
    ps_k = [m.bank[6], m.bank[7]]

    with nc.Block() as block:
        @block.sync
        def _(sp):
            def tile(n, q):
                sp.wait_ge(s["xr"], n + 1)
                settle(sp, m)
                sp.dma_start(m.d_xr[bass.ds(n * P, P), :], xr3[:, q, :]).then_inc(s["stored_r"][q], 16)
            over_tiles(sp, tile)
            for q in range(2):
                sp.wait_ge(s["stored_r"][q], 16 * (TILES // 2))
                sp.wait_ge(s["stored_l"][q], 16 * (TILES // 2))

        @block.gpsimd
        def _(pool):
            pool.memset(neghalf[:, :], -0.5).then_inc(s["neg"], 1)
            pool.wait_ge(s["neg"], 1)

            def turn(lead, ql, lag, qg):
                if lead is not None:
                    pool.wait_ge(s["var"], lead + 1)
                    rstd_pool(pool, rs[:, :], ve[:, :], neghalf[:, :]).then_inc(s["rstd"], 1)
                if lag is not None:
                    pool.wait_ge(s["xn"], lag + 1)
                    pool.tensor_copy(m.xn[:, bass.ds(lag, 1), 0:DIM].rearrange("p t c -> p (t c)"), xn[:, qg, :]).then_inc(s["xn_kept"], 1)
                    pool.wait_ge(s["xt"], lag + 1)
                    pool.tensor_copy(m.xnt[:, bass.ds(lag, 1), :].rearrange("p t c -> p (t c)"), xnt[:, qg, :]).then_inc(s["kept"], 1)
            skewed(pool, turn)

        @block.vector
        def _(dve):
            dve.wait_ge(s["neg"], 1)

            def turn(lead, ql, lag, qg):
                if lead is not None:
                    ch = Chain(dve, s["norm_chain"], lead * 2)
                    row = m.x[:, bass.ds(lead, 1), :].rearrange("p t c -> p (t c)")
                    ch.step(dve.bn_stats(st[:, :], row), settled=m)
                    ch.step(dve.bn_aggr(mv[:, :], st[:, :]))
                    dve.tensor_scalar(ve[:, :], mv[:, 1:2], LN_EPS, None, ALU.add).then_inc(s["var"], 1)
                    dve.wait_ge(s["rstd"], lead + 1)
                    if later(lead):
                        dve.wait_ge(s["xn_kept"], lead - 1)
                        dve.wait_ge(s["xtps"], lead - 1)
                    dve.tensor_scalar(xn[:, ql, :], row, mv[:, 0:1], rs[:, 0:1],
                                      ALU.subtract, ALU.mult).then_inc(s["xn"], 1)
                if lag is not None:
                    ch = Chain(dve, s["split_chain"], lag * 2)
                    dve.wait_ge(s["hi"], lag + 1)
                    if later(lag):
                        dve.wait_ge(s["stored_r"][qg], uses(lag, qg) * 16)
                    dve.tensor_tensor(rest[:, :], ps_r[qg][:, 0:ROW], xr3[:, qg, 0:ROW], ALU.subtract).then_inc(s["rest"], 1)
                    dve.wait_ge(s["rest"], lag + 1)
                    ch.step(dve.tensor_copy(xr3[:, qg, ROW:2 * ROW], rest[:, :]))
                    ch.step(dve.tensor_copy(xr3[:, qg, 3 * ROW:ROW3].bitcast(F32), m.tile_ids[:, bass.ds(lag, 1), :].rearrange("p t i -> p (t i)")))
                    dve.tensor_tensor(xr3[:, qg, 2 * ROW:3 * ROW], rest[:, :], xr3[:, qg, ROW:2 * ROW],
                                      ALU.subtract).then_inc(s["xr"], 1)
                    dve.wait_ge(s["xr"], lag + 1)
                    dve.wait_ge(s["keysps"], lag + 1)
                    valid = LAST if isinstance(lag, int) and lag == TILES - 1 else P
                    dve.tensor_reduce(m.key_max[:, :, bass.ds(lag, 1)].rearrange("p o t -> p (o t)"),
                                      ps_k[qg][:, 0:DIM].rearrange("p (o n) -> p o n", o=2)[:, :, 0:valid], AX.X, ALU.max).then_inc(s["max"], 1)
            skewed(dve, turn)

        @block.tensor
        def _(pe):
            def turn(lead, ql, lag, qg):
                if lead is not None:
                    pe.wait_ge(s["xn"], lead + 1)
                    if later(lead):
                        pe.wait_ge(s["xt"], lead - 1)
                    for half in range(2):
                        last = pe.transpose(ps_x[ql][:, half * P:half * P + P], xn[:, ql, half * P:half * P + P], m.ident[:, :])
                    last.then_inc(s["xtps"], 1)
                if lag is not None:
                    pe.wait_ge(s["xt"], lag + 1)
                    if later(lag):
                        pe.wait_ge(s["rest"], lag - 1)
                        pe.wait_ge(s["xl"], lag - 1)
                        pe.wait_ge(s["max"], lag - 1)
                    for side, bank, done in ((1, ps_r, "right"), (0, ps_l, "left")):
                        for half in range(2):
                            last = pe.matmul(bank[qg][:, 0:ROW], xnt[:, qg, half * P:half * P + P], m.w_lr[:, half, side, :],
                                             start=(half == 0), stop=(half == 1))
                        last.then_inc(s[done], 1)
                    for out in range(2):
                        for half in range(2):
                            last = pe.matmul(ps_k[qg][:, out * P:out * P + P], m.w_k[:, half, out * P:out * P + P],
                                             xnt[:, qg, half * P:half * P + P], start=(half == 0), stop=(half == 1))
                    last.then_inc(s["keysps"], 1)
            skewed(pe, turn)

        @block.scalar
        def _(act):
            def turn(lead, ql, lag, qg):
                if lead is not None:
                    act.wait_ge(s["xtps"], lead + 1)
                    if later(lead):
                        act.wait_ge(s["keysps"], lead - 1)
                        act.wait_ge(s["kept"], lead - 1)
                    act.copy(xnt[:, ql, :], ps_x[ql][:, 0:DIM]).then_inc(s["xt"], 1)
                if lag is not None:
                    act.wait_ge(s["right"], lag + 1)
                    if later(lag):
                        act.wait_ge(s["stored_r"][qg], uses(lag, qg) * 16)
                        act.wait_ge(s["stored_l"][qg], uses(lag, qg) * 16)
                    act.copy(xr3[:, qg, 0:ROW], ps_r[qg][:, 0:ROW]).then_inc(s["hi"], 1)
                    act.wait_ge(s["left"], lag + 1)
                    act.copy(xl[:, qg, :], ps_l[qg][:, 0:ROW]).then_inc(s["xl"], 1)
                    act.wait_ge(s["xl"], lag + 1)
                    settle(act, m)
                    act.dma_start(m.d_xl[bass.ds(lag * P, P), :], xl[:, qg, :]).then_inc(s["stored_l"][qg], 16)
            skewed(act, turn)


def lambdas(nc, ctx, m, a):
    sb = lambda name, shape, dt=F32: ctx.enter_context(nc.sbuf_tensor(name, shape, dt))
    s = sem_set(nc, m.sems, "lam", "const top shiftps shift xt keysps e ctxps ctx turnedps turned chain lam var rstd wqps wq bn mixps mix")
    mx = sb("l_mx", [P, 2])
    shift = sb("l_shift", [1, DIM])
    bk_row = sb("l_bk_row", [1, DIM])
    xnt = sb("l_xnt", [P, 2, DIM])
    e = sb("l_e", [P, 2, DIM])
    ctxt = sb("l_ctxt", [P, 2, DIM + 1])
    acc = sb("l_acc", [P, 2, DIM])
    rz = sb("l_rz", [P, 2])
    lam = sb("l_lam", [P, 2, DIM])
    bn = sb("l_bn", [P, 2, DIM])
    bv = sb("l_bv", [P, DIM])
    cols = sb("l_cols", [P, 2, 4])
    st = sb("l_st", [P, 2, 6])
    mv = sb("l_mv", [P, 2, 2])
    ve = sb("l_ve", [P, 2])
    rs = sb("l_rs", [P, 2])
    sc = sb("l_sc", [P, 2])
    neghalf = sb("l_neghalf", [P, 2])
    wqt = sb("l_wqt", [P, 2, DIM])

    with nc.Block() as block:
        @block.sync
        def _(sp):
            for half in range(2):
                for i, vec in ((3, a.b_qk[1, :]), (0, a.mix_gamma), (1, a.mix_beta), (2, a.b_qk[0, :])):
                    sp.dma_start(cols[:, half, i:i + 1], vec[half * P:half * P + P].unsqueeze(1)).then_inc(s["const"], 16)
            sp.dma_start(bk_row[:, :], a.b_qk[1, :].unsqueeze(0)).then_inc(s["const"], 16)
            sp.dma_start(bv[:, :], a.b_v.partition_broadcast(P)).then_inc(s["const"], 16)
            sp.wait_ge(s["const"], 16 * 10)

        @block.scalar
        def _(act):
            def tile(n, q):
                act.wait_ge(s["keysps"], n + 1)
                if later(n):
                    act.wait_ge(s["ctxps"], n - 1)
                act.activation(e[:, q, :], m.bank[q][:, 0:DIM], ACT.Exp).then_inc(s["e"], 1)
            over_tiles(act, tile)

        @block.gpsimd
        def _(pool):
            def tile(n, q):
                if later(n):
                    pool.wait_ge(s["keysps"], n - 1)
                pool.tensor_copy(xnt[:, q, :], m.xnt[:, bass.ds(n, 1), :].rearrange("p t c -> p (t c)")).then_inc(s["xt"], 1)
            over_tiles(pool, tile)
            pool.memset(neghalf[:, :], -0.5).then_inc(s["rstd"], 1)
            pool.wait_ge(s["rstd"], 1)
            pool.wait_ge(s["var"], 1)
            rstd_pool(pool, rs[:, :], ve[:, :], neghalf[:, :]).then_inc(s["rstd"], 1)

        @block.vector
        def _(dve):
            ch = Chain(dve, s["chain"], 0)
            ch.step(dve.tensor_reduce(mx[:, :], m.key_max[:, :, :], AX.X, ALU.max))
            dve.wait_ge(s["const"], 16 * 10)
            dve.tensor_tensor(mx[:, :], mx[:, :], cols[:, :, 3], ALU.add).then_inc(s["top"], 1)
            dve.wait_ge(s["shiftps"], 1)
            dve.tensor_tensor(shift[:, :], bk_row[:, :], m.bank[5][0:1, 0:DIM], ALU.subtract).then_inc(s["shift"], 1)
            dve.wait_ge(s["wqps"], 1)
            dve.tensor_copy(wqt[:, :, :].rearrange("p h d -> p (h d)"), m.bank[6][:, :]).then_inc(s["wq"], 1)
            dve.wait_ge(s["ctxps"], TILES)
            for half in range(2):
                dve.tensor_copy(ctxt[:, half, :], m.bank[2 + half][:, 0:DIM + 1]).then_inc(s["ctx"], 1)
            dve.wait_ge(s["ctx"], 2)
            ch.step(dve.reciprocal(rz[:, :], ctxt[:, :, DIM]))
            dve.wait_ge(s["turnedps"], 1)
            dve.tensor_copy(acc[:, :, :].rearrange("p h d -> p (h d)"), m.bank[7][:, :]).then_inc(s["turned"], 1)
            dve.wait_ge(s["lam"], 1)
            for half in range(2):
                ch.step(dve.scalar_tensor_tensor(out=lam[:, half, :], in0=m.bank[half][:, 0:DIM],
                                                 scalar=rz[:, half:half + 1], in1=bv[:, :], op0=ALU.mult, op1=ALU.add))
                ch.step(dve.bn_stats(st[:, half, :], lam[:, half, :]), settled=m)
                ch.step(dve.bn_aggr(mv[:, half, :], st[:, half, :]))
            dve.tensor_scalar(ve[:, :], mv[:, :, 1], LN_EPS, None, ALU.add).then_inc(s["var"], 1)
            dve.wait_ge(s["rstd"], 2)
            ch.step(dve.tensor_tensor(sc[:, :], rs[:, :], cols[:, :, 0], ALU.mult))
            for half in range(2):
                ch.step(dve.tensor_scalar(lam[:, half, :], lam[:, half, :], mv[:, half, 0:1], sc[:, half:half + 1],
                                          ALU.subtract, ALU.mult))
                dve.tensor_scalar(bn[:, half, :], lam[:, half, :], cols[:, half, 1:2], None, ALU.add).then_inc(s["bn"], 1)
            dve.wait_ge(s["mixps"], 1)
            for half in range(2):
                dve.tensor_copy(m.w_mix[:, half, :], m.bank[2 + half][:, 0:DIM]).then_inc(s["mix"], 1)
            dve.tensor_copy(m.b_mix[:, :], m.bank[4][0:1, 0:DIM]).then_inc(s["mix"], 1)

        @block.tensor
        def _(pe):
            for half in range(2):
                for inn in range(2):
                    last = pe.transpose(m.bank[6][:, half * DIM + inn * P:half * DIM + inn * P + P],
                                        m.w_q[:, inn, half * P:half * P + P], m.ident[:, :])
            last.then_inc(s["wqps"], 1)
            pe.wait_ge(s["top"], 1)
            for half in range(2):
                last = pe.matmul(m.bank[5][0:1, half * P:half * P + P], mx[:, half:half + 1], m.ident[:, :], start=True, stop=True)
            last.then_inc(s["shiftps"], 1)
            pe.wait_ge(s["shift"], 1)

            def turn(lead, ql, lag, qg):
                if lead is not None:
                    pe.wait_ge(s["xt"], lead + 1)
                    if later(lead):
                        pe.wait_ge(s["e"], lead - 1)
                    for half in range(2):
                        pe.matmul(m.bank[ql][:, 0:DIM], xnt[:, ql, half * P:half * P + P], m.w_k[:, half, :], start=(half == 0), stop=False)
                    pe.matmul(m.bank[ql][:, 0:DIM], m.ones[0:1, :], shift[:, :], start=False, stop=True).then_inc(s["keysps"], 1)
                if lag is not None:
                    pe.wait_ge(s["e"], lag + 1)
                    for half in range(2):
                        last = pe.matmul(m.bank[2 + half][:, 0:DIM + 1], e[:, qg, half * P:half * P + P],
                                         m.xn[:, bass.ds(lag, 1), :].rearrange("p t c -> p (t c)"),
                                         start=isinstance(lag, int) and lag == 0, stop=isinstance(lag, int) and lag == TILES - 1)
                    last.then_inc(s["ctxps"], 1)
            skewed(pe, turn)
            pe.wait_ge(s["ctx"], 2)
            for inn in range(2):
                for half in range(2):
                    last = pe.transpose(m.bank[7][:, inn * DIM + half * P:inn * DIM + half * P + P],
                                        ctxt[:, half, inn * P:inn * P + P], m.ident[:, :])
            last.then_inc(s["turnedps"], 1)
            pe.wait_ge(s["turned"], 1)
            for half in range(2):
                for inn in range(2):
                    last = pe.matmul(m.bank[half][:, 0:DIM], acc[:, inn, half * P:half * P + P], m.w_v[:, inn, :],
                                     start=(inn == 0), stop=(inn == 1))
            last.then_inc(s["lam"], 1)
            pe.wait_ge(s["bn"], 2)
            pe.wait_ge(s["wq"], 1)
            for inn in range(2):
                for half in range(2):
                    pe.matmul(m.bank[2 + inn][:, 0:DIM], wqt[:, half, inn * P:inn * P + P], bn[:, half, :],
                              start=(half == 0), stop=(half == 1))
            for half in range(2):
                last = pe.matmul(m.bank[4][0:1, 0:DIM], cols[:, half, 2:3], bn[:, half, :], start=(half == 0), stop=(half == 1))
            last.then_inc(s["mixps"], 1)


def attend(nc, ctx, m, a):
    sb = lambda name, shape, dt=F32: ctx.enter_context(nc.sbuf_tensor(name, shape, dt))
    s = sem_set(nc, m.sems, "att", "init sel drel selt relu score_e lin gate carry scoreps score scoret run scan mps diff rr rd rps p ex agg f fac facs old acc stored*")
    loaded = [m.sems.enter_context(nc.semaphore(f"att_loaded{r}")) for r in range(RING)]
    gathered = [m.sems.enter_context(nc.semaphore(f"att_gathered{r}")) for r in range(RING)]
    idx = [sb(f"e_idx{r}", [P, G], I32) for r in range(RING)]
    dcol = sb("e_dcol", [P, RING, G])
    drow = sb("e_drow", [P, RING, EDGES_STEP], I16)
    pen = sb("e_pen", [HEADS, RING, EDGES_STEP + 1])
    xr3 = sb("e_xr3", [P, RING, ROW3], BF16)
    xl = [sb(f"e_xl{r}", [P, G, ROW]) for r in range(RING)]
    drel = sb("e_drel", [P, G], BF16)
    sel = sb("e_sel", [P, 2, EDGES_STEP], BF16)
    selt = sb("e_selt", [P, RING, G, P])
    first = sb("e_first", [P, RING])
    same = sb("e_same", [P, RING])
    gate = sb("e_gate", [HEADS, 1])
    carry = sb("e_carry", [HEADS, 1])
    relu = sb("e_relu", [P, 2, EDGES_STEP])
    score = sb("e_score", [P, 2, G, HEADS])
    lin = sb("e_lin", [P, G, HEADS])
    run = sb("e_run", [HEADS, EDGES_STEP])
    top = sb("e_top", [HEADS, 2, EDGES_STEP])
    drop = sb("e_drop", [HEADS, 2])
    rr = sb("e_rr", [HEADS, 2])
    rd = sb("e_rd", [HEADS, 2, HEADS])
    diff = sb("e_diff", [P, G, HEADS])
    prod = sb("e_prod", [P, 2, G, HEADS, HCOLS])
    fac = sb("e_fac", [P, HEADS])
    facs = sb("e_facs", [P, HEADS])
    old = sb("e_old", [P, HEADS, HCOLS])
    acc = sb("e_acc", [P, 2, HEADS, HCOLS])

    ps_e = [m.bank[0], m.bank[1]]
    ps_score = m.bank[2][:, 0:G * 5 * HEADS].rearrange("p (g i h) -> p g i h", g=G, i=5)
    ps_scoret = m.bank[3][0:HEADS, :]
    ps_top = m.bank[4][:, 0:G * HEADS]
    ps_ex = m.bank[5][:, 0:G * HEADS]
    ps_r = m.bank[6][:, 0:HEADS]
    ps_agg = m.bank[7][:, 0:HEADS * HCOLS]
    LOADS = 5 * 16
    TURNS = STEPS // RING
    assert STEPS % RING == 0

    def since(k, first_step):
        return not isinstance(k, int) or k >= first_step

    def is_step(k):
        return not isinstance(k, int) or 0 <= k < STEPS

    def over_steps(eng, body, head=1, behind=0):
        for k in range(head * RING):
            body(k, k % RING, k // RING)
        with eng.Fori(head, TURNS - 1) as it:
            for j in range(RING):
                body(it * RING + j, j, it)
        for k in range(STEPS - RING, STEPS + behind):
            body(k, k % RING, k // RING)

    with nc.Block() as block:
        @block.sync
        def _(sp):
            def store(k, q, uses):
                sp.wait_ge(s["acc"], k + 1)
                if since(k, 1):
                    sp.wait_ge(s["stored"][1 - q], 16 * (uses + q))
                    settle(sp, m)
                t = sp.value_load(m.window[0:1, bass.ds(k, 1)], min_val=0, max_val=TILES - 1)
                sp.dma_start(m.d_acc[bass.ds(t * P, P), :], acc[:, q, :, :].rearrange("p h c -> p (h c)")).then_inc(s["stored"][q], 16)

            def load(k, r, turn):
                if since(k, RING):
                    sp.wait_ge(gathered[r], turn * 64)
                    settle(sp, m)
                    sp.wait_ge(s["scoreps"], k - RING + 1)
                    sp.wait_ge(s["scan"], k - RING + 1)
                    settle(sp, m)
                t = sp.value_load(m.window[0:1, bass.ds(k, 1)], min_val=0, max_val=TILES - 1)
                block_at = sp.value_load(m.start[0:1, bass.ds(k, 1)], min_val=0, max_val=EDGES_PAD - EDGES_STEP)
                edges = bass.ds(block_at, EDGES_STEP)
                sp.dma_start(idx[r][:, :], m.d_src[edges].rearrange("(p g) -> p g", g=G)).then_inc(loaded[r], 16)
                sp.dma_start(dcol[:, r, :], m.d_dst[edges].rearrange("(p g) -> p g", g=G)).then_inc(loaded[r], 16)
                sp.dma_start(drow[:, r, :], m.d_dst16[edges].partition_broadcast(P)).then_inc(loaded[r], 16)
                sp.dma_start(pen[:, r, :], m.d_pen[bass.ds(block_at, EDGES_STEP + 1)].partition_broadcast(HEADS)).then_inc(loaded[r], 16)
                sp.dma_start(xr3[:, r, :], m.d_xr[bass.ds(t * P, P), :]).then_inc(loaded[r], 16)

            def step(k, r, turn):
                if is_step(k):
                    load(k, r, turn)
                if since(k, RING):
                    store(k - RING, r % 2, (turn - 1) * (RING // 2) + r // 2)
            over_steps(sp, step, head=2, behind=RING)
            for q in range(2):
                sp.wait_ge(s["stored"][q], 16 * (STEPS // 2))

        @block.gpsimd
        def _(pool):
            pool.memset(acc[:, :, :, :], 0.0).then_inc(s["init"], 1)
            pool.memset(top[:, :, :], -BIG).then_inc(s["init"], 1)

            def gather(k, r, turn):
                pool.wait_ge(loaded[r], (turn + 1) * LOADS)
                if since(k, RING):
                    pool.wait_ge(s["p"], k - RING + 1)
                settle(pool, m)
                for g in range(G):
                    pool.indirect_dma_start(xl[r][:, g, :], None, m.d_xl, bass.IndirectOffsetOnAxis(
                        ap=idx[r][:, g:g + 1], axis=0)).then_inc(gathered[r], 16)
            over_steps(pool, gather)

        @block.vector
        def _(dve):
            dve.wait_ge(s["init"], 2)

            def select(k, r, turn):
                q, before = r % 2, (r - 1) % RING
                dve.wait_ge(loaded[r], (turn + 1) * LOADS)
                number = xr3[:, r, 3 * ROW:3 * ROW + 2].bitcast(F32)
                start = xr3[:, r, 3 * ROW + 2:ROW3].bitcast(F32)
                start_before = xr3[:, before, 3 * ROW + 2:ROW3].bitcast(F32)
                dve.tensor_scalar(sel[:, q, :], drow[:, r, :], number, None, ALU.is_equal).then_inc(s["sel"], 1)
                if since(k, 1):
                    dve.wait_ge(s["selt"], k)
                dve.tensor_scalar(drel[:, :], dcol[:, r, :], start, None, ALU.subtract).then_inc(s["drel"], 1)
                dve.tensor_scalar(first[:, r:r + 1], drow[:, r, 0:1], number, None, ALU.is_equal)
                if since(k, 1):
                    dve.tensor_scalar(same[:, r:r + 1], start, start_before, None, ALU.is_equal)
                else:
                    dve.memset(same[:, r:r + 1], 0.0)
                dve.wait_ge(s["drel"], k + 1)
                dve.tensor_tensor(selt[:, r, :, :], m.lane_row[:, :].unsqueeze(1).to_broadcast([P, G, P]),
                                  drel[:, :].unsqueeze(2).to_broadcast([P, G, P]), ALU.is_equal).then_inc(s["selt"], 1)

            def close_score(k, r, turn):
                q = r % 2
                dve.wait_ge(s["scoreps"], k + 1)
                dve.wait_ge(gathered[r], (turn + 1) * 64)
                if since(k, 1):
                    dve.wait_ge(s["score"], k)
                    dve.wait_ge(s["f"], k)
                dve.tensor_reduce(lin[:, :, :], ps_score.rearrange("p g i h -> p g h i"), AX.X, ALU.add).then_inc(s["lin"], 1)
                dve.tensor_scalar(gate[:, :], same[0:HEADS, r:r + 1], -1.0, BIG, ALU.add, ALU.mult).then_inc(s["gate"], 1)
                dve.wait_ge(s["lin"], k + 1)
                dve.tensor_tensor(score[:, q, :, :], lin[:, :, :], xl[r][:, :, DIM:ROW], ALU.add).then_inc(s["score"], 1)
                dve.wait_ge(s["gate"], k + 1)
                dve.tensor_tensor(carry[:, :], top[:, 1 - q, EDGES_STEP - 1:EDGES_STEP], gate[:, :], ALU.add).then_inc(s["carry"], 1)

            def forward_scan(k, r):
                dve.wait_ge(s["scoret"], k + 1)
                dve.wait_ge(s["carry"], k + 1)
                if since(k, 1):
                    dve.wait_ge(s["scan"], k)
                dve.tensor_tensor_scan(run[:, :], pen[:, r, 0:EDGES_STEP], ps_scoret, carry[:, 0:1], ALU.add, ALU.max).then_inc(s["run"], 1)

            def backward_scan(k, r):
                back = slice(None, None, -1)
                dve.wait_ge(s["run"], k + 1)
                dve.tensor_tensor_scan(top[:, r % 2, back], pen[:, r, 1:EDGES_STEP + 1][:, back], run[:, back], -BIG,
                                       ALU.add, ALU.max).then_inc(s["scan"], 1)

            def open_drop(k, q):
                dve.wait_ge(s["scan"], k + 1)
                dve.tensor_scalar(drop[:, q:q + 1], carry[:, :], top[:, q, 0:1], 0.0, ALU.subtract, ALU.min).then_inc(s["f"], 1)

            def less_top(k, q):
                dve.wait_ge(s["mps"], k + 1)
                dve.tensor_tensor(diff[:, :, :], score[:, q, :, :], ps_top.rearrange("p (g h) -> p g h", g=G),
                                  ALU.subtract).then_inc(s["diff"], 1)

            def weigh(k, r):
                q = r % 2
                dve.wait_ge(s["ex"], k + 1)
                ex = ps_ex.rearrange("p (g h) -> p g h", g=G)
                dve.tensor_copy(prod[:, q, :, :, HEAD:HCOLS], ex.unsqueeze(3))
                dve.tensor_tensor(prod[:, q, :, :, 0:HEAD], xl[r][:, :, 0:DIM].rearrange("p g (h c) -> p g h c", h=HEADS),
                                  ex.unsqueeze(3).to_broadcast([P, G, HEADS, HEAD]), ALU.mult).then_inc(s["p"], 1)

            def factor(k, r):
                dve.wait_ge(s["rps"], k + 1)
                if since(k, 1):
                    dve.wait_ge(s["facs"], k)
                dve.tensor_scalar(fac[:, :], ps_r, -1.0, first[:, r:r + 1], ALU.add, ALU.mult).then_inc(s["fac"], 1)

            def window_factor(k, r):
                dve.wait_ge(s["fac"], k + 1)
                if since(k, 1):
                    dve.wait_ge(s["old"], k)
                dve.tensor_scalar(facs[:, :], fac[:, :], 1.0, same[:, r:r + 1], ALU.add, ALU.mult).then_inc(s["facs"], 1)

            def rescaled(k, q):
                dve.wait_ge(s["facs"], k + 1)
                if since(k, 1):
                    dve.wait_ge(s["acc"], k)
                dve.tensor_tensor(old[:, :, :], acc[:, 1 - q, :, :],
                                  facs[:, :].unsqueeze(2).to_broadcast([P, HEADS, HCOLS]), ALU.mult).then_inc(s["old"], 1)

            def add_sums(k, q, uses):
                dve.wait_ge(s["old"], k + 1)
                dve.wait_ge(s["agg"], k + 1)
                if since(k, 2):
                    dve.wait_ge(s["stored"][q], 16 * uses)
                dve.tensor_tensor(acc[:, q, :, :], old[:, :, :], ps_agg.rearrange("p (h c) -> p h c", h=HEADS),
                                  ALU.add).then_inc(s["acc"], 1)

            def step(k, r, turn):
                before, two_before = (r - 1) % RING, (r - 2) % RING
                maxima = since(k, 1) and is_step(k - 1)
                closing = since(k, 2)
                if maxima:
                    close_score(k - 1, before, turn if r >= 1 else turn - 1)
                if is_step(k + 1):
                    select(k + 1, (r + 1) % RING, turn if r + 1 < RING else turn + 1)
                if maxima:
                    forward_scan(k - 1, before)
                if closing:
                    factor(k - 2, two_before)
                if maxima:
                    backward_scan(k - 1, before)
                if closing:
                    window_factor(k - 2, two_before)
                if maxima:
                    open_drop(k - 1, before % 2)
                if closing:
                    rescaled(k - 2, two_before % 2)
                if maxima:
                    less_top(k - 1, before % 2)
                if closing:
                    add_sums(k - 2, two_before % 2, turn * (RING // 2) + (r - 2) // 2)
                if maxima:
                    weigh(k - 1, before)
            select(0, 0, 0)
            over_steps(dve, step, behind=2)

        @block.tensor
        def _(pe):
            def edge_features(k, r, turn, half):
                q = r % 2
                if half == 0:
                    pe.wait_ge(gathered[r], (turn + 1) * 64)
                if since(k, 1):
                    pe.wait_ge(s["relu"], 2 * k - 1 + half)

                for g in range(G):
                    pe.matmul(ps_e[half][:, g::G], xl[r][:, g, half * P:half * P + P], m.ident[:, :], is_transpose=True,
                              start=(g == 0), stop=False)
                if half == 0:
                    pe.wait_ge(s["sel"], k + 1)
                elif since(k, 1):
                    tops(k - 1, 1 - q)
                for part in range(3):
                    at = part * ROW + half * P
                    last = pe.matmul(ps_e[half][:, :], xr3[:, r, at:at + P], sel[:, q, :], start=False, stop=(part == 2))
                last.then_inc(s["score_e"], 1)

            def tops(k, q):
                pe.wait_ge(s["scan"], k + 1)
                if since(k, 1):
                    pe.wait_ge(s["diff"], k)
                settle(pe, m)
                for g in range(G):
                    last = pe.transpose(ps_top[:, g * HEADS:(g + 1) * HEADS], top[:, q, g::G], m.ident[0:HEADS, 0:HEADS])
                last.then_inc(s["mps"], 1)

            def linear_scores(k, r):
                if since(k, 1):
                    pe.wait_ge(s["score"], k)
                parts = xr3[:, r, 0:3 * ROW].rearrange("p (i c) -> p i c", i=3)[:, :, DIM:ROW]
                for g in range(G):
                    pe.matmul(ps_score[:, g, 0:3, :], sel[:, r % 2, g::G], parts, start=True, stop=True)

            def scores(k, half):
                pe.wait_ge(s["relu"], 2 * k + 1 + half)
                for g in range(G):
                    last = pe.matmul(ps_score[:, g, 3 + half, :], relu[:, half, g::G], m.att_col[:, half, :], start=True, stop=True)
                if half == 1:
                    last.then_inc(s["scoreps"], 1)

            def score_rows(k, q):
                pe.wait_ge(s["score"], k + 1)
                if since(k, 1):
                    pe.wait_ge(s["scan"], k)
                for g in range(G):
                    last = pe.transpose(ps_scoret[:, g::G], score[:, q, g, :], m.ident[:, :])
                last.then_inc(s["scoret"], 1)

            def sums(k, r):
                q = r % 2
                pe.wait_ge(s["rd"], k + 1)
                pe.wait_ge(s["selt"], k + 1)
                if since(k, 1):
                    pe.wait_ge(s["acc"], k)
                pe.matmul(ps_r, m.ones[0:HEADS, :], rd[:, q, :], start=True, stop=True).then_inc(s["rps"], 1)
                pe.wait_ge(s["p"], k + 1)
                for g in range(G):
                    last = pe.matmul(ps_agg, selt[:, r, g, :], prod[:, q, g, :, :].rearrange("p h c -> p (h c)"),
                                     start=(g == 0), stop=(g == G - 1))
                last.then_inc(s["agg"], 1)

            def step(k, r, turn):
                if is_step(k):
                    edge_features(k, r, turn, 0)
                if since(k, 1) and is_step(k - 1):
                    score_rows(k - 1, 1 - r % 2)
                if since(k, 2):
                    sums(k - 2, (r - 2) % RING)
                if is_step(k):
                    edge_features(k, r, turn, 1)
                    linear_scores(k, r)
                    scores(k, 0)
                    scores(k, 1)
                elif is_step(k - 1):
                    tops(k - 1, 1 - r % 2)
            over_steps(pe, step, behind=2)

        @block.scalar
        def _(act):
            def rescale(k, q):
                act.wait_ge(s["f"], k + 1)
                act.activation(rr[:, q:q + 1], drop[:, q:q + 1], ACT.Exp).then_inc(s["rr"], 1)
                act.wait_ge(s["rr"], k + 1)
                if since(k, 2):
                    act.wait_ge(s["rps"], k - 1)
                act.activation(rd[:, q, :], m.ident[0:HEADS, 0:HEADS], ACT.Copy, scale=rr[:, q:q + 1]).then_inc(s["rd"], 1)

            def relus(k, half):
                act.wait_ge(s["score_e"], 2 * k + 1 + half)
                if since(k, 1):
                    act.wait_ge(s["scoreps"], k)
                act.activation(relu[:, half, :], ps_e[half][:, :], ACT.Relu).then_inc(s["relu"], 1)

            def weights(k):
                act.wait_ge(s["diff"], k + 1)
                if since(k, 1):
                    act.wait_ge(s["p"], k)
                act.activation(ps_ex, diff[:, :, :].rearrange("p g h -> p (g h)"), ACT.Exp).then_inc(s["ex"], 1)

            def step(k, r, turn):
                if is_step(k):
                    relus(k, 0)
                if since(k, 1):
                    rescale(k - 1, 1 - r % 2)
                    weights(k - 1)
                if is_step(k):
                    relus(k, 1)
            over_steps(act, step, behind=1)


def node_update(nc, ctx, m, a):
    sb = lambda name, shape, dt=F32: ctx.enter_context(nc.sbuf_tensor(name, shape, dt))
    s = sem_set(nc, m.sems, "upd", "const init in* xt shifted mixps out neg_part low_e var rstd row_chain gate_chain x1 norm normps normt logits gex gexed oh posps slot scattered*")
    bias = sb("u_bias", [P, DIM])
    gamma = sb("u_gamma", [P, DIM])
    beta = sb("u_beta", [P, DIM])
    gate_w = sb("u_gate_w", [P, 2, EXPERTS])
    gate_b = sb("u_gate_b", [1, EXPERTS])
    xnt = sb("u_xnt", [P, 2, DIM])
    xb = sb("u_xb", [P, DIM])
    acc = sb("u_acc", [P, 2, HEADS, HCOLS])
    den = sb("u_den", [P, HEADS])
    out = sb("u_out", [P, DIM])
    low = sb("u_low", [P, DIM])
    lowe = sb("u_lowe", [P, DIM])
    hid = sb("u_hid", [P, DIM])
    st = sb("u_st", [P, 6])
    mv = sb("u_mv", [P, 2])
    ve = sb("u_ve", [P, 1])
    rs = sb("u_rs", [P, 1])
    neghalf = sb("u_neghalf", [P, 1])
    norm = [sb(f"u_norm{q}", [P, DIM]) for q in range(2)]
    normt = sb("u_normt", [P, DIM])
    lg = sb("u_lg", [P, EXPERTS])
    mx = sb("u_mx", [P, 1])
    ex = sb("u_ex", [P, EXPERTS])
    tot = sb("u_tot", [P, 1])
    rtot = sb("u_rtot", [P, 1])
    prob = sb("u_prob", [P, EXPERTS])
    best = sb("u_best", [P, 1])
    cand = sb("u_cand", [P, EXPERTS])
    which = sb("u_which", [P, 1])
    hot = sb("u_hot", [P, EXPERTS])
    seen = sb("u_seen", [P, EXPERTS])
    pos = sb("u_pos", [P, EXPERTS])
    posr = sb("u_posr", [P, 1])
    kept = sb("u_kept", [P, 1])
    first = sb("u_first", [P, 1])
    at = sb("u_at", [P, 1])
    trash = sb("u_trash", [P, TILES])
    place = [sb(f"u_place{q}", [P, 1], I32) for q in range(2)]
    ps_mix = [m.bank[0], m.bank[1]]
    ps_t = m.bank[2]
    ps_log = m.bank[3][:, 0:EXPERTS]
    ps_pos = m.bank[4][:, 0:EXPERTS]
    ROWS_CH, GATE_CH = 13, 12

    def tile_of(t, n):
        return t[:, bass.ds(n, 1), 0:DIM].rearrange("p t c -> p (t c)")

    with nc.Block() as block:
        @block.sync
        def _(sp):
            for t, vec in ((bias, a.bias), (gamma, a.gamma), (beta, a.beta)):
                sp.dma_start(t[:, :], vec.partition_broadcast(P)).then_inc(s["const"], 16)
            for half in range(2):
                sp.dma_start(gate_w[:, half, :], a.gate_w[half * P:half * P + P, :]).then_inc(s["const"], 16)
            sp.dma_start(gate_b[:, :], a.gate_b.unsqueeze(0)).then_inc(s["const"], 16)

            def tile(n, q):
                if later(n):
                    sp.wait_ge(s["out"], n - 1)
                    settle(sp, m)
                sp.dma_start(acc[:, q, :, :].rearrange("p h c -> p (h c)"), m.d_acc[bass.ds(n * P, P), :]).then_inc(s["in"][q], 16)
            over_tiles(sp, tile)
            sp.wait_ge(s["const"], 96)

        @block.gpsimd
        def _(pool):
            pool.memset(neghalf[:, :], -0.5).then_inc(s["init"], 1)
            pool.memset(seen[:, :], 0.0).then_inc(s["init"], 1)
            pool.wait_ge(s["init"], 2)
            pool.wait_ge(s["const"], 96)

            def turn(lead, ql, lag, qg):
                if lead is not None:
                    if later(lead) or lead >= 1:
                        pool.wait_ge(s["x1"], lead)
                    pool.tensor_tensor(xb[:, :], tile_of(m.x, lead), beta[:, :], ALU.add).then_inc(s["shifted"], 1)
                    for norms in (1, 2):
                        pool.wait_ge(s["var"], lead * 2 + norms)
                        rstd_pool(pool, rs[:, :], ve[:, :], neghalf[:, :]).then_inc(s["rstd"], 1)
                if lag is not None:
                    pool.wait_ge(s["slot"], lag + 1)
                    settle(pool, m)
                    pool.indirect_dma_start(m.d_in, bass.IndirectOffsetOnAxis(ap=place[qg][:, 0:1], axis=0),
                                            norm[qg][:, :], None).then_inc(s["scattered"][qg], 16)
            skewed(pool, turn)
            for q in range(2):
                pool.wait_ge(s["scattered"][q], 16 * (TILES // 2))

        @block.scalar
        def _(act):
            def turn(lead, ql, lag, qg):
                if lead is not None:
                    if later(lead):
                        act.wait_ge(s["mixps"], lead - 1)
                    act.copy(xnt[:, ql, :], tile_of(m.xnt, lead)).then_inc(s["xt"], 1)
                    act.wait_ge(s["out"], lead + 1)
                    act.activation(low[:, :], out[:, :], ACT.Relu, scale=-1.0).then_inc(s["neg_part"], 1)
                    act.wait_ge(s["neg_part"], lead + 1)
                    act.activation(lowe[:, :], low[:, :], ACT.Exp, scale=-1.0).then_inc(s["low_e"], 1)
                if lag is not None:
                    act.wait_ge(s["gex"], lag + 1)
                    act.activation(ex[:, :], lg[:, :], ACT.Exp, accum_out=tot[:, 0:1]).then_inc(s["gexed"], 1)
                if lead is not None:
                    act.wait_ge(s["normps"], lead + 1)
                    act.copy(normt[:, :], ps_t[:, 0:DIM]).then_inc(s["normt"], 1)
            skewed(act, turn)

        @block.vector
        def _(dve):
            dve.wait_ge(s["const"], 96)
            dve.wait_ge(s["init"], 2)
            dve.tensor_scalar(trash[:, :], m.tile_ids[:, :, 0], float(TRASH), None, ALU.add).then_inc(s["init"], 1)
            dve.wait_ge(s["init"], 3)
            heads = lambda t: t.rearrange("p (h c) -> p h c", h=HEADS)

            def close_softmax(n, q, ch):
                dve.wait_ge(s["in"][q], (uses(n, q) + 1) * 16)
                ch.step(dve.tensor_scalar(den[:, :], acc[:, q, :, HEAD], 1e-16, None, ALU.add))
                ch.step(dve.reciprocal(den[:, :], den[:, :]))
                ch.step(dve.tensor_tensor(heads(out[:, :]), acc[:, q, :, 0:HEAD], den[:, :].unsqueeze(2).to_broadcast([P, HEADS, HEAD]), ALU.mult))
                dve.tensor_tensor(out[:, :], out[:, :], bias[:, :], ALU.add).then_inc(s["out"], 1)
                dve.wait_ge(s["out"], n + 1)

            def residual(n, q, ch):
                dve.wait_ge(s["low_e"], n + 1)
                ch.step(dve.scalar_tensor_tensor(out=hid[:, :], in0=out[:, :], scalar=0.0, in1=lowe[:, :], op0=ALU.max, op1=ALU.add))
                ch.step(dve.scalar_tensor_tensor(out=hid[:, :], in0=hid[:, :], scalar=-1.0, in1=tile_of(m.xn, n), op0=ALU.add, op1=ALU.add))
                ch.step(dve.bn_stats(st[:, :], hid[:, :]), settled=m)
                ch.step(dve.bn_aggr(mv[:, :], st[:, :]))
                dve.tensor_scalar(ve[:, :], mv[:, 1:2], LN_EPS, None, ALU.add).then_inc(s["var"], 1)

            def first_sum(n, q, ch):
                dve.wait_ge(s["rstd"], n * 2 + 1)
                ch.step(dve.tensor_scalar(hid[:, :], hid[:, :], mv[:, 0:1], rs[:, 0:1], ALU.subtract, ALU.mult))
                ch.step(dve.tensor_tensor(hid[:, :], hid[:, :], gamma[:, :], ALU.mult))
                dve.wait_ge(s["shifted"], n + 1)
                ch.step(dve.tensor_tensor(hid[:, :], hid[:, :], xb[:, :], ALU.add))
                dve.wait_ge(s["mixps"], n + 1)
                ch.step(dve.tensor_tensor(hid[:, :], hid[:, :], ps_mix[q][:, 0:DIM], ALU.add))
                dve.tensor_copy(tile_of(m.x, n), hid[:, :]).then_inc(s["x1"], 1)
                ch.step(dve.bn_stats(st[:, :], hid[:, :]), settled=m)
                ch.step(dve.bn_aggr(mv[:, :], st[:, :]))
                dve.tensor_scalar(ve[:, :], mv[:, 1:2], LN_EPS, None, ALU.add).then_inc(s["var"], 1)

            def second_norm(n, q, ch):
                dve.wait_ge(s["rstd"], n * 2 + 2)
                if later(n):
                    dve.wait_ge(s["scattered"][q], uses(n, q) * 16)
                    dve.wait_ge(s["normps"], n - 1)
                dve.tensor_scalar(norm[q][:, :], hid[:, :], mv[:, 0:1], rs[:, 0:1], ALU.subtract, ALU.mult).then_inc(s["norm"], 1)
                dve.wait_ge(s["norm"], n + 1)

            def gate_shift(n, ch):
                dve.wait_ge(s["logits"], n + 1)
                ch.step(dve.tensor_reduce(mx[:, :], ps_log, AX.X, ALU.max))
                dve.tensor_scalar(lg[:, :], ps_log, mx[:, 0:1], None, ALU.subtract).then_inc(s["gex"], 1)

            def gate_choice(n, ch):
                dve.wait_ge(s["gexed"], n + 1)
                ch.step(dve.reciprocal(rtot[:, :], tot[:, :]))
                ch.step(dve.tensor_scalar(prob[:, :], ex[:, :], rtot[:, 0:1], None, ALU.mult))
                ch.step(dve.tensor_reduce(best[:, :], prob[:, :], AX.X, ALU.max))
                ch.step(dve.tensor_scalar(cand[:, :], prob[:, :], best[:, 0:1], 100.0, ALU.is_lt, ALU.mult))
                ch.step(dve.tensor_tensor(cand[:, :], cand[:, :], m.expert_row[:, :], ALU.add))
                ch.step(dve.tensor_reduce(which[:, :], cand[:, :], AX.X, ALU.min))
                dve.tensor_scalar(first[:, :], which[:, :], float(CAP), None, ALU.mult)
                dve.tensor_scalar(hot[:, :], m.expert_row[:, :], which[:, 0:1], None, ALU.is_equal).then_inc(s["oh"], 1)
                dve.wait_ge(s["oh"], n + 1)

            def places(n, q, ch):
                dve.wait_ge(s["posps"], n + 1)
                ch.step(dve.tensor_tensor(pos[:, :], ps_pos, hot[:, :], ALU.mult))
                dve.tensor_tensor(seen[:, :], seen[:, :], hot[:, :], ALU.add)
                ch.step(dve.tensor_reduce(posr[:, :], pos[:, :], AX.X, ALU.add))
                dve.tensor_scalar(kept[:, :], posr[:, :], float(CAP), None, ALU.is_le)
                ch.step(dve.tensor_scalar(at[:, :], posr[:, :], float(CAP), -1.0, ALU.min, ALU.add))
                ch.step(dve.tensor_tensor(at[:, :], at[:, :], first[:, :], ALU.add))
                dve.tensor_copy(m.slot[:, bass.ds(n, 1)], at[:, :])
                dve.tensor_tensor(m.share[:, bass.ds(n, 1)], best[:, :], kept[:, :], ALU.mult)
                ch.step(dve.tensor_tensor(at[:, :], at[:, :], trash[:, bass.ds(n, 1)], ALU.subtract))
                dve.scalar_tensor_tensor(out=place[q][:, :], in0=at[:, :], scalar=kept[:, 0:1], in1=trash[:, bass.ds(n, 1)],
                                         op0=ALU.mult, op1=ALU.add).then_inc(s["slot"], 1)
                dve.wait_ge(s["slot"], n + 1)
                assert ch.n == GATE_CH, ch.n

            def turn(lead, ql, lag, qg):
                rows = lead is not None and Chain(dve, s["row_chain"], lead * ROWS_CH)
                gates = lag is not None and Chain(dve, s["gate_chain"], lag * GATE_CH)
                if rows:
                    close_softmax(lead, ql, rows)
                if gates:
                    gate_shift(lag, gates)
                if rows:
                    residual(lead, ql, rows)
                if gates:
                    gate_choice(lag, gates)
                if rows:
                    first_sum(lead, ql, rows)
                if gates:
                    places(lag, qg, gates)
                if rows:
                    second_norm(lead, ql, rows)
                    assert rows.n == ROWS_CH, rows.n
            skewed(dve, turn)

        @block.tensor
        def _(pe):
            pe.wait_ge(s["const"], 96)
            pe.wait_ge(s["init"], 2)

            def turn(lead, ql, lag, qg):
                if lead is not None:
                    pe.wait_ge(s["xt"], lead + 1)
                    if later(lead):
                        pe.wait_ge(s["x1"], lead - 1)
                    for half in range(2):
                        pe.matmul(ps_mix[ql][:, 0:DIM], xnt[:, ql, half * P:half * P + P], m.w_mix[:, half, :], start=(half == 0), stop=False)
                    pe.matmul(ps_mix[ql][:, 0:DIM], m.ones[0:1, :], m.b_mix[:, :], start=False, stop=True).then_inc(s["mixps"], 1)
                if lag is not None:
                    pe.wait_ge(s["oh"], lag + 1)
                    pe.matmul(ps_pos, m.tri[:, :], hot[:, :], start=True, stop=False)
                    pe.matmul(ps_pos, m.ones[:, :], seen[:, :], start=False, stop=True).then_inc(s["posps"], 1)
                if lead is not None:
                    pe.wait_ge(s["norm"], lead + 1)
                    for half in range(2):
                        last = pe.transpose(ps_t[:, half * P:half * P + P], norm[ql][:, half * P:half * P + P], m.ident[:, :])
                    last.then_inc(s["normps"], 1)
                    pe.wait_ge(s["normt"], lead + 1)
                    for half in range(2):
                        pe.matmul(ps_log, normt[:, half * P:half * P + P], gate_w[:, half, :], start=(half == 0), stop=False)
                    pe.matmul(ps_log, m.ones[0:1, :], gate_b[:, :], start=False, stop=True).then_inc(s["logits"], 1)
            skewed(pe, turn)


def experts(nc, ctx, m, a):
    sb = lambda name, shape, dt=F32: ctx.enter_context(nc.sbuf_tensor(name, shape, dt))
    s = sem_set(nc, m.sems, "exp", "w* rows* rowst rowsb up hid down y yt yb stored*")
    w1 = sb("f_w1", [P, 2, 2, FF])
    w2 = sb("f_w2", [P, 2, FCH, DIM])
    b1 = sb("f_b1", [P, 2, FCH])
    b2 = sb("f_b2", [P, 2, 2])
    rows = sb("f_rows", [P, 2, 4, DIM])
    rowst = sb("f_rowst", [P, 2, CAP])
    hid = sb("f_hid", [P, FCH, CAP])
    yt = sb("f_yt", [P, 2, CAP])
    y = sb("f_y", [P, 2, 4, DIM])
    WL = 16 * 4

    def over_experts(eng, body):
        body(0, 0, 0)
        body(1, 1, 0)
        with eng.Fori(1, EXPERTS // 2) as it:
            body(it * 2, 0, it)
            body(it * 2 + 1, 1, it)

    with nc.Block() as block:
        @block.sync
        def _(sp):
            def expert(e, q, turn):
                if later(e):
                    sp.wait_ge(s["y"], (e - 1) * 2)
                    settle(sp, m)
                one = bass.ds(e, 1)
                sp.dma_start(w1[:, q, :, :], a.w1[one].rearrange("e (c p) f -> p (e c) f", p=P)).then_inc(s["w"][q], 16)
                sp.dma_start(w2[:, q, :, :], a.w2[one].rearrange("e (c p) d -> p (e c) d", p=P)).then_inc(s["w"][q], 16)
                sp.dma_start(b1[:, q, :], a.b1[one].rearrange("e (c p) -> p (e c)", p=P), allow_slow_non_contiguous=True).then_inc(s["w"][q], 16)
                sp.dma_start(b2[:, q, :], a.b2[one].rearrange("e (c p) -> p (e c)", p=P), allow_slow_non_contiguous=True).then_inc(s["w"][q], 16)
                for j, n in enumerate(CTS):
                    sp.dma_start(rows[0:n, q, j, :], m.d_in[bass.ds(e * CAP + j * CT, n), :]).then_inc(s["rows"][q], 16)
            over_experts(sp, expert)

        @block.tensor
        def _(pe):
            def expert(e, q, turn):
                pe.wait_ge(s["rows"][q], (turn + 1) * 64)
                if later(e) or e >= 1:
                    pe.wait_ge(s["y"], e * 2)
                    pe.wait_ge(s["rowsb"], e * 2)
                for half in range(2):
                    for j, n in enumerate(CTS):
                        last = pe.transpose(m.bank[half][:, j * CT:j * CT + n], rows[0:n, q, j, half * P:half * P + P], m.ident[0:n, 0:n])
                    last.then_inc(s["rowst"], 1)
                pe.wait_ge(s["w"][q], (turn + 1) * WL)
                pe.wait_ge(s["rowsb"], e * 2 + 2)
                for f in range(FCH):
                    if not (isinstance(e, int) and e == 0 and f < 2):
                        pe.wait_ge(s["hid"], e * FCH + f - 1)
                    for half in range(2):
                        last = pe.matmul(m.bank[2 + f % 2][:, 0:CAP], w1[:, q, half, f * P:f * P + P], rowst[:, half, :],
                                         start=(half == 0), stop=(half == 1))
                    last.then_inc(s["up"], 1)
                for out in range(2):
                    for f in range(FCH):
                        pe.wait_ge(s["hid"], e * FCH + f + 1)
                        last = pe.matmul(m.bank[4 + out][:, 0:CAP], w2[:, q, f, out * P:out * P + P], hid[:, f, :],
                                         start=(f == 0), stop=(f == FCH - 1))
                    last.then_inc(s["down"], 1)
                pe.wait_ge(s["y"], e * 2 + 2)
                for j, n in enumerate(CTS):
                    if j % 2 == 0 and not (isinstance(e, int) and e == 0):
                        pe.wait_ge(s["yb"], e * 4)
                    for out in range(2):
                        last = pe.transpose(m.bank[6 + j // 2][0:n, (j % 2) * DIM + out * P:(j % 2) * DIM + out * P + P],
                                            yt[:, out, j * CT:j * CT + n], m.ident[:, :])
                    last.then_inc(s["yt"], 1)
            over_experts(pe, expert)

        @block.scalar
        def _(act):
            def expert(e, q, turn):
                for half in range(2):
                    act.wait_ge(s["rowst"], e * 2 + 1 + half)
                    act.copy(rowst[:, half, :], m.bank[half][:, 0:CAP]).then_inc(s["rowsb"], 1)
                act.wait_ge(s["w"][q], (turn + 1) * WL)
                for f in range(FCH):
                    act.wait_ge(s["up"], e * FCH + f + 1)
                    act.activation(hid[:, f, :], m.bank[2 + f % 2][:, 0:CAP], ACT.Relu, bias=b1[:, q, f:f + 1]).then_inc(s["hid"], 1)
                for out in range(2):
                    act.wait_ge(s["down"], e * 2 + out + 1)
                    if later(e) or e >= 1:
                        act.wait_ge(s["yt"], e * 4)
                    act.activation(yt[:, out, :], m.bank[4 + out][:, 0:CAP], ACT.Identity, bias=b2[:, q, out:out + 1]).then_inc(s["y"], 1)
            over_experts(act, expert)

        @block.vector
        def _(dve):
            def expert(e, q, turn):
                if later(e):
                    dve.wait_ge(s["stored"][q], turn * 64)
                for j, n in enumerate(CTS):
                    dve.wait_ge(s["yt"], e * 4 + j // 2 * 2 + 2)
                    dve.tensor_copy(y[0:n, q, j, :], m.bank[6 + j // 2][0:n, (j % 2) * DIM:(j % 2) * DIM + DIM]).then_inc(s["yb"], 1)
            over_experts(dve, expert)

        @block.gpsimd
        def _(pool):
            def expert(e, q, turn):
                for j, n in enumerate(CTS):
                    pool.wait_ge(s["yb"], e * 4 + j + 1)
                    settle(pool, m)
                    pool.dma_start(m.d_out[bass.ds(e * CAP + j * CT, n), :], y[0:n, q, j, :]).then_inc(s["stored"][q], 16)
            over_experts(pool, expert)
            for q in range(2):
                pool.wait_ge(s["stored"][q], 64 * (EXPERTS // 2))


def combine(nc, ctx, m, a):
    sb = lambda name, shape, dt=F32: ctx.enter_context(nc.sbuf_tensor(name, shape, dt))
    s = sem_set(nc, m.sems, "cmb", "init places y* gated chain out stored*")
    slot = [sb(f"c_slot{q}", [P, 1], I32) for q in range(2)]
    y = [sb(f"c_y{q}", [P, DIM]) for q in range(2)]
    ys = sb("c_ys", [P, 2, DIM])
    bad = sb("c_bad", [P, 3, DIM], I32)
    subst = sb("c_subst", [P, 3, DIM])
    out = sb("c_out", [P, 2, DIM])
    HUGE = 3.4028234663852886e38
    CH = 5

    def all_tiles(eng, body):
        body(0, 0, P)
        body(1, 1, P)
        with eng.Fori(1, TILES // 2 - 1) as it:
            body(it * 2, 0, P)
            body(it * 2 + 1, 1, P)
        body(TILES - 2, 0, P)
        body(TILES - 1, 1, LAST)

    with nc.Block() as block:
        @block.gpsimd
        def _(pool):
            for i, value in enumerate((0.0, 1e4, -1e4)):
                pool.memset(subst[:, i, :], value).then_inc(s["init"], 1)

            def tile(n, q, rows):
                if later(n):
                    pool.wait_ge(s["y"][q], uses(n, q) * 16)
                pool.tensor_copy(slot[q][:, :], m.slot[:, bass.ds(n, 1)]).then_inc(s["places"], 1)
                pool.wait_ge(s["places"], n + 1)
                if later(n):
                    pool.wait_ge(s["gated"], n - 1)
                settle(pool, m)
                pool.indirect_dma_start(y[q][:, :], None, m.d_out, bass.IndirectOffsetOnAxis(ap=slot[q][:, 0:1], axis=0)).then_inc(s["y"][q], 16)
            all_tiles(pool, tile)

        @block.vector
        def _(dve):
            dve.wait_ge(s["init"], 3)

            def tile(n, q, rows):
                ch = Chain(dve, s["chain"], n * CH)
                dve.wait_ge(s["gated"], n + 1)
                dve.tensor_tensor(bad[:, 0, :], ys[:, q, :], ys[:, q, :], ALU.not_equal)
                ch.step(dve.tensor_scalar(bad[:, 1, :], ys[:, q, :], HUGE, None, ALU.is_gt))
                ch.step(dve.tensor_scalar(bad[:, 2, :], ys[:, q, :], -HUGE, None, ALU.is_lt), settled=m)
                for i in range(3):
                    ch.step(dve.copy_predicated(ys[:, q, :], bad[:, i, :], subst[:, i, :]), settled=m if i < 2 else None)
                if later(n):
                    dve.wait_ge(s["stored"][q], uses(n, q) * 16)
                dve.tensor_tensor(out[:, q, :], ys[:, q, :], m.x[:, bass.ds(n, 1), :].rearrange("p t c -> p (t c)"), ALU.add).then_inc(s["out"], 1)
                assert ch.n == CH
            all_tiles(dve, tile)

        @block.scalar
        def _(act):
            def tile(n, q, rows):
                act.wait_ge(s["y"][q], (uses(n, q) + 1) * 16)
                if later(n):
                    act.wait_ge(s["out"], n - 1)
                act.activation(ys[:, q, :], y[q][:, :], ACT.Copy, scale=m.share[:, bass.ds(n, 1)]).then_inc(s["gated"], 1)
            all_tiles(act, tile)

        @block.sync
        def _(sp):
            def tile(n, q, rows):
                sp.wait_ge(s["out"], n + 1)
                settle(sp, m)
                sp.dma_start(a.out[bass.ds(n * P, rows), :], out[0:rows, q, :]).then_inc(s["stored"][q], 16)
            all_tiles(sp, tile)
            for q in range(2):
                sp.wait_ge(s["stored"][q], 16 * (TILES // 2))


_INS = ["x", "src", "dst", "L0_gnn_W_l", "L0_gnn_W_r", "L0_gnn_att", "L0_gnn_bias", "L0_gnn_gamma", "L0_gnn_beta",
        "L0_mix_W_qk", "L0_mix_b_qk", "L0_mix_W_v", "L0_mix_b_v", "L0_mix_gamma", "L0_mix_beta", "L0_ffn_gate_w",
        "L0_ffn_gate_b", "L0_ffn_w1", "L0_ffn_b1", "L0_ffn_w2", "L0_ffn_b2"]


def graph_block(nc, x, src, dst, W_l, W_r, att, bias, gamma, beta, W_qk, b_qk, W_v, b_v, mix_gamma, mix_beta,
                gate_w, gate_b, w1, b1, w2, b2, out):
    a = Arrays()
    a.x, a.src, a.dst, a.out = x, src, dst, out
    a.W_l, a.W_r, a.att, a.bias, a.gamma, a.beta = W_l, W_r, att, bias, gamma, beta
    a.W_qk, a.b_qk, a.W_v, a.b_v, a.mix_gamma, a.mix_beta = W_qk, b_qk, W_v, b_v, mix_gamma, mix_beta
    a.gate_w, a.gate_b, a.w1, a.b1, a.w2, a.b2 = gate_w, gate_b, w1, b1, w2, b2
    with ExitStack() as whole:
        m = memory(nc, whole)
        m.sems = whole
        for stage in (prepare, project, lambdas, attend, node_update, experts, combine):
            with ExitStack() as buffers:
                stage(nc, buffers, m, a)


def kernel(**inputs):
    import numpy as _np
    import concourse.bacc as _bacc
    from concourse import mybir as _mybir
    from concourse.bass_utils import run_bass_kernel_spmd as _run

    nc = _bacc.Bacc("TRN2", target_bir_lowering=False, num_devices=1)
    arrays, args = {}, []
    for name in _INS:
        a = _np.ascontiguousarray(inputs[name])
        arrays[f"in_{name}_dram"] = a
        args.append(nc.dram_tensor(f"in_{name}_dram", a.shape, _mybir.dt.from_np(a.dtype), kind="ExternalInput").ap())
    args.append(nc.dram_tensor("out_0_dram", (NODES, DIM), F32, kind="ExternalOutput").ap())
    graph_block(nc, *args)
    r = _run(nc, [arrays], core_ids=[0])
    return r.results[0]["out_0_dram"]
```

```python
from contextlib import ExitStack

import concourse.bass as bass
from concourse import mybir

F32 = mybir.dt.float32
BF16 = mybir.dt.bfloat16
I32 = mybir.dt.int32
I16 = mybir.dt.int16
U32 = mybir.dt.uint32
ALU = mybir.AluOpType
ACT = mybir.ActivationFunctionType
AX = mybir.AxisListType

P = 128
NODES, DIM = 2500, 256
HEADS, HEAD = 4, 64
EDGES = 80000
TILES = -(-NODES // P)
PAD = TILES * P
LAST = NODES - (TILES - 1) * P
G = 4
EDGES_STEP = G * P
BLOCKS = -(-EDGES // EDGES_STEP)
EDGES_PAD = BLOCKS * EDGES_STEP
STEPS = BLOCKS + TILES - 1
ECOLS = EDGES // P
ROW = DIM + HEADS
ROW3 = 3 * ROW + 4
HCOLS = HEAD + 1
RING = 4
BIG = 1e30
EXPERTS, FF = 8, 1024
CAP = -(-5 * NODES // (4 * EXPERTS))
FCH = FF // P
CT = -(-CAP // 4)
CTS = [CT, CT, CT, CAP - 3 * CT]
TRASH = EXPERTS * CAP
LN_EPS = 1e-5
CONSTANTS = 16 * 16


def settle(eng, m):
    eng.sem_inc(m.met, 1)


class Chain:

    def __init__(self, eng, sem, base):
        self.eng, self.sem, self.base, self.n = eng, sem, base, 0

    def step(self, ins, settled=None):
        self.n += 1
        ins.then_inc(self.sem, 1)
        self.eng.wait_ge(self.sem, self.base + self.n)
        if settled:
            settle(self.eng, settled)


def over_tiles(eng, body, count=TILES):
    body(0, 0)
    body(1, 1)
    with eng.Fori(1, count // 2) as it:
        body(it * 2, 0)
        body(it * 2 + 1, 1)


def skewed(eng, turn):
    turn(0, 0, None, None)
    for n in range(1, 4):
        turn(n, n % 2, n - 1, (n - 1) % 2)
    with eng.Fori(2, TILES // 2) as it:
        turn(it * 2, 0, it * 2 - 1, 1)
        turn(it * 2 + 1, 1, it * 2, 0)
    turn(None, None, TILES - 1, (TILES - 1) % 2)


def over_fours(eng, body, tail=0):
    for n in range(4):
        body(n, n)
    with eng.Fori(1, TILES // 4 - tail) as it:
        for r in range(4):
            body(it * 4 + r, r)
    for n in range(TILES - 4 * tail, TILES):
        body(n, n % 4)


def turns(n, r):
    return n // 4 if isinstance(n, int) else (n - r) // 4


def uses(n, q):
    return n // 2 if isinstance(n, int) else (n - q) // 2


def later(n):
    return not isinstance(n, int) or n >= 2



def sem_set(nc, ctx, prefix, names):
    sems = {}
    for name in names.split():
        if name[-1] == "*":
            sems[name[:-1]] = [ctx.enter_context(nc.semaphore(f"{prefix}_{name[:-1]}{i}")) for i in range(2)]
        else:
            sems[name] = ctx.enter_context(nc.semaphore(f"{prefix}_{name}"))
    return sems


class Memory:
    pass


class Arrays:
    pass


def memory(nc, ctx):
    m = Memory()

    def sb(name, shape, dt=F32):
        return ctx.enter_context(nc.sbuf_tensor(name, shape, dt))

    def dram(name, shape, dt=F32):
        return nc.dram_tensor(name, shape, dt, kind="Internal").ap()

    m.ident = sb("ident", [P, P])
    m.ones = sb("ones", [P, P])
    m.tri = sb("tri", [P, P])
    m.lane_row = sb("lane_row", [P, P], BF16)
    m.tile_ids = sb("tile_ids", [P, TILES, 2])
    m.expert_row = sb("expert_row", [P, EXPERTS])
    m.dstf = sb("dst_f32", [P, ECOLS])
    m.dst16 = sb("dst_i16", [P, ECOLS], I16)
    m.pen = sb("penalty", [P, ECOLS])
    m.padf = sb("pad_f32", [P, 8])
    m.padpen = sb("pad_penalty", [P, 8])
    m.pad16 = sb("pad_i16", [P, 8], I16)
    m.padi = sb("pad_i32", [P, 8], I32)
    m.zero = sb("zero", [P, 2048])
    m.window = sb("window", [1, STEPS], I32)
    m.start = sb("start", [1, STEPS], I32)
    m.x = sb("x_rows", [P, TILES, DIM])
    m.xn = sb("xn_rows", [P, TILES, DIM + 1])
    m.xnt = sb("xnt_rows", [P, TILES, DIM])
    m.w_lr = sb("w_lr", [P, 2, 2, ROW])
    m.w_q = sb("w_q", [P, 2, DIM])
    m.w_k = sb("w_k", [P, 2, DIM])
    m.w_v = sb("w_v", [P, 2, DIM])
    m.att_row = sb("att_row", [P, DIM])
    m.att_col = sb("att_col", [P, 2, HEADS])
    m.key_max = sb("key_max", [P, 2, TILES])
    m.w_mix = sb("w_mix", [P, 2, DIM])
    m.b_mix = sb("b_mix", [1, DIM])
    m.slot = sb("slot", [P, TILES], I32)
    m.share = sb("share", [P, TILES])
    m.bank = [ctx.enter_context(nc.psum_tensor(f"bank{i}", [P, 512], F32)) for i in range(8)]

    m.w1 = sb("w1_rows", [P, 2, 2, FF])
    m.w2 = sb("w2_rows", [P, 2, FCH, DIM])
    m.b1 = sb("b1_cols", [P, 2, FCH])
    m.b2 = sb("b2_cols", [P, 2, 2])
    m.bv = sb("b_v", [P, DIM])
    m.bk_row = sb("b_k_row", [1, DIM])
    m.cols = sb("lambda_cols", [P, 2, 4])
    m.bias = sb("gat_bias", [P, DIM])
    m.gamma = sb("gat_gamma", [P, DIM])
    m.beta = sb("gat_beta", [P, DIM])
    m.gate_w = sb("gate_w", [P, 2, EXPERTS])
    m.gate_b = sb("gate_b", [1, EXPERTS])
    m.constants = ctx.enter_context(nc.semaphore("constants"))
    m.prepared = ctx.enter_context(nc.semaphore("prepared"))
    m.weights_in = [ctx.enter_context(nc.semaphore(f"weights_in{q}")) for q in range(2)]
    m.met = ctx.enter_context(nc.semaphore("met"))
    m.d_xl = dram("d_xl", (PAD, ROW))
    m.d_xr = dram("d_xr", (PAD, ROW3), BF16)
    m.d_src = dram("d_src", (EDGES_PAD,), I32)
    m.d_dst = dram("d_dst", (EDGES_PAD,))
    m.d_dst16 = dram("d_dst16", (EDGES_PAD,), I16)
    m.d_pen = dram("d_pen", (EDGES_PAD + P,))
    m.d_acc = dram("d_acc", (PAD, HEADS * HCOLS))
    m.d_in = dram("d_in", (TRASH + PAD, DIM))
    m.d_out = dram("d_out", (TRASH, DIM))
    return m


def prepare(nc, ctx, m, a):
    sb = lambda name, shape, dt=F32: ctx.enter_context(nc.sbuf_tensor(name, shape, dt))
    s = sem_set(nc, m.sems, "pre", "weights att ids dst ident ones chain scaled edges fill")
    dst = sb("p_dst", [P, ECOLS], I32)
    prev = sb("p_prev", [P, ECOLS], I32)
    dstf = m.dstf
    prevf = sb("p_prevf", [P, ECOLS])
    dst16, pen, padf, padpen, pad16, padi, zero = m.dst16, m.pen, m.padf, m.padpen, m.pad16, m.padi, m.zero
    lane = sb("p_lane", [P, P], I32)
    ids = sb("p_ids", [P, TILES, 2], I32)
    eids = sb("p_eids", [P, EXPERTS], I32)
    att_raw = sb("p_att_raw", [P, DIM])
    wa = sb("p_wa", [P, DIM])
    tail = EDGES_PAD - EDGES
    TAILS = 48
    assert tail == TAILS * 8

    with nc.Block() as block:
        @block.sync
        def _(sp):
            sp.wait_ge(s["ones"], 9)
            flat = a.dst
            sp.dma_start(dst[:, :], flat.rearrange("(p c) -> p c", p=P)).then_inc(s["dst"], 16)
            sp.dma_start(prev[0:1, 1:ECOLS], flat[0:ECOLS - 1].unsqueeze(0)).then_inc(s["dst"], 16)
            sp.dma_start(prev[1:P, :], flat[ECOLS - 1:EDGES - 1].rearrange("(p c) -> p c", c=ECOLS)).then_inc(s["dst"], 16)
            sp.dma_start(m.d_src[0:EDGES].rearrange("(r c) -> r c", r=16), a.src.rearrange("(r c) -> r c", r=16)).then_inc(s["fill"], 16)
            full = TILES - 1
            sp.dma_start(m.x[:, 0:full, :], a.x[0:full * P, :].rearrange("(t p) c -> p t c", p=P)).then_inc(s["fill"], 16)
            sp.dma_start(m.x[0:LAST, full, :], a.x[full * P:NODES, :]).then_inc(s["fill"], 16)
            sp.dma_start(att_raw[:, :], a.att.rearrange("h c -> (h c)").partition_broadcast(P)).then_inc(s["att"], 16)
            for h in range(HEADS):
                lo = (h % 2) * HEAD
                sp.dma_start(m.att_col[lo:lo + HEAD, h // 2, h:h + 1], a.att[h, :].unsqueeze(1)).then_inc(s["att"], 16)
            for half in range(2):
                rows = slice(half * P, half * P + P)
                sp.dma_start(m.w_lr[:, half, 0, 0:DIM], a.W_l[rows, :]).then_inc(s["weights"], 16)
                sp.dma_start(m.w_lr[:, half, 1, 0:DIM], a.W_r[rows, :]).then_inc(s["weights"], 16)
                sp.dma_start(m.w_q[:, half, :], a.W_qk[0, rows, :]).then_inc(s["weights"], 16)
                sp.dma_start(m.w_k[:, half, :], a.W_qk[1, rows, :]).then_inc(s["weights"], 16)
                sp.dma_start(m.w_v[:, half, :], a.W_v[rows, :]).then_inc(s["weights"], 16)
            sp.wait_ge(s["edges"], 3)
            for out, inn, pad in ((m.d_dst, dstf, padf[0:TAILS, :]), (m.d_dst16, dst16, pad16[0:TAILS, :]), (m.d_pen, pen, None)):
                sp.dma_start(out[0:EDGES].rearrange("(p c) -> p c", p=P), inn[:, :]).then_inc(m.prepared, 16)
                if pad is not None:
                    sp.dma_start(out[EDGES:EDGES_PAD].rearrange("(p c) -> p c", c=8), pad).then_inc(m.prepared, 16)
            sp.dma_start(m.d_pen[EDGES:EDGES_PAD + P].rearrange("(p c) -> p c", c=8), padpen[0:(tail + P) // 8, :]).then_inc(m.prepared, 16)
            sp.dma_start(m.d_src[EDGES:EDGES_PAD].rearrange("(p c) -> p c", c=8), padi[0:TAILS, :]).then_inc(m.prepared, 16)
            total = TRASH * DIM
            m.edges_stored = 16 * (7 + -(-total // (P * 2048)))
            for lo in range(0, total, P * 2048):
                n = min(P * 2048, total - lo) // 2048
                sp.dma_start(m.d_in.rearrange("r c -> (r c)")[lo:lo + n * 2048].rearrange("(p c) -> p c", c=2048),
                             zero[0:n, :]).then_inc(m.prepared, 16)
            sp.wait_ge(s["weights"], 160)
            sp.wait_ge(s["fill"], 48)

        @block.gpsimd
        def _(pool):
            pool.memset(prev[:, :], -1).then_inc(s["ones"], 1)
            pool.memset(m.att_col[:, :, :], 0.0).then_inc(s["ones"], 1)
            pool.memset(zero[:, :], 0.0).then_inc(s["ones"], 1)
            pool.memset(m.ones[:, :], 1.0).then_inc(s["ones"], 1)
            pool.memset(m.ident[:, :], 0.0).then_inc(s["ones"], 1)
            pool.memset(padf[:, :], 4095.0).then_inc(s["ones"], 1)
            pool.memset(m.x[:, TILES - 1, :], 0.0).then_inc(s["ones"], 1)
            pool.memset(padi[:, :], 0).then_inc(s["ones"], 1)
            pool.memset(padpen[:, :], -BIG).then_inc(s["ones"], 1)
            pool.iota(lane[:, :], [[1, P]], base=0, channel_multiplier=0).then_inc(s["ids"], 1)
            pool.iota(ids[:, :, 0], [[P, TILES]], base=0, channel_multiplier=1).then_inc(s["ids"], 1)
            pool.iota(ids[:, :, 1], [[P, TILES]], base=0, channel_multiplier=0).then_inc(s["ids"], 1)
            pool.iota(eids[:, :], [[1, EXPERTS]], base=0, channel_multiplier=0).then_inc(s["ids"], 1)
            pool.wait_ge(s["ones"], 9)
            pool.affine_select(out=m.ident[:, :], in_=m.ident[:, :], compare_op=ALU.not_equal, fill=1.0, base=0,
                               pattern=[[-1, P]], channel_multiplier=1).then_inc(s["ident"], 1)
            pool.affine_select(out=m.tri[:, :], in_=m.ones[:, :], compare_op=ALU.is_ge, fill=0.0, base=0,
                               pattern=[[1, P]], channel_multiplier=-1).then_inc(s["ident"], 1)

        @block.vector
        def _(dve):
            ch = Chain(dve, s["chain"], 0)
            dve.wait_ge(s["dst"], 48)
            ch.step(dve.tensor_copy(dstf[:, :], dst[:, :]))
            ch.step(dve.tensor_copy(prevf[:, :], prev[:, :]))
            ch.step(dve.tensor_tensor(pen[:, :], dstf[:, :], prevf[:, :], ALU.not_equal))
            dve.tensor_copy(dst16[:, :], dstf[:, :]).then_inc(s["edges"], 1)
            dve.tensor_scalar(pen[:, :], pen[:, :], -BIG, None, ALU.mult).then_inc(s["edges"], 1)
            dve.wait_ge(s["ones"], 9)
            dve.tensor_copy(pad16[:, :], padf[:, :]).then_inc(s["edges"], 1)
            dve.wait_ge(s["ids"], 4)
            dve.tensor_copy(m.lane_row[:, :], lane[:, :]).then_inc(s["scaled"], 1)
            dve.tensor_copy(m.tile_ids[:, :, :], ids[:, :, :]).then_inc(s["scaled"], 1)
            dve.wait_ge(s["scaled"], 2)
            dve.tensor_scalar(m.xn[:, :, DIM], m.tile_ids[:, :, 0], float(NODES), None, ALU.is_lt).then_inc(s["scaled"], 1)
            dve.tensor_copy(m.expert_row[:, :], eids[:, :]).then_inc(s["scaled"], 1)
            dve.wait_ge(s["att"], 80)
            dve.tensor_scalar(m.att_row[:, :], att_raw[:, :], 0.2, None, ALU.mult).then_inc(s["scaled"], 1)
            dve.tensor_scalar(m.att_col[:, :, :], m.att_col[:, :, :], 0.8, None, ALU.mult).then_inc(s["scaled"], 1)
            dve.wait_ge(s["weights"], 160)
            dve.wait_ge(s["scaled"], 6)
            for half in range(2):
                for side in range(2):
                    ch.step(dve.tensor_tensor(wa[:, :], m.w_lr[:, half, side, 0:DIM], m.att_row[:, :], ALU.mult))
                    ch.step(dve.tensor_reduce(m.w_lr[:, half, side, DIM:ROW], wa[:, :].rearrange("p (h c) -> p h c", h=HEADS),
                                              AX.X, ALU.add))


def rstd_pool(pool, out, var, halves):
    return pool.tensor_tensor(out, var, halves, ALU.pow)


def project(nc, ctx, m, a):
    sb = lambda name, shape, dt=F32: ctx.enter_context(nc.sbuf_tensor(name, shape, dt))
    s = sem_set(nc, m.sems, "prj", "var rstd xn xn_kept norm_chain split_chain xtps xt kept right left keysps hi xl rest xr max stored_l* stored_r* neg")
    st = sb("a_st", [P, 6])
    mv = sb("a_mv", [P, 2])
    ve = sb("a_ve", [P, 1])
    rs = sb("a_rs", [P, 1])
    neghalf = sb("a_neghalf", [P, 1])
    xn = sb("a_xn", [P, 2, DIM])
    xnt = sb("a_xnt", [P, 2, DIM])
    xl = sb("a_xl", [P, 2, ROW])
    rest = sb("a_rest", [P, ROW])
    xr3 = sb("a_xr3", [P, 2, ROW3], BF16)
    ps_x = [m.bank[0], m.bank[1]]
    ps_l = [m.bank[2], m.bank[3]]
    ps_r = [m.bank[4], m.bank[5]]
    ps_k = [m.bank[6], m.bank[7]]

    with nc.Block() as block:
        @block.sync
        def _(sp):
            for half in range(2):
                for i, vec in ((3, a.b_qk[1, :]), (0, a.mix_gamma), (1, a.mix_beta), (2, a.b_qk[0, :])):
                    sp.dma_start(m.cols[:, half, i:i + 1], vec[half * P:half * P + P].unsqueeze(1)).then_inc(m.constants, 16)
            sp.dma_start(m.bk_row[:, :], a.b_qk[1, :].unsqueeze(0)).then_inc(m.constants, 16)
            sp.dma_start(m.bv[:, :], a.b_v.partition_broadcast(P)).then_inc(m.constants, 16)
            for t, vec in ((m.bias, a.bias), (m.gamma, a.gamma), (m.beta, a.beta)):
                sp.dma_start(t[:, :], vec.partition_broadcast(P)).then_inc(m.constants, 16)
            for half in range(2):
                sp.dma_start(m.gate_w[:, half, :], a.gate_w[half * P:half * P + P, :]).then_inc(m.constants, 16)
            sp.dma_start(m.gate_b[:, :], a.gate_b.unsqueeze(0)).then_inc(m.constants, 16)

            def tile(n, q):
                sp.wait_ge(s["xr"], n + 1)
                settle(sp, m)
                sp.dma_start(m.d_xr[bass.ds(n * P, P), :], xr3[:, q, :]).then_inc(s["stored_r"][q], 16)
            over_tiles(sp, tile)
            for q in range(2):
                sp.wait_ge(s["stored_r"][q], 16 * (TILES // 2))
                sp.wait_ge(s["stored_l"][q], 16 * (TILES // 2))

        @block.gpsimd
        def _(pool):
            pool.memset(neghalf[:, :], -0.5).then_inc(s["neg"], 1)
            pool.wait_ge(s["neg"], 1)

            def turn(lead, ql, lag, qg):
                if lead is not None:
                    pool.wait_ge(s["var"], lead + 1)
                    rstd_pool(pool, rs[:, :], ve[:, :], neghalf[:, :]).then_inc(s["rstd"], 1)
            skewed(pool, turn)

        @block.vector
        def _(dve):
            dve.wait_ge(s["neg"], 1)

            def key_maximum(n, q, valid=P):
                dve.wait_ge(s["keysps"], n + 1)
                dve.tensor_reduce(m.key_max[:, :, bass.ds(n, 1)].rearrange("p o t -> p (o t)"),
                                  ps_k[q][:, 0:DIM].rearrange("p (o n) -> p o n", o=2)[:, :, 0:valid], AX.X, ALU.max).then_inc(s["max"], 1)

            def layer_norm(n, q):
                ch = Chain(dve, s["norm_chain"], n * 2)
                row = m.x[:, bass.ds(n, 1), :].rearrange("p t c -> p (t c)")
                ch.step(dve.bn_stats(st[:, :], row), settled=m)
                ch.step(dve.bn_aggr(mv[:, :], st[:, :]))
                dve.tensor_scalar(ve[:, :], mv[:, 1:2], LN_EPS, None, ALU.add).then_inc(s["var"], 1)
                dve.wait_ge(s["rstd"], n + 1)
                if later(n):
                    dve.wait_ge(s["xn_kept"], n - 1)
                    dve.wait_ge(s["xtps"], n - 1)
                dve.tensor_scalar(xn[:, q, :], row, mv[:, 0:1], rs[:, 0:1],
                                  ALU.subtract, ALU.mult).then_inc(s["xn"], 1)

            def split(n, q):
                ch = Chain(dve, s["split_chain"], n * 2)
                dve.wait_ge(s["hi"], n + 1)
                if later(n) or n == 1:
                    dve.wait_ge(s["xr"], n)
                if later(n):
                    dve.wait_ge(s["stored_r"][q], uses(n, q) * 16)
                dve.tensor_tensor(rest[:, :], ps_r[q][:, 0:ROW], xr3[:, q, 0:ROW], ALU.subtract).then_inc(s["rest"], 1)
                dve.wait_ge(s["rest"], n + 1)
                ch.step(dve.tensor_copy(xr3[:, q, ROW:2 * ROW], rest[:, :]))
                ch.step(dve.tensor_copy(xr3[:, q, 3 * ROW:ROW3].bitcast(F32), m.tile_ids[:, bass.ds(n, 1), :].rearrange("p t i -> p (t i)")))
                dve.tensor_tensor(xr3[:, q, 2 * ROW:3 * ROW], rest[:, :], xr3[:, q, ROW:2 * ROW],
                                  ALU.subtract).then_inc(s["xr"], 1)

            def tile(n, q, more=True):
                if more:
                    layer_norm(n + 2, q)
                if later(n) or n == 1:
                    key_maximum(n - 1, 1 - q)
                split(n, q)
            layer_norm(0, 0)
            layer_norm(1, 1)
            over_tiles(dve, tile, TILES - 2)
            tile(TILES - 2, 0, more=False)
            tile(TILES - 1, 1, more=False)
            key_maximum(TILES - 1, (TILES - 1) % 2, LAST)

        @block.tensor
        def _(pe):
            def turn(lead, ql, lag, qg):
                if lead is not None:
                    pe.wait_ge(s["xn"], lead + 1)
                    if later(lead):
                        pe.wait_ge(s["xt"], lead - 1)
                    for half in range(2):
                        last = pe.transpose(ps_x[ql][:, half * P:half * P + P], xn[:, ql, half * P:half * P + P], m.ident[:, :])
                    last.then_inc(s["xtps"], 1)
                if lag is not None:
                    pe.wait_ge(s["xt"], lag + 1)
                    if later(lag):
                        pe.wait_ge(s["rest"], lag - 1)
                        pe.wait_ge(s["xl"], lag - 1)
                        pe.wait_ge(s["max"], lag - 1)
                    for side, bank, done in ((1, ps_r, "right"), (0, ps_l, "left")):
                        for half in range(2):
                            last = pe.matmul(bank[qg][:, 0:ROW], xnt[:, qg, half * P:half * P + P], m.w_lr[:, half, side, :],
                                             start=(half == 0), stop=(half == 1))
                        last.then_inc(s[done], 1)
                    for out in range(2):
                        for half in range(2):
                            last = pe.matmul(ps_k[qg][:, out * P:out * P + P], m.w_k[:, half, out * P:out * P + P],
                                             xnt[:, qg, half * P:half * P + P], start=(half == 0), stop=(half == 1))
                    last.then_inc(s["keysps"], 1)
            skewed(pe, turn)

        @block.scalar
        def _(act):
            def turn(lead, ql, lag, qg):
                if lead is not None:
                    act.wait_ge(s["xtps"], lead + 1)
                    if later(lead):
                        act.wait_ge(s["keysps"], lead - 1)
                        act.wait_ge(s["kept"], lead - 1)
                    act.copy(xnt[:, ql, :], ps_x[ql][:, 0:DIM]).then_inc(s["xt"], 1)
                    act.wait_ge(s["xn"], lead + 1)
                    act.copy(m.xn[:, bass.ds(lead, 1), 0:DIM].rearrange("p t c -> p (t c)"), xn[:, ql, :]).then_inc(s["xn_kept"], 1)
                    act.wait_ge(s["xt"], lead + 1)
                    act.copy(m.xnt[:, bass.ds(lead, 1), :].rearrange("p t c -> p (t c)"), xnt[:, ql, :]).then_inc(s["kept"], 1)
                if lag is not None:
                    act.wait_ge(s["right"], lag + 1)
                    if later(lag):
                        act.wait_ge(s["stored_r"][qg], uses(lag, qg) * 16)
                        act.wait_ge(s["stored_l"][qg], uses(lag, qg) * 16)
                    act.copy(xr3[:, qg, 0:ROW], ps_r[qg][:, 0:ROW]).then_inc(s["hi"], 1)
                    act.wait_ge(s["left"], lag + 1)
                    act.copy(xl[:, qg, :], ps_l[qg][:, 0:ROW]).then_inc(s["xl"], 1)
                    act.wait_ge(s["xl"], lag + 1)
                    settle(act, m)
                    act.dma_start(m.d_xl[bass.ds(lag * P, P), :], xl[:, qg, :]).then_inc(s["stored_l"][qg], 16)
            skewed(act, turn)


def lambdas(nc, ctx, m, a):
    sb = lambda name, shape, dt=F32: ctx.enter_context(nc.sbuf_tensor(name, shape, dt))
    s = sem_set(nc, m.sems, "lam", "limit cntps step stepps top shiftps shift xt keysps e ctxps ctx turnedps turned chain lam var rstd wqps wq bn mixps mix")
    mx = sb("l_mx", [P, 2])
    shift = sb("l_shift", [1, DIM])
    xnt = sb("l_xnt", [P, 2, DIM])
    e = sb("l_e", [P, 2, DIM])
    ctxt = sb("l_ctxt", [P, 2, DIM + 1])
    acc = sb("l_acc", [P, 2, DIM])
    rz = sb("l_rz", [P, 2])
    lam = sb("l_lam", [P, 2, DIM])
    bn = sb("l_bn", [P, 2, DIM])
    bv, bk_row, cols = m.bv, m.bk_row, m.cols
    st = sb("l_st", [P, 2, 6])
    mv = sb("l_mv", [P, 2, 2])
    ve = sb("l_ve", [P, 2])
    rs = sb("l_rs", [P, 2])
    sc = sb("l_sc", [P, 2])
    neghalf = sb("l_neghalf", [P, 2])
    wqt = sb("l_wqt", [P, 2, DIM])
    junk = sb("l_junk", [P, 2, ECOLS])
    limit = sb("l_limit", [TILES - 1, STEPS], I32)
    limitf = sb("l_limitf", [TILES - 1, STEPS])
    below = sb("l_below", [P, TILES - 1])
    cnt = sb("l_cnt", [TILES - 1, 1])
    passed = sb("l_passed", [TILES - 1, STEPS])

    with nc.Block() as block:
        @block.sync
        def _(sp):
            sp.wait_ge(m.prepared, m.edges_stored)

        @block.scalar
        def _(act):
            def tile(n, q):
                act.wait_ge(s["keysps"], n + 1)
                if later(n):
                    act.wait_ge(s["ctxps"], n - 1)
                act.activation(e[:, q, :], m.bank[q][:, 0:DIM], ACT.Exp).then_inc(s["e"], 1)
            over_tiles(act, tile)

        @block.gpsimd
        def _(pool):
            pool.iota(limit[:, :], [[EDGES_STEP, STEPS]], base=0, channel_multiplier=-EDGES_STEP).then_inc(s["limit"], 1)

            def tile(n, q):
                if later(n):
                    pool.wait_ge(s["keysps"], n - 1)
                pool.tensor_copy(xnt[:, q, :], m.xnt[:, bass.ds(n, 1), :].rearrange("p t c -> p (t c)")).then_inc(s["xt"], 1)
            over_tiles(pool, tile)
            pool.memset(neghalf[:, :], -0.5).then_inc(s["rstd"], 1)
            pool.wait_ge(s["rstd"], 1)
            pool.wait_ge(s["var"], 1)
            rstd_pool(pool, rs[:, :], ve[:, :], neghalf[:, :]).then_inc(s["rstd"], 1)

        @block.vector
        def _(dve):
            ch = Chain(dve, s["chain"], 0)
            ch.step(dve.tensor_reduce(mx[:, :], m.key_max[:, :, :], AX.X, ALU.max))
            dve.wait_ge(m.constants, CONSTANTS)
            dve.tensor_tensor(mx[:, :], mx[:, :], cols[:, :, 3], ALU.add).then_inc(s["top"], 1)
            dve.wait_ge(s["shiftps"], 1)
            dve.tensor_tensor(shift[:, :], bk_row[:, :], m.bank[5][0:1, 0:DIM], ALU.subtract).then_inc(s["shift"], 1)
            dve.wait_ge(s["wqps"], 1)
            dve.tensor_copy(wqt[:, :, :].rearrange("p h d -> p (h d)"), m.bank[6][:, :]).then_inc(s["wq"], 1)

            for t in range(1, TILES):
                if t > 2:
                    dve.wait_ge(s["chain"], ch.n - 1)
                ch.n += 1
                dve.tensor_scalar(junk[:, t % 2, :], m.dstf[:, :], float(P * t), 0.0, ALU.is_lt, ALU.add,
                                  accum_out=below[:, t - 1:t]).then_inc(s["chain"], 1)
            dve.wait_ge(s["limit"], 1)
            ch.step(dve.tensor_copy(limitf[:, :], limit[:, :]))
            dve.wait_ge(s["cntps"], 1)
            ch.step(dve.tensor_copy(cnt[:, :], m.bank[4][0:TILES - 1, 0:1]))
            dve.tensor_scalar(passed[:, :], limitf[:, :], cnt[:, 0:1], None, ALU.is_gt).then_inc(s["step"], 1)
            dve.wait_ge(s["stepps"], 1)
            dve.tensor_copy(m.window[:, :], m.bank[5][0:1, 0:STEPS]).then_inc(s["step"], 1)
            dve.scalar_tensor_tensor(out=m.start[:, :], in0=m.bank[5][0:1, 0:STEPS], scalar=-float(EDGES_STEP),
                                     in1=limitf[0:1, :], op0=ALU.mult, op1=ALU.add).then_inc(s["step"], 1)

            dve.wait_ge(s["ctxps"], TILES)
            for half in range(2):
                dve.tensor_copy(ctxt[:, half, :], m.bank[2 + half][:, 0:DIM + 1]).then_inc(s["ctx"], 1)
            dve.wait_ge(s["ctx"], 2)
            ch.step(dve.reciprocal(rz[:, :], ctxt[:, :, DIM]))
            dve.wait_ge(s["turnedps"], 1)
            dve.tensor_copy(acc[:, :, :].rearrange("p h d -> p (h d)"), m.bank[7][:, :]).then_inc(s["turned"], 1)
            dve.wait_ge(s["lam"], 1)
            for half in range(2):
                ch.step(dve.scalar_tensor_tensor(out=lam[:, half, :], in0=m.bank[half][:, 0:DIM],
                                                 scalar=rz[:, half:half + 1], in1=bv[:, :], op0=ALU.mult, op1=ALU.add))
                ch.step(dve.bn_stats(st[:, half, :], lam[:, half, :]), settled=m)
                ch.step(dve.bn_aggr(mv[:, half, :], st[:, half, :]))
            dve.tensor_scalar(ve[:, :], mv[:, :, 1], LN_EPS, None, ALU.add).then_inc(s["var"], 1)
            dve.wait_ge(s["rstd"], 2)
            ch.step(dve.tensor_tensor(sc[:, :], rs[:, :], cols[:, :, 0], ALU.mult))
            for half in range(2):
                ch.step(dve.tensor_scalar(lam[:, half, :], lam[:, half, :], mv[:, half, 0:1], sc[:, half:half + 1],
                                          ALU.subtract, ALU.mult))
                dve.tensor_scalar(bn[:, half, :], lam[:, half, :], cols[:, half, 1:2], None, ALU.add).then_inc(s["bn"], 1)
            dve.wait_ge(s["mixps"], 1)
            for half in range(2):
                dve.tensor_copy(m.w_mix[:, half, :], m.bank[2 + half][:, 0:DIM]).then_inc(s["mix"], 1)
            dve.tensor_copy(m.b_mix[:, :], m.bank[4][0:1, 0:DIM]).then_inc(s["mix"], 1)

        @block.tensor
        def _(pe):
            for half in range(2):
                for inn in range(2):
                    last = pe.transpose(m.bank[6][:, half * DIM + inn * P:half * DIM + inn * P + P],
                                        m.w_q[:, inn, half * P:half * P + P], m.ident[:, :])
            last.then_inc(s["wqps"], 1)
            pe.wait_ge(s["top"], 1)
            for half in range(2):
                last = pe.matmul(m.bank[5][0:1, half * P:half * P + P], mx[:, half:half + 1], m.ident[:, :], start=True, stop=True)
            last.then_inc(s["shiftps"], 1)
            pe.wait_ge(s["shift"], 1)

            def turn(lead, ql, lag, qg):
                if lead is not None:
                    pe.wait_ge(s["xt"], lead + 1)
                    if later(lead):
                        pe.wait_ge(s["e"], lead - 1)
                    for half in range(2):
                        pe.matmul(m.bank[ql][:, 0:DIM], xnt[:, ql, half * P:half * P + P], m.w_k[:, half, :], start=(half == 0), stop=False)
                    pe.matmul(m.bank[ql][:, 0:DIM], m.ones[0:1, :], shift[:, :], start=False, stop=True).then_inc(s["keysps"], 1)
                if lag is not None:
                    pe.wait_ge(s["e"], lag + 1)
                    for half in range(2):
                        last = pe.matmul(m.bank[2 + half][:, 0:DIM + 1], e[:, qg, half * P:half * P + P],
                                         m.xn[:, bass.ds(lag, 1), :].rearrange("p t c -> p (t c)"),
                                         start=isinstance(lag, int) and lag == 0, stop=isinstance(lag, int) and lag == TILES - 1)
                    last.then_inc(s["ctxps"], 1)
            skewed(pe, turn)
            pe.wait_ge(s["chain"], 1 + TILES - 1)
            pe.matmul(m.bank[4][0:TILES - 1, 0:1], below[:, :], m.ones[:, 0:1], start=True, stop=True).then_inc(s["cntps"], 1)
            pe.wait_ge(s["step"], 1)
            pe.matmul(m.bank[5][0:1, 0:STEPS], m.ones[0:TILES - 1, 0:1], passed[:, :], start=True, stop=True).then_inc(s["stepps"], 1)
            pe.wait_ge(s["ctx"], 2)
            for inn in range(2):
                for half in range(2):
                    last = pe.transpose(m.bank[7][:, inn * DIM + half * P:inn * DIM + half * P + P],
                                        ctxt[:, half, inn * P:inn * P + P], m.ident[:, :])
            last.then_inc(s["turnedps"], 1)
            pe.wait_ge(s["turned"], 1)
            for half in range(2):
                for inn in range(2):
                    last = pe.matmul(m.bank[half][:, 0:DIM], acc[:, inn, half * P:half * P + P], m.w_v[:, inn, :],
                                     start=(inn == 0), stop=(inn == 1))
            last.then_inc(s["lam"], 1)
            pe.wait_ge(s["bn"], 2)
            pe.wait_ge(s["wq"], 1)
            for inn in range(2):
                for half in range(2):
                    pe.matmul(m.bank[2 + inn][:, 0:DIM], wqt[:, half, inn * P:inn * P + P], bn[:, half, :],
                              start=(half == 0), stop=(half == 1))
            for half in range(2):
                last = pe.matmul(m.bank[4][0:1, 0:DIM], cols[:, half, 2:3], bn[:, half, :], start=(half == 0), stop=(half == 1))
            last.then_inc(s["mixps"], 1)


def attend(nc, ctx, m, a):
    sb = lambda name, shape, dt=F32: ctx.enter_context(nc.sbuf_tensor(name, shape, dt))
    s = sem_set(nc, m.sems, "att", "init sel drel selt relu score_e lin gate carry scoreps score scoret run scan mps diff rr rd rps p ex agg f fac facs old acc stored*")
    loaded = [m.sems.enter_context(nc.semaphore(f"att_loaded{r}")) for r in range(RING)]
    gathered = [m.sems.enter_context(nc.semaphore(f"att_gathered{r}")) for r in range(RING)]
    idx = [sb(f"e_idx{r}", [P, G], I32) for r in range(RING)]
    dcol = sb("e_dcol", [P, RING, G])
    drow = sb("e_drow", [P, RING, EDGES_STEP], I16)
    pen = sb("e_pen", [HEADS, RING, EDGES_STEP + 1])
    xr3 = sb("e_xr3", [P, RING, ROW3], BF16)
    xl = [sb(f"e_xl{r}", [P, G, ROW]) for r in range(RING)]
    drel = sb("e_drel", [P, G], BF16)
    sel = sb("e_sel", [P, 2, EDGES_STEP], BF16)
    selt = sb("e_selt", [P, RING, G, P])
    first = sb("e_first", [P, RING])
    same = sb("e_same", [P, RING])
    gate = sb("e_gate", [HEADS, 1])
    carry = sb("e_carry", [HEADS, 1])
    relu = sb("e_relu", [P, 2, EDGES_STEP])
    score = sb("e_score", [P, 2, G, HEADS])
    lin = sb("e_lin", [P, G, HEADS])
    run = sb("e_run", [HEADS, EDGES_STEP])
    top = sb("e_top", [HEADS, 2, EDGES_STEP])
    drop = sb("e_drop", [HEADS, 2])
    rr = sb("e_rr", [HEADS, 2])
    rd = sb("e_rd", [HEADS, 2, HEADS])
    diff = sb("e_diff", [P, G, HEADS])
    prod = sb("e_prod", [P, 2, G, HEADS, HCOLS])
    fac = sb("e_fac", [P, HEADS])
    facs = sb("e_facs", [P, HEADS])
    old = sb("e_old", [P, HEADS, HCOLS])
    acc = sb("e_acc", [P, 2, HEADS, HCOLS])

    ps_e = [m.bank[0], m.bank[1]]
    ps_score = m.bank[2][:, 0:G * 5 * HEADS].rearrange("p (g i h) -> p g i h", g=G, i=5)
    ps_scoret = m.bank[3][0:HEADS, :]
    ps_top = m.bank[4][:, 0:G * HEADS]
    ps_ex = m.bank[5][:, 0:G * HEADS]
    ps_r = m.bank[6][:, 0:HEADS]
    ps_agg = m.bank[7][:, 0:HEADS * HCOLS]
    LOADS = 5 * 16
    TURNS = STEPS // RING
    assert STEPS % RING == 0

    def since(k, first_step):
        return not isinstance(k, int) or k >= first_step

    def is_step(k):
        return not isinstance(k, int) or 0 <= k < STEPS

    def over_steps(eng, body, head=1, behind=0):
        for k in range(head * RING):
            body(k, k % RING, k // RING)
        with eng.Fori(head, TURNS - 1) as it:
            for j in range(RING):
                body(it * RING + j, j, it)
        for k in range(STEPS - RING, STEPS + behind):
            body(k, k % RING, k // RING)

    with nc.Block() as block:
        @block.sync
        def _(sp):
            def store(k, q, uses):
                sp.wait_ge(s["acc"], k + 1)
                if since(k, 1):
                    sp.wait_ge(s["stored"][1 - q], 16 * (uses + q))
                    settle(sp, m)
                t = sp.value_load(m.window[0:1, bass.ds(k, 1)], min_val=0, max_val=TILES - 1)
                sp.dma_start(m.d_acc[bass.ds(t * P, P), :], acc[:, q, :, :].rearrange("p h c -> p (h c)")).then_inc(s["stored"][q], 16)

            def load(k, r, turn):
                if since(k, RING):
                    sp.wait_ge(gathered[r], turn * 64)
                    settle(sp, m)
                    sp.wait_ge(s["scoreps"], k - RING + 1)
                    sp.wait_ge(s["scan"], k - RING + 1)
                    settle(sp, m)
                t = sp.value_load(m.window[0:1, bass.ds(k, 1)], min_val=0, max_val=TILES - 1)
                block_at = sp.value_load(m.start[0:1, bass.ds(k, 1)], min_val=0, max_val=EDGES_PAD - EDGES_STEP)
                edges = bass.ds(block_at, EDGES_STEP)
                sp.dma_start(idx[r][:, :], m.d_src[edges].rearrange("(p g) -> p g", g=G)).then_inc(loaded[r], 16)
                sp.dma_start(dcol[:, r, :], m.d_dst[edges].rearrange("(p g) -> p g", g=G)).then_inc(loaded[r], 16)
                sp.dma_start(drow[:, r, :], m.d_dst16[edges].partition_broadcast(P)).then_inc(loaded[r], 16)
                sp.dma_start(pen[:, r, :], m.d_pen[bass.ds(block_at, EDGES_STEP + 1)].partition_broadcast(HEADS)).then_inc(loaded[r], 16)
                sp.dma_start(xr3[:, r, :], m.d_xr[bass.ds(t * P, P), :]).then_inc(loaded[r], 16)

            def step(k, r, turn):
                if is_step(k):
                    load(k, r, turn)
                if since(k, RING):
                    store(k - RING, r % 2, (turn - 1) * (RING // 2) + r // 2)
            over_steps(sp, step, head=2, behind=RING)
            for q in range(2):
                sp.wait_ge(s["stored"][q], 16 * (STEPS // 2))

        @block.gpsimd
        def _(pool):
            pool.memset(acc[:, :, :, :], 0.0).then_inc(s["init"], 1)
            pool.memset(top[:, :, :], -BIG).then_inc(s["init"], 1)

            def gather(k, r, turn):
                pool.wait_ge(loaded[r], (turn + 1) * LOADS)
                if since(k, RING):
                    pool.wait_ge(s["p"], k - RING + 1)
                settle(pool, m)
                for g in range(G):
                    pool.indirect_dma_start(xl[r][:, g, :], None, m.d_xl, bass.IndirectOffsetOnAxis(
                        ap=idx[r][:, g:g + 1], axis=0)).then_inc(gathered[r], 16)
            over_steps(pool, gather)

        @block.vector
        def _(dve):
            dve.wait_ge(s["init"], 2)

            def select(k, r, turn):
                q, before = r % 2, (r - 1) % RING
                dve.wait_ge(loaded[r], (turn + 1) * LOADS)
                number = xr3[:, r, 3 * ROW:3 * ROW + 2].bitcast(F32)
                start = xr3[:, r, 3 * ROW + 2:ROW3].bitcast(F32)
                start_before = xr3[:, before, 3 * ROW + 2:ROW3].bitcast(F32)
                dve.tensor_scalar(sel[:, q, :], drow[:, r, :], number, None, ALU.is_equal).then_inc(s["sel"], 1)
                if since(k, 1):
                    dve.wait_ge(s["selt"], k)
                dve.tensor_scalar(drel[:, :], dcol[:, r, :], start, None, ALU.subtract).then_inc(s["drel"], 1)
                dve.tensor_scalar(first[:, r:r + 1], drow[:, r, 0:1], number, None, ALU.is_equal)
                if since(k, 1):
                    dve.tensor_scalar(same[:, r:r + 1], start, start_before, None, ALU.is_equal)
                else:
                    dve.memset(same[:, r:r + 1], 0.0)
                dve.wait_ge(s["drel"], k + 1)
                dve.tensor_tensor(selt[:, r, :, :], m.lane_row[:, :].unsqueeze(1).to_broadcast([P, G, P]),
                                  drel[:, :].unsqueeze(2).to_broadcast([P, G, P]), ALU.is_equal).then_inc(s["selt"], 1)

            def close_score(k, r, turn):
                q = r % 2
                dve.wait_ge(s["scoreps"], k + 1)
                dve.wait_ge(gathered[r], (turn + 1) * 64)
                if since(k, 1):
                    dve.wait_ge(s["score"], k)
                    dve.wait_ge(s["f"], k)
                dve.tensor_reduce(lin[:, :, :], ps_score.rearrange("p g i h -> p g h i"), AX.X, ALU.add).then_inc(s["lin"], 1)
                dve.tensor_scalar(gate[:, :], same[0:HEADS, r:r + 1], -1.0, BIG, ALU.add, ALU.mult).then_inc(s["gate"], 1)
                dve.wait_ge(s["lin"], k + 1)
                dve.tensor_tensor(score[:, q, :, :], lin[:, :, :], xl[r][:, :, DIM:ROW], ALU.add).then_inc(s["score"], 1)
                dve.wait_ge(s["gate"], k + 1)
                dve.tensor_tensor(carry[:, :], top[:, 1 - q, EDGES_STEP - 1:EDGES_STEP], gate[:, :], ALU.add).then_inc(s["carry"], 1)

            def forward_scan(k, r):
                dve.wait_ge(s["scoret"], k + 1)
                dve.wait_ge(s["carry"], k + 1)
                if since(k, 1):
                    dve.wait_ge(s["scan"], k)
                dve.tensor_tensor_scan(run[:, :], pen[:, r, 0:EDGES_STEP], ps_scoret, carry[:, 0:1], ALU.add, ALU.max).then_inc(s["run"], 1)

            def backward_scan(k, r):
                back = slice(None, None, -1)
                dve.wait_ge(s["run"], k + 1)
                dve.tensor_tensor_scan(top[:, r % 2, back], pen[:, r, 1:EDGES_STEP + 1][:, back], run[:, back], -BIG,
                                       ALU.add, ALU.max).then_inc(s["scan"], 1)

            def open_drop(k, q):
                dve.wait_ge(s["scan"], k + 1)
                dve.tensor_scalar(drop[:, q:q + 1], carry[:, :], top[:, q, 0:1], 0.0, ALU.subtract, ALU.min).then_inc(s["f"], 1)

            def less_top(k, q):
                dve.wait_ge(s["mps"], k + 1)
                dve.tensor_tensor(diff[:, :, :], score[:, q, :, :], ps_top.rearrange("p (g h) -> p g h", g=G),
                                  ALU.subtract).then_inc(s["diff"], 1)

            def weigh(k, r):
                q = r % 2
                dve.wait_ge(s["ex"], k + 1)
                ex = ps_ex.rearrange("p (g h) -> p g h", g=G)
                dve.tensor_copy(prod[:, q, :, :, HEAD:HCOLS], ex.unsqueeze(3))
                dve.tensor_tensor(prod[:, q, :, :, 0:HEAD], xl[r][:, :, 0:DIM].rearrange("p g (h c) -> p g h c", h=HEADS),
                                  ex.unsqueeze(3).to_broadcast([P, G, HEADS, HEAD]), ALU.mult).then_inc(s["p"], 1)

            def factor(k, r):
                dve.wait_ge(s["rps"], k + 1)
                if since(k, 1):
                    dve.wait_ge(s["facs"], k)
                dve.tensor_scalar(fac[:, :], ps_r, -1.0, first[:, r:r + 1], ALU.add, ALU.mult).then_inc(s["fac"], 1)

            def window_factor(k, r):
                dve.wait_ge(s["fac"], k + 1)
                if since(k, 1):
                    dve.wait_ge(s["old"], k)
                dve.tensor_scalar(facs[:, :], fac[:, :], 1.0, same[:, r:r + 1], ALU.add, ALU.mult).then_inc(s["facs"], 1)

            def rescaled(k, q):
                dve.wait_ge(s["facs"], k + 1)
                if since(k, 1):
                    dve.wait_ge(s["acc"], k)
                dve.tensor_tensor(old[:, :, :], acc[:, 1 - q, :, :],
                                  facs[:, :].unsqueeze(2).to_broadcast([P, HEADS, HCOLS]), ALU.mult).then_inc(s["old"], 1)

            def add_sums(k, q, uses):
                dve.wait_ge(s["old"], k + 1)
                dve.wait_ge(s["agg"], k + 1)
                if since(k, 2):
                    dve.wait_ge(s["stored"][q], 16 * uses)
                dve.tensor_tensor(acc[:, q, :, :], old[:, :, :], ps_agg.rearrange("p (h c) -> p h c", h=HEADS),
                                  ALU.add).then_inc(s["acc"], 1)

            def step(k, r, turn):
                before, two_before = (r - 1) % RING, (r - 2) % RING
                maxima = since(k, 1) and is_step(k - 1)
                closing = since(k, 2)
                if maxima:
                    close_score(k - 1, before, turn if r >= 1 else turn - 1)
                if is_step(k + 1):
                    select(k + 1, (r + 1) % RING, turn if r + 1 < RING else turn + 1)
                if maxima:
                    forward_scan(k - 1, before)
                if closing:
                    factor(k - 2, two_before)
                if maxima:
                    backward_scan(k - 1, before)
                if closing:
                    window_factor(k - 2, two_before)
                if maxima:
                    open_drop(k - 1, before % 2)
                if closing:
                    rescaled(k - 2, two_before % 2)
                if maxima:
                    less_top(k - 1, before % 2)
                if closing:
                    add_sums(k - 2, two_before % 2, turn * (RING // 2) + (r - 2) // 2)
                if maxima:
                    weigh(k - 1, before)
            select(0, 0, 0)
            over_steps(dve, step, behind=2)

        @block.tensor
        def _(pe):
            def edge_features(k, r, turn, half):
                q = r % 2
                if half == 0:
                    pe.wait_ge(gathered[r], (turn + 1) * 64)
                if since(k, 1):
                    pe.wait_ge(s["relu"], 2 * k - 1 + half)

                for g in range(G):
                    pe.matmul(ps_e[half][:, g::G], xl[r][:, g, half * P:half * P + P], m.ident[:, :], is_transpose=True,
                              start=(g == 0), stop=False)
                if half == 0:
                    pe.wait_ge(s["sel"], k + 1)
                elif since(k, 1):
                    tops(k - 1, 1 - q)
                for part in range(3):
                    at = part * ROW + half * P
                    last = pe.matmul(ps_e[half][:, :], xr3[:, r, at:at + P], sel[:, q, :], start=False, stop=(part == 2))
                last.then_inc(s["score_e"], 1)

            def tops(k, q):
                pe.wait_ge(s["scan"], k + 1)
                if since(k, 1):
                    pe.wait_ge(s["diff"], k)
                settle(pe, m)
                for g in range(G):
                    last = pe.transpose(ps_top[:, g * HEADS:(g + 1) * HEADS], top[:, q, g::G], m.ident[0:HEADS, 0:HEADS])
                last.then_inc(s["mps"], 1)

            def linear_scores(k, r):
                if since(k, 1):
                    pe.wait_ge(s["score"], k)
                parts = xr3[:, r, 0:3 * ROW].rearrange("p (i c) -> p i c", i=3)[:, :, DIM:ROW]
                for g in range(G):
                    pe.matmul(ps_score[:, g, 0:3, :], sel[:, r % 2, g::G], parts, start=True, stop=True)

            def scores(k, half):
                pe.wait_ge(s["relu"], 2 * k + 1 + half)
                for g in range(G):
                    last = pe.matmul(ps_score[:, g, 3 + half, :], relu[:, half, g::G], m.att_col[:, half, :], start=True, stop=True)
                if half == 1:
                    last.then_inc(s["scoreps"], 1)

            def score_rows(k, q):
                pe.wait_ge(s["score"], k + 1)
                if since(k, 1):
                    pe.wait_ge(s["scan"], k)
                for g in range(G):
                    last = pe.transpose(ps_scoret[:, g::G], score[:, q, g, :], m.ident[:, :])
                last.then_inc(s["scoret"], 1)

            def sums(k, r):
                q = r % 2
                pe.wait_ge(s["rd"], k + 1)
                pe.wait_ge(s["selt"], k + 1)
                if since(k, 1):
                    pe.wait_ge(s["acc"], k)
                pe.matmul(ps_r, m.ones[0:HEADS, :], rd[:, q, :], start=True, stop=True).then_inc(s["rps"], 1)
                pe.wait_ge(s["p"], k + 1)
                for g in range(G):
                    last = pe.matmul(ps_agg, selt[:, r, g, :], prod[:, q, g, :, :].rearrange("p h c -> p (h c)"),
                                     start=(g == 0), stop=(g == G - 1))
                last.then_inc(s["agg"], 1)

            def step(k, r, turn):
                if is_step(k):
                    edge_features(k, r, turn, 0)
                if since(k, 1) and is_step(k - 1):
                    score_rows(k - 1, 1 - r % 2)
                if since(k, 2):
                    sums(k - 2, (r - 2) % RING)
                if is_step(k):
                    edge_features(k, r, turn, 1)
                    linear_scores(k, r)
                    scores(k, 0)
                    scores(k, 1)
                elif is_step(k - 1):
                    tops(k - 1, 1 - r % 2)
            over_steps(pe, step, behind=2)

        @block.scalar
        def _(act):
            def rescale(k, q):
                act.wait_ge(s["f"], k + 1)
                act.activation(rr[:, q:q + 1], drop[:, q:q + 1], ACT.Exp).then_inc(s["rr"], 1)
                act.wait_ge(s["rr"], k + 1)
                if since(k, 2):
                    act.wait_ge(s["rps"], k - 1)
                act.activation(rd[:, q, :], m.ident[0:HEADS, 0:HEADS], ACT.Copy, scale=rr[:, q:q + 1]).then_inc(s["rd"], 1)

            def relus(k, half):
                act.wait_ge(s["score_e"], 2 * k + 1 + half)
                if since(k, 1):
                    act.wait_ge(s["scoreps"], k)
                act.activation(relu[:, half, :], ps_e[half][:, :], ACT.Relu).then_inc(s["relu"], 1)

            def weights(k):
                act.wait_ge(s["diff"], k + 1)
                if since(k, 1):
                    act.wait_ge(s["p"], k)
                act.activation(ps_ex, diff[:, :, :].rearrange("p g h -> p (g h)"), ACT.Exp).then_inc(s["ex"], 1)

            def step(k, r, turn):
                if is_step(k):
                    relus(k, 0)
                if since(k, 1):
                    rescale(k - 1, 1 - r % 2)
                    weights(k - 1)
                if is_step(k):
                    relus(k, 1)
            over_steps(act, step, behind=1)


def node_update(nc, ctx, m, a):
    sb = lambda name, shape, dt=F32: ctx.enter_context(nc.sbuf_tensor(name, shape, dt))
    s = sem_set(nc, m.sems, "upd", "init in* xt shifted mixps out neg_part low_e var1 var2 rstd1 rstd2 close_chain sum_chain aggr1 aggr2 x1 norm normps normt norm_kept logits gex gexed oh posps gate_chain places placed row")
    scattered = [m.sems.enter_context(nc.semaphore(f"upd_scattered{r}")) for r in range(4)]
    bias, gamma, beta, gate_w, gate_b = m.bias, m.gamma, m.beta, m.gate_w, m.gate_b
    xnt = sb("u_xnt", [P, 2, DIM])
    xb = sb("u_xb", [P, 2, DIM])
    acc = sb("u_acc", [P, 2, HEADS, HCOLS])
    den = sb("u_den", [P, HEADS])
    out = sb("u_out", [P, DIM])
    low = sb("u_low", [P, DIM])
    lowe = sb("u_lowe", [P, DIM])
    hid = sb("u_hid", [P, 2, DIM])
    st = sb("u_st", [P, 2, 6])
    mv1 = sb("u_mv1", [P, 2, 2])
    mv2 = sb("u_mv2", [P, 2])
    ve = sb("u_ve", [P, 2])
    rs = sb("u_rs", [P, 2])
    neghalf = sb("u_neghalf", [P, 1])
    norm = sb("u_norm", [P, 2, DIM])
    norms = sb("u_norms", [P, TILES, DIM])
    normt = sb("u_normt", [P, DIM])
    mx = sb("u_mx", [P, TILES])
    lg = sb("u_lg", [P, TILES, EXPERTS])
    ex = sb("u_ex", [P, TILES, EXPERTS])
    tot = sb("u_tot", [P, TILES])
    best = sb("u_best", [P, TILES])
    which = sb("u_which", [P, TILES])
    hot = sb("u_hot", [P, TILES, EXPERTS])
    total = sb("u_total", [P, EXPERTS, TILES])
    upto = sb("u_upto", [P, EXPERTS, TILES])
    go_on = sb("u_go_on", [P, EXPERTS, TILES])
    pos = sb("u_pos", [P, TILES, EXPERTS])
    posr = sb("u_posr", [P, TILES])
    kept = sb("u_kept", [P, TILES])
    at = sb("u_at", [P, TILES])
    trash = sb("u_trash", [P, TILES])
    place_all = sb("u_place_all", [P, TILES], I32)
    row = [sb(f"u_row{r}", [P, DIM]) for r in range(4)]
    place = [sb(f"u_place{r}", [P, 1], I32) for r in range(4)]
    ps_mix = [m.bank[0], m.bank[1]]
    ps_t = m.bank[2]
    ps_log = m.bank[3][:, 0:TILES * EXPERTS]
    ps_pos = m.bank[4][:, 0:TILES * EXPERTS]
    ps_tot = m.bank[5][:, 0:TILES * EXPERTS]
    CLOSE, SUM = 6, 4

    def tile_of(t, n):
        return t[:, bass.ds(n, 1), 0:DIM].rearrange("p t c -> p (t c)")

    def flat(t):
        return t[:, :, :].rearrange("p a b -> p (a b)")

    with nc.Block() as block:
        @block.sync
        def _(sp):
            def tile(n, q):
                if later(n):
                    sp.wait_ge(s["out"], n - 1)
                    settle(sp, m)
                sp.dma_start(acc[:, q, :, :].rearrange("p h c -> p (h c)"), m.d_acc[bass.ds(n * P, P), :]).then_inc(s["in"][q], 16)
            over_tiles(sp, tile)
            for e in range(2):
                load_expert(sp, m, a, e, e)

        @block.gpsimd
        def _(pool):
            pool.memset(neghalf[:, :], -0.5).then_inc(s["init"], 1)
            pool.memset(go_on[:, :, :], 1.0).then_inc(s["init"], 1)
            pool.wait_ge(s["init"], 2)
            pool.memset(go_on[:, :, 0:1], 0.0).then_inc(s["init"], 1)
            pool.wait_ge(m.constants, CONSTANTS)

            def turn(lead, ql, lag, qg):
                if lag is not None:
                    pool.wait_ge(s["var2"], lag + 1)
                    rstd_pool(pool, rs[:, 1:2], ve[:, 1:2], neghalf[:, :]).then_inc(s["rstd2"], 1)
                if lead is not None:
                    pool.wait_ge(s["var1"], lead + 1)
                    rstd_pool(pool, rs[:, 0:1], ve[:, 0:1], neghalf[:, :]).then_inc(s["rstd1"], 1)
                    if later(lead):
                        pool.wait_ge(s["x1"], lead - 1)
                    pool.tensor_tensor(xb[:, ql, :], tile_of(m.x, lead), beta[:, :], ALU.add).then_inc(s["shifted"], 1)
            skewed(pool, turn)
            pool.wait_ge(s["placed"], 1)

            def send(n, r):
                if not isinstance(n, int) or n >= 4:
                    pool.wait_ge(scattered[r], turns(n, r) * 16)
                pool.tensor_copy(place[r][:, :], place_all[:, bass.ds(n, 1)]).then_inc(s["places"], 1)
                pool.wait_ge(s["places"], n + 1)
                pool.wait_ge(s["row"], n + 1)
                settle(pool, m)
                pool.indirect_dma_start(m.d_in, bass.IndirectOffsetOnAxis(ap=place[r][:, 0:1], axis=0),
                                        row[r][:, :], None).then_inc(scattered[r], 16)
            over_fours(pool, send)
            for r in range(4):
                pool.wait_ge(scattered[r], 16 * (TILES // 4))

        @block.scalar
        def _(act):
            def turn(lead, ql, lag, qg):
                if lead is not None:
                    if later(lead):
                        act.wait_ge(s["mixps"], lead - 1)
                    act.copy(xnt[:, ql, :], tile_of(m.xnt, lead)).then_inc(s["xt"], 1)
                    act.wait_ge(s["out"], lead + 1)
                    act.activation(low[:, :], out[:, :], ACT.Relu, scale=-1.0).then_inc(s["neg_part"], 1)
                    act.wait_ge(s["neg_part"], lead + 1)
                    act.activation(lowe[:, :], low[:, :], ACT.Exp, scale=-1.0).then_inc(s["low_e"], 1)
                if lag is not None:
                    act.wait_ge(s["normps"], lag + 1)
                    if later(lag) or lag == 1:
                        act.wait_ge(s["logits"], lag)
                    act.copy(normt[:, :], ps_t[:, 0:DIM]).then_inc(s["normt"], 1)
                    act.copy(tile_of(norms, lag), norm[:, qg, :]).then_inc(s["norm_kept"], 1)
            skewed(act, turn)
            act.wait_ge(s["gex"], 1)
            act.activation(flat(ex), flat(lg), ACT.Exp).then_inc(s["gexed"], 1)
            act.wait_ge(s["norm_kept"], TILES)

            def send(n, r):
                if not isinstance(n, int) or n >= 4:
                    act.wait_ge(scattered[r], turns(n, r) * 16)
                act.copy(row[r][:, :], tile_of(norms, n)).then_inc(s["row"], 1)
            over_fours(act, send)

        @block.vector
        def _(dve):
            dve.wait_ge(m.constants, CONSTANTS)
            dve.wait_ge(s["init"], 3)
            heads = lambda t: t.rearrange("p (h c) -> p h c", h=HEADS)

            def turn(lead, ql, lag, qg):
                close = lead is not None and Chain(dve, s["close_chain"], lead * CLOSE)
                add = lag is not None and Chain(dve, s["sum_chain"], lag * SUM)
                if close:
                    dve.wait_ge(s["in"][ql], (uses(lead, ql) + 1) * 16)
                    if later(lead) or lead == 1:
                        dve.wait_ge(s["low_e"], lead)
                    dve.tensor_scalar(den[:, :], acc[:, ql, :, HEAD], 1e-16, None, ALU.add).then_inc(s["close_chain"], 1)
                if add:
                    dve.wait_ge(s["rstd1"], lag + 1)
                    dve.tensor_scalar(hid[:, qg, :], hid[:, qg, :], mv1[:, qg, 0:1], rs[:, 0:1], ALU.subtract, ALU.mult).then_inc(s["sum_chain"], 1)
                if close:
                    dve.wait_ge(s["close_chain"], lead * CLOSE + 1)
                    dve.reciprocal(den[:, :], den[:, :]).then_inc(s["close_chain"], 1)
                if add:
                    dve.wait_ge(s["sum_chain"], lag * SUM + 1)
                    dve.tensor_tensor(hid[:, qg, :], hid[:, qg, :], gamma[:, :], ALU.mult).then_inc(s["sum_chain"], 1)
                if close:
                    dve.wait_ge(s["close_chain"], lead * CLOSE + 2)
                    dve.tensor_tensor(heads(out[:, :]), acc[:, ql, :, 0:HEAD], den[:, :].unsqueeze(2).to_broadcast([P, HEADS, HEAD]), ALU.mult).then_inc(s["close_chain"], 1)
                if add:
                    dve.wait_ge(s["sum_chain"], lag * SUM + 2)
                    dve.wait_ge(s["shifted"], lag + 1)
                    dve.tensor_tensor(hid[:, qg, :], hid[:, qg, :], xb[:, qg, :], ALU.add).then_inc(s["sum_chain"], 1)
                if close:
                    dve.wait_ge(s["close_chain"], lead * CLOSE + 3)
                    dve.tensor_tensor(out[:, :], out[:, :], bias[:, :], ALU.add).then_inc(s["out"], 1)
                if add:
                    dve.wait_ge(s["sum_chain"], lag * SUM + 3)
                    dve.wait_ge(s["mixps"], lag + 1)
                    dve.tensor_tensor(tile_of(m.x, lag), hid[:, qg, :], ps_mix[qg][:, 0:DIM], ALU.add).then_inc(s["x1"], 1)
                    dve.wait_ge(s["x1"], lag + 1)
                    settle(dve, m)
                    dve.bn_stats(st[:, 1, :], tile_of(m.x, lag)).then_inc(s["sum_chain"], 1)
                    dve.wait_ge(s["sum_chain"], lag * SUM + 4)
                    settle(dve, m)
                    dve.bn_aggr(mv2[:, :], st[:, 1, :]).then_inc(s["aggr2"], 1)
                if close:
                    dve.wait_ge(s["low_e"], lead + 1)
                    dve.scalar_tensor_tensor(out=hid[:, ql, :], in0=out[:, :], scalar=0.0, in1=lowe[:, :], op0=ALU.max, op1=ALU.add).then_inc(s["close_chain"], 1)
                if add:
                    dve.wait_ge(s["aggr2"], lag + 1)
                    dve.tensor_scalar(ve[:, 1:2], mv2[:, 1:2], LN_EPS, None, ALU.add).then_inc(s["var2"], 1)
                if close:
                    dve.wait_ge(s["close_chain"], lead * CLOSE + 4)
                    dve.scalar_tensor_tensor(out=hid[:, ql, :], in0=hid[:, ql, :], scalar=-1.0, in1=tile_of(m.xn, lead), op0=ALU.add, op1=ALU.add).then_inc(s["close_chain"], 1)
                    dve.wait_ge(s["close_chain"], lead * CLOSE + 5)
                    settle(dve, m)
                    dve.bn_stats(st[:, 0, :], hid[:, ql, :]).then_inc(s["close_chain"], 1)
                if close:
                    dve.wait_ge(s["close_chain"], lead * CLOSE + 6)
                    settle(dve, m)
                    dve.bn_aggr(mv1[:, ql, :], st[:, 0, :]).then_inc(s["aggr1"], 1)
                    dve.wait_ge(s["aggr1"], lead + 1)
                    dve.tensor_scalar(ve[:, 0:1], mv1[:, ql, 1:2], LN_EPS, None, ALU.add).then_inc(s["var1"], 1)
                if add:
                    dve.wait_ge(s["rstd2"], lag + 1)
                    if later(lag):
                        dve.wait_ge(s["norm_kept"], lag - 1)
                        dve.wait_ge(s["normps"], lag - 1)
                    dve.tensor_scalar(norm[:, qg, :], tile_of(m.x, lag), mv2[:, 0:1], rs[:, 1:2], ALU.subtract, ALU.mult).then_inc(s["norm"], 1)
                if add:
                    dve.wait_ge(s["norm"], lag + 1)
            skewed(dve, turn)

            ch = Chain(dve, s["gate_chain"], 0)
            each = lambda t: t[:, :].unsqueeze(2).to_broadcast([P, TILES, EXPERTS])
            experts_row = m.expert_row[:, :].unsqueeze(1).to_broadcast([P, TILES, EXPERTS])
            by_tile = lambda t: t.rearrange("p (n e) -> p n e", n=TILES)
            dve.wait_ge(s["logits"], TILES)
            ch.step(dve.tensor_scalar(trash[:, :], m.tile_ids[:, :, 0], float(TRASH), None, ALU.add))
            ch.step(dve.tensor_reduce(mx[:, :], by_tile(ps_log), AX.X, ALU.max))
            dve.tensor_tensor(lg[:, :, :], by_tile(ps_log), each(mx), ALU.subtract).then_inc(s["gex"], 1)
            dve.wait_ge(s["gexed"], 1)
            ch.step(dve.tensor_reduce(tot[:, :], ex[:, :, :], AX.X, ALU.add))
            ch.step(dve.reciprocal(tot[:, :], tot[:, :]))
            ch.step(dve.tensor_tensor(ex[:, :, :], ex[:, :, :], each(tot), ALU.mult))
            ch.step(dve.tensor_reduce(best[:, :], ex[:, :, :], AX.X, ALU.max))
            ch.step(dve.tensor_tensor(ex[:, :, :], ex[:, :, :], each(best), ALU.is_lt))
            ch.step(dve.scalar_tensor_tensor(out=ex[:, :, :], in0=ex[:, :, :], scalar=100.0, in1=experts_row, op0=ALU.mult, op1=ALU.add))
            ch.step(dve.tensor_reduce(which[:, :], ex[:, :, :], AX.X, ALU.min))
            dve.tensor_tensor(hot[:, :, :], experts_row, each(which), ALU.is_equal).then_inc(s["oh"], 1)
            dve.wait_ge(s["posps"], 1)
            ch.step(dve.tensor_copy(total[:, :, :], ps_tot.rearrange("p (n e) -> p e n", n=TILES)))
            ch.step(dve.tensor_tensor_scan(flat(upto), flat(go_on), flat(total), 0.0, ALU.mult, ALU.add))
            ch.step(dve.tensor_tensor(upto[:, :, :], upto[:, :, :], total[:, :, :], ALU.subtract))
            ch.step(dve.tensor_tensor(pos[:, :, :], by_tile(ps_pos), upto[:, :, :].rearrange("p e n -> p n e"), ALU.add))
            ch.step(dve.tensor_tensor(pos[:, :, :], pos[:, :, :], hot[:, :, :], ALU.mult))
            ch.step(dve.tensor_reduce(posr[:, :], pos[:, :, :], AX.X, ALU.add))
            ch.step(dve.tensor_scalar(kept[:, :], posr[:, :], float(CAP), None, ALU.is_le))
            ch.step(dve.tensor_scalar(at[:, :], posr[:, :], float(CAP), -1.0, ALU.min, ALU.add))
            ch.step(dve.scalar_tensor_tensor(out=at[:, :], in0=which[:, :], scalar=float(CAP), in1=at[:, :], op0=ALU.mult, op1=ALU.add))
            ch.step(dve.tensor_copy(m.slot[:, :], at[:, :]))
            dve.tensor_tensor(m.share[:, :], best[:, :], kept[:, :], ALU.mult)
            ch.step(dve.tensor_tensor(at[:, :], at[:, :], trash[:, :], ALU.subtract))
            ch.step(dve.tensor_tensor(at[:, :], at[:, :], kept[:, :], ALU.mult))
            dve.tensor_tensor(place_all[:, :], at[:, :], trash[:, :], ALU.add).then_inc(s["placed"], 1)

        @block.tensor
        def _(pe):
            pe.wait_ge(m.constants, CONSTANTS)

            def turn(lead, ql, lag, qg):
                if lead is not None:
                    pe.wait_ge(s["xt"], lead + 1)
                    if later(lead):
                        pe.wait_ge(s["x1"], lead - 1)
                    for half in range(2):
                        pe.matmul(ps_mix[ql][:, 0:DIM], xnt[:, ql, half * P:half * P + P], m.w_mix[:, half, :], start=(half == 0), stop=False)
                    pe.matmul(ps_mix[ql][:, 0:DIM], m.ones[0:1, :], m.b_mix[:, :], start=False, stop=True).then_inc(s["mixps"], 1)
                if lag is not None:
                    pe.wait_ge(s["norm"], lag + 1)
                    if later(lag) or lag == 1:
                        pe.wait_ge(s["normt"], lag)
                    for half in range(2):
                        last = pe.transpose(ps_t[:, half * P:half * P + P], norm[:, qg, half * P:half * P + P], m.ident[:, :])
                    last.then_inc(s["normps"], 1)
                    pe.wait_ge(s["normt"], lag + 1)
                    log = ps_log[:, bass.ds(lag * EXPERTS, EXPERTS)]
                    for half in range(2):
                        pe.matmul(log, normt[:, half * P:half * P + P], gate_w[:, half, :], start=(half == 0), stop=False)
                    pe.matmul(log, m.ones[0:1, :], gate_b[:, :], start=False, stop=True).then_inc(s["logits"], 1)
            skewed(pe, turn)
            pe.wait_ge(s["oh"], 1)
            pe.matmul(ps_pos, m.tri[:, :], flat(hot), start=True, stop=True)
            pe.matmul(ps_tot, m.ones[:, :], flat(hot), start=True, stop=True).then_inc(s["posps"], 1)


def load_expert(sp, m, a, e, q):
    one = bass.ds(e, 1)
    sp.dma_start(m.w1[:, q, :, :], a.w1[one].rearrange("e (c p) f -> p (e c) f", p=P)).then_inc(m.weights_in[q], 16)
    sp.dma_start(m.w2[:, q, :, :], a.w2[one].rearrange("e (c p) d -> p (e c) d", p=P)).then_inc(m.weights_in[q], 16)
    sp.dma_start(m.b1[:, q, :], a.b1[one].rearrange("e (c p) -> p (e c)", p=P), allow_slow_non_contiguous=True).then_inc(m.weights_in[q], 16)
    sp.dma_start(m.b2[:, q, :], a.b2[one].rearrange("e (c p) -> p (e c)", p=P), allow_slow_non_contiguous=True).then_inc(m.weights_in[q], 16)


def experts(nc, ctx, m, a):
    sb = lambda name, shape, dt=F32: ctx.enter_context(nc.sbuf_tensor(name, shape, dt))
    s = sem_set(nc, m.sems, "exp", "rows* rowst rowsb up hid down y yt yb stored*")
    w1, w2, b1, b2 = m.w1, m.w2, m.b1, m.b2
    rows = sb("f_rows", [P, 2, 4, DIM])
    rowst = sb("f_rowst", [P, 2, CAP])
    hid = sb("f_hid", [P, FCH, CAP])
    yt = sb("f_yt", [P, 2, CAP])
    y = sb("f_y", [P, 2, 4, DIM])
    WL = 16 * 4

    def over_experts(eng, body):
        body(0, 0, 0)
        body(1, 1, 0)
        with eng.Fori(1, EXPERTS // 2) as it:
            body(it * 2, 0, it)
            body(it * 2 + 1, 1, it)

    with nc.Block() as block:
        @block.sync
        def _(sp):
            def store(e, q):
                for j, n in enumerate(CTS):
                    sp.wait_ge(s["yb"], e * 4 + j + 1)
                    settle(sp, m)
                    sp.dma_start(m.d_out[bass.ds(e * CAP + j * CT, n), :], y[0:n, q, j, :]).then_inc(s["stored"][q], 16)

            def expert(e, q, turn):
                if later(e):
                    sp.wait_ge(s["y"], (e - 1) * 2)
                    settle(sp, m)
                    load_expert(sp, m, a, e, q)
                for j, n in enumerate(CTS):
                    sp.dma_start(rows[0:n, q, j, :], m.d_in[bass.ds(e * CAP + j * CT, n), :]).then_inc(s["rows"][q], 16)
                if later(e):
                    store(e - 2, q)
            over_experts(sp, expert)
            for e in (EXPERTS - 2, EXPERTS - 1):
                store(e, e % 2)
            for q in range(2):
                sp.wait_ge(s["stored"][q], 64 * (EXPERTS // 2))

        @block.tensor
        def _(pe):
            def expert(e, q, turn):
                pe.wait_ge(s["rows"][q], (turn + 1) * 64)
                if later(e) or e >= 1:
                    pe.wait_ge(s["y"], e * 2)
                    pe.wait_ge(s["rowsb"], e * 2)
                for half in range(2):
                    for j, n in enumerate(CTS):
                        last = pe.transpose(m.bank[half][:, j * CT:j * CT + n], rows[0:n, q, j, half * P:half * P + P], m.ident[0:n, 0:n])
                    last.then_inc(s["rowst"], 1)
                pe.wait_ge(m.weights_in[q], (turn + 1) * WL)
                pe.wait_ge(s["rowsb"], e * 2 + 2)
                for f in range(FCH):
                    if not (isinstance(e, int) and e == 0 and f < 2):
                        pe.wait_ge(s["hid"], e * FCH + f - 1)
                    for half in range(2):
                        last = pe.matmul(m.bank[2 + f % 2][:, 0:CAP], w1[:, q, half, f * P:f * P + P], rowst[:, half, :],
                                         start=(half == 0), stop=(half == 1))
                    last.then_inc(s["up"], 1)
                for out in range(2):
                    for f in range(FCH):
                        pe.wait_ge(s["hid"], e * FCH + f + 1)
                        last = pe.matmul(m.bank[4 + out][:, 0:CAP], w2[:, q, f, out * P:out * P + P], hid[:, f, :],
                                         start=(f == 0), stop=(f == FCH - 1))
                    last.then_inc(s["down"], 1)
                pe.wait_ge(s["y"], e * 2 + 2)
                for j, n in enumerate(CTS):
                    if j % 2 == 0 and not (isinstance(e, int) and e == 0):
                        pe.wait_ge(s["yb"], e * 4)
                    for out in range(2):
                        last = pe.transpose(m.bank[6 + j // 2][0:n, (j % 2) * DIM + out * P:(j % 2) * DIM + out * P + P],
                                            yt[:, out, j * CT:j * CT + n], m.ident[:, :])
                    last.then_inc(s["yt"], 1)
            over_experts(pe, expert)

        @block.scalar
        def _(act):
            def expert(e, q, turn):
                for half in range(2):
                    act.wait_ge(s["rowst"], e * 2 + 1 + half)
                    act.copy(rowst[:, half, :], m.bank[half][:, 0:CAP]).then_inc(s["rowsb"], 1)
                act.wait_ge(m.weights_in[q], (turn + 1) * WL)
                for f in range(FCH):
                    act.wait_ge(s["up"], e * FCH + f + 1)
                    act.activation(hid[:, f, :], m.bank[2 + f % 2][:, 0:CAP], ACT.Relu, bias=b1[:, q, f:f + 1]).then_inc(s["hid"], 1)
                for out in range(2):
                    act.wait_ge(s["down"], e * 2 + out + 1)
                    if later(e) or e >= 1:
                        act.wait_ge(s["yt"], e * 4)
                    act.activation(yt[:, out, :], m.bank[4 + out][:, 0:CAP], ACT.Identity, bias=b2[:, q, out:out + 1]).then_inc(s["y"], 1)
            over_experts(act, expert)

        @block.vector
        def _(dve):
            def expert(e, q, turn):
                if later(e):
                    dve.wait_ge(s["stored"][q], turn * 64)
                for j, n in enumerate(CTS):
                    dve.wait_ge(s["yt"], e * 4 + j // 2 * 2 + 2)
                    dve.tensor_copy(y[0:n, q, j, :], m.bank[6 + j // 2][0:n, (j % 2) * DIM:(j % 2) * DIM + DIM]).then_inc(s["yb"], 1)
            over_experts(dve, expert)


def combine(nc, ctx, m, a):
    sb = lambda name, shape, dt=F32: ctx.enter_context(nc.sbuf_tensor(name, shape, dt))
    s = sem_set(nc, m.sems, "cmb", "init places gated chain out stored*")
    slot = [sb(f"c_slot{r}", [P, 1], I32) for r in range(4)]
    y = [sb(f"c_y{r}", [P, DIM]) for r in range(4)]
    fetched = [m.sems.enter_context(nc.semaphore(f"cmb_fetched{r}")) for r in range(4)]
    ys = sb("c_ys", [P, 2, 2, DIM])
    bad = sb("c_bad", [P, 3, 2, DIM], I32)
    subst = sb("c_subst", [P, 3, 2, DIM])
    out = sb("c_out", [P, 2, 2, DIM])
    HUGE = 3.4028234663852886e38
    CH = 5
    PAIRS = TILES // 2

    def over_pairs(eng, body):
        body(0, 0)
        body(1, 1)
        with eng.Fori(1, PAIRS // 2 - 1) as it:
            body(it * 2, 0)
            body(it * 2 + 1, 1)
        body(PAIRS - 2, 0)
        body(PAIRS - 1, 1)

    with nc.Block() as block:
        @block.gpsimd
        def _(pool):
            for i, value in enumerate((0.0, 1e4, -1e4)):
                pool.memset(subst[:, i, :, :], value).then_inc(s["init"], 1)

            def tile(n, r):
                if not isinstance(n, int) or n >= 4:
                    pool.wait_ge(fetched[r], turns(n, r) * 16)
                pool.tensor_copy(slot[r][:, :], m.slot[:, bass.ds(n, 1)]).then_inc(s["places"], 1)
                pool.wait_ge(s["places"], n + 1)
                if not isinstance(n, int) or n >= 4:
                    pool.wait_ge(s["gated"], n - 3)
                settle(pool, m)
                pool.indirect_dma_start(y[r][:, :], None, m.d_out, bass.IndirectOffsetOnAxis(ap=slot[r][:, 0:1], axis=0)).then_inc(fetched[r], 16)
            over_fours(pool, tile)

        @block.vector
        def _(dve):
            dve.wait_ge(s["init"], 3)

            def pair(t, q):
                ch = Chain(dve, s["chain"], t * CH)
                one = ys[:, q, :, :]
                dve.wait_ge(s["gated"], t * 2 + 2)
                dve.tensor_tensor(bad[:, 0, :, :], one, one, ALU.not_equal)
                dve.tensor_scalar(bad[:, 1, :, :], one, HUGE, None, ALU.is_gt).then_inc(s["chain"], 1)
                dve.tensor_scalar(bad[:, 2, :, :], one, -HUGE, None, ALU.is_lt).then_inc(s["chain"], 1)
                ch.n = 2
                dve.wait_ge(s["chain"], t * CH + 2)
                settle(dve, m)
                for i in range(3):
                    ch.step(dve.copy_predicated(one, bad[:, i, :, :], subst[:, i, :, :]), settled=m if i < 2 else None)
                if later(t):
                    dve.wait_ge(s["stored"][q], uses(t, q) * 16)
                dve.tensor_tensor(out[:, q, :, :], one, m.x[:, bass.ds(t * 2, 2), :], ALU.add).then_inc(s["out"], 2)
                assert ch.n == CH
            over_pairs(dve, pair)

        @block.scalar
        def _(act):
            def tile(n, r):
                act.wait_ge(fetched[r], (turns(n, r) + 1) * 16)
                if not isinstance(n, int) or n >= 4:
                    act.wait_ge(s["out"], n - 2 - r % 2)
                act.activation(ys[:, r // 2, r % 2, :], y[r][:, :], ACT.Copy, scale=m.share[:, bass.ds(n, 1)]).then_inc(s["gated"], 1)
            over_fours(act, tile)

        @block.sync
        def _(sp):
            def pair(t, q):
                sp.wait_ge(s["out"], t * 2 + 2)
                settle(sp, m)
                if isinstance(t, int) and t == PAIRS - 1:
                    lo = t * 2 * P
                    sp.dma_start(a.out[lo:lo + P, :], out[:, q, 0, :]).then_inc(s["stored"][q], 16)
                    sp.dma_start(a.out[lo + P:NODES, :], out[0:LAST, q, 1, :]).then_inc(s["stored"][q], 16)
                else:
                    sp.dma_start(a.out[bass.ds(t * 2 * P, 2 * P), :].rearrange("(t p) c -> p t c", p=P), out[:, q, :, :]).then_inc(s["stored"][q], 16)
            over_pairs(sp, pair)
            sp.wait_ge(s["stored"][0], 16 * (PAIRS // 2))
            sp.wait_ge(s["stored"][1], 16 * (PAIRS // 2 + 1))


_INS = ["x", "src", "dst", "L0_gnn_W_l", "L0_gnn_W_r", "L0_gnn_att", "L0_gnn_bias", "L0_gnn_gamma", "L0_gnn_beta",
        "L0_mix_W_qk", "L0_mix_b_qk", "L0_mix_W_v", "L0_mix_b_v", "L0_mix_gamma", "L0_mix_beta", "L0_ffn_gate_w",
        "L0_ffn_gate_b", "L0_ffn_w1", "L0_ffn_b1", "L0_ffn_w2", "L0_ffn_b2"]


def graph_block(nc, x, src, dst, W_l, W_r, att, bias, gamma, beta, W_qk, b_qk, W_v, b_v, mix_gamma, mix_beta,
                gate_w, gate_b, w1, b1, w2, b2, out):
    a = Arrays()
    a.x, a.src, a.dst, a.out = x, src, dst, out
    a.W_l, a.W_r, a.att, a.bias, a.gamma, a.beta = W_l, W_r, att, bias, gamma, beta
    a.W_qk, a.b_qk, a.W_v, a.b_v, a.mix_gamma, a.mix_beta = W_qk, b_qk, W_v, b_v, mix_gamma, mix_beta
    a.gate_w, a.gate_b, a.w1, a.b1, a.w2, a.b2 = gate_w, gate_b, w1, b1, w2, b2
    with ExitStack() as whole:
        m = memory(nc, whole)
        m.sems = whole
        for stage in (prepare, project, lambdas, attend, node_update, experts, combine):
            with ExitStack() as buffers:
                stage(nc, buffers, m, a)


def kernel(**inputs):
    import numpy as _np
    import concourse.bacc as _bacc
    from concourse import mybir as _mybir
    from concourse.bass_utils import run_bass_kernel_spmd as _run

    nc = _bacc.Bacc("TRN2", target_bir_lowering=False, num_devices=1)
    arrays, args = {}, []
    for name in _INS:
        a = _np.ascontiguousarray(inputs[name])
        arrays[f"in_{name}_dram"] = a
        args.append(nc.dram_tensor(f"in_{name}_dram", a.shape, _mybir.dt.from_np(a.dtype), kind="ExternalInput").ap())
    args.append(nc.dram_tensor("out_0_dram", (NODES, DIM), F32, kind="ExternalOutput").ap())
    graph_block(nc, *args)
    r = _run(nc, [arrays], core_ids=[0])
    return r.results[0]["out_0_dram"]
```
